# Optimizing a Trainium2 kernel written in Bass

```python
import numpy as np
import jax
import jax.numpy as jnp

def _softmax(x, axis=-1):
    return jax.nn.softmax(x, axis=axis)

def _gelu(x):
    return jax.nn.gelu(x, approximate=True)

def _silu(x):
    return jax.nn.silu(x)

def _sigmoid(x):
    return jax.nn.sigmoid(x)

def _layernorm(x, axis=-1, eps=1e-05):
    m = jnp.mean(x, axis=axis, keepdims=True)
    v = jnp.var(x, axis=axis, keepdims=True)
    return (x - m) / jnp.sqrt(v + eps)

def _scatter_add(tgt, idx, src, axis=0):
    return tgt.at[idx].add(src)

def _segment_sum(src, seg, n):
    return jax.ops.segment_sum(src, seg, n)
kernel_name = 'mk_pixart_seq_d4_seqx_r8_0637cb'

def setup_inputs(seed: int=0):
    np.random.seed(seed)
    _w = jnp.asarray

    def _rec_inputs():
        import jax
        import jax.numpy as jnp
        _rk = jax.random.key(seed)
        x = -0.0003929 + 0.9999 * jax.random.normal(jax.random.fold_in(_rk, 1), (16, 256, 128), jnp.float32)
        _lenS = 256 - jax.random.randint(jax.random.fold_in(_rk, 7), (16,), 0, max(1, 256 // 4) + 1, jnp.int32)
        _lenS2 = 1601 - jax.random.randint(jax.random.fold_in(_rk, 8), (16,), 0, max(1, 1601 // 4) + 1, jnp.int32)
        cond_1024 = 0.00782532 + 1.00527 * jax.random.normal(jax.random.fold_in(_rk, 11), (16, 128), jnp.float32)
        _ctx_1024P = jax.random.normal(jax.random.fold_in(_rk, 12), (16, 16, 128), jnp.float32)
        _ctx_1024c = jax.random.dirichlet(jax.random.fold_in(_rk, 512), 0.3 * jnp.ones((16,), jnp.float32), (16, 1601))
        _ctx_1024t = jnp.einsum('bsk,bkd->bsd', _ctx_1024c, _ctx_1024P)
        _ctx_1024t = _ctx_1024t * jax.lax.rsqrt(jnp.mean(jnp.square(_ctx_1024t)) + 1e-12) * 0.953939
        ctx_1024 = -0.000761806 + 0.999296 * (_ctx_1024t + 0.3 * jax.random.normal(jax.random.fold_in(_rk, 612), (16, 1601, 128), jnp.float32))
        return (x, cond_1024, ctx_1024)
    x, cond_1024, ctx_1024 = _rec_inputs()

    def _L0_xcond_setup():
        import jax, jax.numpy as jnp
        import numpy as np
        H = 128
        RH = 2 * H
        E = 3
        B, T, P = (8, 256, 64)
        LN_EPS = 1e-05

        def _layer_norm(x, gamma, beta):
            mu = jnp.mean(x, axis=-1, keepdims=True)
            var = jnp.mean(jnp.square(x - mu), axis=-1, keepdims=True)
            return (x - mu) * jax.lax.rsqrt(var + LN_EPS) * gamma + beta
        key = jax.random.key(seed)
        ks = jax.random.split(key, 24)
        s = lambda fan_in: 1.0 / np.sqrt(fan_in)
        inp = {'mix_hidden_states': jax.random.normal(ks[0], (B, T, H), jnp.float32), 'global_anchor': jax.random.normal(ks[1], (B, H), jnp.float32), 'prototype_bank': jax.random.normal(ks[2], (B, P, H), jnp.float32), 'ln_gamma': jnp.ones((H,), jnp.float32), 'ln_beta': jnp.zeros((H,), jnp.float32), 'Wq': jax.random.normal(ks[3], (H, H), jnp.float32) * s(H), 'Wk': jax.random.normal(ks[4], (H, H), jnp.float32) * s(H), 'Wv': jax.random.normal(ks[5], (H, H), jnp.float32) * s(H), 'router_W': jax.random.normal(ks[6], (3 * H, E), jnp.float32) * s(3 * H), 'router_b': jnp.zeros((E,), jnp.float32), 'e_w1': jax.random.normal(ks[7], (E, 3 * H, RH), jnp.float32) * s(3 * H), 'e_b1': jnp.zeros((E, RH), jnp.float32), 'e_w2': jax.random.normal(ks[8], (E, RH, H), jnp.float32) * s(RH), 'e_b2': jnp.zeros((E, H), jnp.float32), 'gate_w1': jax.random.normal(ks[9], (3 * H, H), jnp.float32) * s(3 * H), 'gate_b1': jnp.zeros((H,), jnp.float32), 'gate_w2': jax.random.normal(ks[10], (H, H), jnp.float32) * s(H), 'gate_b2': jnp.zeros((H,), jnp.float32), 'out_w': jax.random.normal(ks[11], (H, H), jnp.float32) * s(H), 'out_b': jnp.zeros((H,), jnp.float32)}
        return inp
    _L0_xcond_all = _L0_xcond_setup()
    _L0_xcond_in = {k: v for k, v in _L0_xcond_all.items() if k in ('ln_gamma', 'ln_beta', 'Wq', 'Wk', 'Wv', 'router_W', 'router_b', 'e_w1', 'e_b1', 'e_w2', 'e_b2', 'gate_w1', 'gate_b1', 'gate_w2', 'gate_b2', 'out_w', 'out_b')}
    del _L0_xcond_all

    def _L1_xcond_setup():
        import jax, jax.numpy as jnp
        import numpy as np
        C = 128
        H = 16
        D = C // H
        WIN = 64
        SHIFT = 32
        TOPK = 16
        HID = 512
        EPS = 1e-06

        def _ln(x):
            x32 = x.astype(jnp.float32)
            m = x32.mean(-1, keepdims=True)
            v = jnp.mean((x32 - m) ** 2, axis=-1, keepdims=True)
            return ((x32 - m) * jax.lax.rsqrt(v + EPS)).astype(x.dtype)

        def _self_attn(h, w_qkv, b_qkv, w_so, b_so):
            B, L, _ = h.shape
            qkv = h @ w_qkv + b_qkv
            qkv = jnp.roll(qkv, -SHIFT, axis=1)
            nw = L // WIN
            qkv = qkv.reshape(B, nw, WIN, 3, H, D)
            q, k, v = (qkv[:, :, :, 0], qkv[:, :, :, 1], qkv[:, :, :, 2])
            scores = jnp.einsum('bnqhd,bnkhd->bnhqk', q, k) / jnp.sqrt(jnp.float32(D)).astype(h.dtype)
            attn = jax.nn.softmax(scores, axis=-1)
            o = jnp.einsum('bnhqk,bnkhd->bnqhd', attn, v).reshape(B, L, C)
            o = jnp.roll(o, SHIFT, axis=1)
            return o @ w_so + b_so

        def _topk_cross_attn(h, ctx, w_q, b_q, w_kv, b_kv, w_co, b_co):
            B, L, _ = h.shape
            Lc = ctx.shape[1]
            q = (h @ w_q + b_q).reshape(B, L, H, D)
            kv = (ctx @ w_kv + b_kv).reshape(B, Lc, 2, H, D)
            k, v = (kv[:, :, 0], kv[:, :, 1])
            scores = jnp.einsum('bqhd,bkhd->bhqk', q, k) / jnp.sqrt(jnp.float32(D)).astype(h.dtype)
            top_s, top_i = jax.lax.top_k(scores, TOPK)
            attn = jax.nn.softmax(top_s, axis=-1)
            v_bh = jnp.transpose(v, (0, 2, 1, 3))
            vg = jnp.take_along_axis(v_bh[:, :, None, :, :], top_i[..., None], axis=3)
            o = jnp.einsum('bhqk,bhqkd->bqhd', attn, vg).reshape(B, L, C)
            return o @ w_co + b_co

        def _swiglu(h, w_m1, b_m1, w_m2, b_m2):
            u = h @ w_m1 + b_m1
            a, b = (u[..., :HID], u[..., HID:])
            return jax.nn.silu(a) * b @ w_m2 + b_m2
        key = jax.random.key(seed)
        ks = jax.random.split(key, 24)
        s = 0.02
        inp = {'x': jax.random.normal(ks[0], (2, 512, C), jnp.float32), 'mod': jax.random.normal(ks[1], (2, C), jnp.float32), 'context': jax.random.normal(ks[2], (2, 128, C), jnp.float32), 'w_ada': jax.random.normal(ks[3], (C, 9 * C), jnp.float32) * s, 'b_ada': jnp.zeros((9 * C,), jnp.float32), 'w_qkv': jax.random.normal(ks[4], (C, 3 * C), jnp.float32) * s, 'b_qkv': jnp.zeros((3 * C,), jnp.float32), 'w_so': jax.random.normal(ks[5], (C, C), jnp.float32) * s, 'b_so': jnp.zeros((C,), jnp.float32), 'w_q': jax.random.normal(ks[6], (C, C), jnp.float32) * s, 'b_q': jnp.zeros((C,), jnp.float32), 'w_kv': jax.random.normal(ks[7], (C, 2 * C), jnp.float32) * s, 'b_kv': jnp.zeros((2 * C,), jnp.float32), 'w_co': jax.random.normal(ks[8], (C, C), jnp.float32) * s, 'b_co': jnp.zeros((C,), jnp.float32), 'w_m1': jax.random.normal(ks[9], (C, 2 * HID), jnp.float32) * s, 'b_m1': jnp.zeros((2 * HID,), jnp.float32), 'w_m2': jax.random.normal(ks[10], (HID, C), jnp.float32) * s, 'b_m2': jnp.zeros((C,), jnp.float32)}
        return inp
    _L1_xcond_all = _L1_xcond_setup()
    _L1_xcond_in = {k: v for k, v in _L1_xcond_all.items() if k in ('w_ada', 'b_ada', 'w_qkv', 'b_qkv', 'w_so', 'b_so', 'w_q', 'b_q', 'w_kv', 'b_kv', 'w_co', 'b_co', 'w_m1', 'b_m1', 'w_m2', 'b_m2')}
    del _L1_xcond_all

    def _L2_xcond_setup():
        import jax, jax.numpy as jnp
        import numpy as np
        D = 128
        H = 16
        HD = D // H
        MLP = 4 * D
        EPS = 1e-06
        SCALE = HD ** (-0.5)

        def _p(key, shape, s=0.02):
            return jax.random.normal(key, shape, dtype=jnp.float32) * s

        def _ln(x):
            mu = jnp.mean(x, axis=-1, keepdims=True)
            var = jnp.var(x, axis=-1, keepdims=True)
            return (x - mu) * jax.lax.rsqrt(var + EPS)

        def _heads(t):
            B, L, _ = t.shape
            return t.reshape(B, L, H, HD).transpose(0, 2, 1, 3)

        def _attend(q, k, v):
            attn = jnp.einsum('bhnd,bhsd->bhns', q, k) * SCALE
            attn = jax.nn.softmax(attn, axis=-1)
            o = jnp.einsum('bhns,bhsd->bhnd', attn, v)
            B, _, N, _ = q.shape
            return o.transpose(0, 2, 1, 3).reshape(B, N, D)
        key = jax.random.key(seed)
        ks = jax.random.split(key, 24)
        B, N, S = (4, 128, 77)
        return {'x': jax.random.normal(ks[0], (B, N, D), dtype=jnp.float32), 't_emb': jax.random.normal(ks[1], (B, D), dtype=jnp.float32), 'context': jax.random.normal(ks[2], (B, S, D), dtype=jnp.float32), 'adaln_w': _p(ks[3], (D, 6 * D)), 'adaln_b': _p(ks[4], (6 * D,)), 'qkv_w': _p(ks[5], (D, 3 * D)), 'qkv_b': _p(ks[6], (3 * D,)), 'sa_proj_w': _p(ks[7], (D, D)), 'sa_proj_b': _p(ks[8], (D,)), 'q_w': _p(ks[9], (D, D)), 'q_b': _p(ks[10], (D,)), 'kv_w': _p(ks[11], (D, 2 * D)), 'kv_b': _p(ks[12], (2 * D,)), 'ca_proj_w': _p(ks[13], (D, D)), 'ca_proj_b': _p(ks[14], (D,)), 'fc1_w': _p(ks[15], (D, MLP)), 'fc1_b': _p(ks[16], (MLP,)), 'fc2_w': _p(ks[17], (MLP, D)), 'fc2_b': _p(ks[18], (D,))}
    _L2_xcond_all = _L2_xcond_setup()
    _L2_xcond_in = {k: v for k, v in _L2_xcond_all.items() if k in ('adaln_w', 'adaln_b', 'qkv_w', 'qkv_b', 'sa_proj_w', 'sa_proj_b', 'q_w', 'q_b', 'kv_w', 'kv_b', 'ca_proj_w', 'ca_proj_b', 'fc1_w', 'fc1_b', 'fc2_w', 'fc2_b')}
    del _L2_xcond_all

    def _L3_xcond_setup():
        import jax, jax.numpy as jnp
        import numpy as np
        EPS = 1e-05

        def _ada_ln(x, c, W_ss, b_ss):
            mu = jnp.mean(x, axis=-1, keepdims=True)
            var = jnp.mean((x - mu) ** 2, axis=-1, keepdims=True)
            h = (x - mu) / jnp.sqrt(var + EPS)
            ss = jax.nn.silu(c) @ W_ss + b_ss
            scale, bias = jnp.split(ss, 2, axis=-1)
            return (1.0 + scale)[:, None, :] * h + bias[:, None, :]
        key = jax.random.key(seed)
        ks = jax.random.split(key, 12)
        B, Lq, Lkv, H = (8, 256, 64, 128)
        s = 0.02
        return {'x_q': jax.random.normal(ks[0], (B, Lq, H), jnp.float32), 'x_kv': jax.random.normal(ks[1], (B, Lkv, H), jnp.float32), 't_vec': jax.random.normal(ks[2], (B, H), jnp.float32), 'Wq': jax.random.normal(ks[3], (H, H), jnp.float32) * s, 'bq': jnp.zeros((H,), jnp.float32), 'Wkv': jax.random.normal(ks[4], (H, 2 * H), jnp.float32) * s, 'bkv': jnp.zeros((2 * H,), jnp.float32), 'Wp': jax.random.normal(ks[5], (H, H), jnp.float32) * s, 'bp': jnp.zeros((H,), jnp.float32), 'Wss_q': jax.random.normal(ks[6], (H, 2 * H), jnp.float32) * s, 'bss_q': jnp.zeros((2 * H,), jnp.float32), 'Wss_kv': jax.random.normal(ks[7], (H, 2 * H), jnp.float32) * s, 'bss_kv': jnp.zeros((2 * H,), jnp.float32)}
    _L3_xcond_all = _L3_xcond_setup()
    _L3_xcond_in = {k: v for k, v in _L3_xcond_all.items() if k in ('Wq', 'bq', 'Wkv', 'bkv', 'Wp', 'bp', 'Wss_q', 'bss_q', 'Wss_kv', 'bss_kv')}
    del _L3_xcond_all
    return {'x': x, 'cond_1024': cond_1024, 'ctx_1024': ctx_1024, 'L0_xcond_ln_gamma': _L0_xcond_in['ln_gamma'], 'L0_xcond_ln_beta': _L0_xcond_in['ln_beta'], 'L0_xcond_Wq': _L0_xcond_in['Wq'], 'L0_xcond_Wk': _L0_xcond_in['Wk'], 'L0_xcond_Wv': _L0_xcond_in['Wv'], 'L0_xcond_router_W': _L0_xcond_in['router_W'], 'L0_xcond_router_b': _L0_xcond_in['router_b'], 'L0_xcond_e_w1': _L0_xcond_in['e_w1'], 'L0_xcond_e_b1': _L0_xcond_in['e_b1'], 'L0_xcond_e_w2': _L0_xcond_in['e_w2'], 'L0_xcond_e_b2': _L0_xcond_in['e_b2'], 'L0_xcond_gate_w1': _L0_xcond_in['gate_w1'], 'L0_xcond_gate_b1': _L0_xcond_in['gate_b1'], 'L0_xcond_gate_w2': _L0_xcond_in['gate_w2'], 'L0_xcond_gate_b2': _L0_xcond_in['gate_b2'], 'L0_xcond_out_w': _L0_xcond_in['out_w'], 'L0_xcond_out_b': _L0_xcond_in['out_b'], 'L1_xcond_w_ada': _L1_xcond_in['w_ada'], 'L1_xcond_b_ada': _L1_xcond_in['b_ada'], 'L1_xcond_w_qkv': _L1_xcond_in['w_qkv'], 'L1_xcond_b_qkv': _L1_xcond_in['b_qkv'], 'L1_xcond_w_so': _L1_xcond_in['w_so'], 'L1_xcond_b_so': _L1_xcond_in['b_so'], 'L1_xcond_w_q': _L1_xcond_in['w_q'], 'L1_xcond_b_q': _L1_xcond_in['b_q'], 'L1_xcond_w_kv': _L1_xcond_in['w_kv'], 'L1_xcond_b_kv': _L1_xcond_in['b_kv'], 'L1_xcond_w_co': _L1_xcond_in['w_co'], 'L1_xcond_b_co': _L1_xcond_in['b_co'], 'L1_xcond_w_m1': _L1_xcond_in['w_m1'], 'L1_xcond_b_m1': _L1_xcond_in['b_m1'], 'L1_xcond_w_m2': _L1_xcond_in['w_m2'], 'L1_xcond_b_m2': _L1_xcond_in['b_m2'], 'L2_xcond_adaln_w': _L2_xcond_in['adaln_w'], 'L2_xcond_adaln_b': _L2_xcond_in['adaln_b'], 'L2_xcond_qkv_w': _L2_xcond_in['qkv_w'], 'L2_xcond_qkv_b': _L2_xcond_in['qkv_b'], 'L2_xcond_sa_proj_w': _L2_xcond_in['sa_proj_w'], 'L2_xcond_sa_proj_b': _L2_xcond_in['sa_proj_b'], 'L2_xcond_q_w': _L2_xcond_in['q_w'], 'L2_xcond_q_b': _L2_xcond_in['q_b'], 'L2_xcond_kv_w': _L2_xcond_in['kv_w'], 'L2_xcond_kv_b': _L2_xcond_in['kv_b'], 'L2_xcond_ca_proj_w': _L2_xcond_in['ca_proj_w'], 'L2_xcond_ca_proj_b': _L2_xcond_in['ca_proj_b'], 'L2_xcond_fc1_w': _L2_xcond_in['fc1_w'], 'L2_xcond_fc1_b': _L2_xcond_in['fc1_b'], 'L2_xcond_fc2_w': _L2_xcond_in['fc2_w'], 'L2_xcond_fc2_b': _L2_xcond_in['fc2_b'], 'L3_xcond_Wq': _L3_xcond_in['Wq'], 'L3_xcond_bq': _L3_xcond_in['bq'], 'L3_xcond_Wkv': _L3_xcond_in['Wkv'], 'L3_xcond_bkv': _L3_xcond_in['bkv'], 'L3_xcond_Wp': _L3_xcond_in['Wp'], 'L3_xcond_bp': _L3_xcond_in['bp'], 'L3_xcond_Wss_q': _L3_xcond_in['Wss_q'], 'L3_xcond_bss_q': _L3_xcond_in['bss_q'], 'L3_xcond_Wss_kv': _L3_xcond_in['Wss_kv'], 'L3_xcond_bss_kv': _L3_xcond_in['bss_kv']}

def reference(x, cond_1024, ctx_1024, L0_xcond_ln_gamma, L0_xcond_ln_beta, L0_xcond_Wq, L0_xcond_Wk, L0_xcond_Wv, L0_xcond_router_W, L0_xcond_router_b, L0_xcond_e_w1, L0_xcond_e_b1, L0_xcond_e_w2, L0_xcond_e_b2, L0_xcond_gate_w1, L0_xcond_gate_b1, L0_xcond_gate_w2, L0_xcond_gate_b2, L0_xcond_out_w, L0_xcond_out_b, L1_xcond_w_ada, L1_xcond_b_ada, L1_xcond_w_qkv, L1_xcond_b_qkv, L1_xcond_w_so, L1_xcond_b_so, L1_xcond_w_q, L1_xcond_b_q, L1_xcond_w_kv, L1_xcond_b_kv, L1_xcond_w_co, L1_xcond_b_co, L1_xcond_w_m1, L1_xcond_b_m1, L1_xcond_w_m2, L1_xcond_b_m2, L2_xcond_adaln_w, L2_xcond_adaln_b, L2_xcond_qkv_w, L2_xcond_qkv_b, L2_xcond_sa_proj_w, L2_xcond_sa_proj_b, L2_xcond_q_w, L2_xcond_q_b, L2_xcond_kv_w, L2_xcond_kv_b, L2_xcond_ca_proj_w, L2_xcond_ca_proj_b, L2_xcond_fc1_w, L2_xcond_fc1_b, L2_xcond_fc2_w, L2_xcond_fc2_b, L3_xcond_Wq, L3_xcond_bq, L3_xcond_Wkv, L3_xcond_bkv, L3_xcond_Wp, L3_xcond_bp, L3_xcond_Wss_q, L3_xcond_bss_q, L3_xcond_Wss_kv, L3_xcond_bss_kv):
    import jax
    import jax.numpy as jnp

    def _L0_xcond_ref(mix_hidden_states, global_anchor, prototype_bank, ln_gamma, ln_beta, Wq, Wk, Wv, router_W, router_b, e_w1, e_b1, e_w2, e_b2, gate_w1, gate_b1, gate_w2, gate_b2, out_w, out_b):
        import jax, jax.numpy as jnp
        import numpy as np
        H = 128
        RH = 2 * H
        E = 3
        B, T, P = (8, 256, 64)
        LN_EPS = 1e-05

        def _layer_norm(x, gamma, beta):
            mu = jnp.mean(x, axis=-1, keepdims=True)
            var = jnp.mean(jnp.square(x - mu), axis=-1, keepdims=True)
            return (x - mu) * jax.lax.rsqrt(var + LN_EPS) * gamma + beta
        x = mix_hidden_states
        nx = _layer_norm(x, ln_gamma, ln_beta)
        q = nx @ Wq
        k = prototype_bank @ Wk
        v = prototype_bank @ Wv
        scores = jnp.einsum('bth,bph->btp', q, k) * H ** (-0.5)
        weights = jax.nn.softmax(scores, axis=-1)
        evidence = jnp.einsum('btp,bph->bth', weights, v)
        anchor = jnp.broadcast_to(global_anchor[:, None, :], nx.shape)
        combined = jnp.concatenate([nx, evidence, anchor], axis=-1)
        router_logits = combined @ router_W + router_b
        router_probs = jax.nn.softmax(router_logits, axis=-1)
        h = jax.nn.silu(jnp.einsum('btc,ecr->bter', combined, e_w1) + e_b1)
        expert_out = jnp.einsum('bter,erh->bteh', h, e_w2) + e_b2
        routed = jnp.sum(expert_out * router_probs[..., None], axis=-2)
        g = jax.nn.sigmoid(jax.nn.silu(combined @ gate_w1 + gate_b1) @ gate_w2 + gate_b2)
        refined_delta = g * (routed @ out_w + out_b)
        return x + refined_delta

    def _L1_xcond_ref(x, mod, context, w_ada, b_ada, w_qkv, b_qkv, w_so, b_so, w_q, b_q, w_kv, b_kv, w_co, b_co, w_m1, b_m1, w_m2, b_m2):
        import jax, jax.numpy as jnp
        import numpy as np
        C = 128
        H = 16
        D = C // H
        WIN = 64
        SHIFT = 32
        TOPK = 16
        HID = 512
        EPS = 1e-06

        def _ln(x):
            x32 = x.astype(jnp.float32)
            m = x32.mean(-1, keepdims=True)
            v = jnp.mean((x32 - m) ** 2, axis=-1, keepdims=True)
            return ((x32 - m) * jax.lax.rsqrt(v + EPS)).astype(x.dtype)

        def _self_attn(h, w_qkv, b_qkv, w_so, b_so):
            B, L, _ = h.shape
            qkv = h @ w_qkv + b_qkv
            qkv = jnp.roll(qkv, -SHIFT, axis=1)
            nw = L // WIN
            qkv = qkv.reshape(B, nw, WIN, 3, H, D)
            q, k, v = (qkv[:, :, :, 0], qkv[:, :, :, 1], qkv[:, :, :, 2])
            scores = jnp.einsum('bnqhd,bnkhd->bnhqk', q, k) / jnp.sqrt(jnp.float32(D)).astype(h.dtype)
            attn = jax.nn.softmax(scores, axis=-1)
            o = jnp.einsum('bnhqk,bnkhd->bnqhd', attn, v).reshape(B, L, C)
            o = jnp.roll(o, SHIFT, axis=1)
            return o @ w_so + b_so

        def _topk_cross_attn(h, ctx, w_q, b_q, w_kv, b_kv, w_co, b_co):
            B, L, _ = h.shape
            Lc = ctx.shape[1]
            q = (h @ w_q + b_q).reshape(B, L, H, D)
            kv = (ctx @ w_kv + b_kv).reshape(B, Lc, 2, H, D)
            k, v = (kv[:, :, 0], kv[:, :, 1])
            scores = jnp.einsum('bqhd,bkhd->bhqk', q, k) / jnp.sqrt(jnp.float32(D)).astype(h.dtype)
            top_s, top_i = jax.lax.top_k(scores, TOPK)
            attn = jax.nn.softmax(top_s, axis=-1)
            v_bh = jnp.transpose(v, (0, 2, 1, 3))
            vg = jnp.take_along_axis(v_bh[:, :, None, :, :], top_i[..., None], axis=3)
            o = jnp.einsum('bhqk,bhqkd->bqhd', attn, vg).reshape(B, L, C)
            return o @ w_co + b_co

        def _swiglu(h, w_m1, b_m1, w_m2, b_m2):
            u = h @ w_m1 + b_m1
            a, b = (u[..., :HID], u[..., HID:])
            return jax.nn.silu(a) * b @ w_m2 + b_m2
        m = jax.nn.silu(mod) @ w_ada + b_ada
        sh_msa, sc_msa, g_msa, sh_mca, sc_mca, g_mca, sh_mlp, sc_mlp, g_mlp = [m[:, i * C:(i + 1) * C][:, None, :] for i in range(9)]
        h = _ln(x) * (1 + sc_msa) + sh_msa
        h = _self_attn(h, w_qkv, b_qkv, w_so, b_so)
        x = x + h * g_msa
        h = _ln(x) * (1 + sc_mca) + sh_mca
        h = _topk_cross_attn(h, context, w_q, b_q, w_kv, b_kv, w_co, b_co)
        x = x + h * g_mca
        h = _ln(x) * (1 + sc_mlp) + sh_mlp
        h = _swiglu(h, w_m1, b_m1, w_m2, b_m2)
        x = x + h * g_mlp
        return x

    def _L2_xcond_ref(x, t_emb, context, adaln_w, adaln_b, qkv_w, qkv_b, sa_proj_w, sa_proj_b, q_w, q_b, kv_w, kv_b, ca_proj_w, ca_proj_b, fc1_w, fc1_b, fc2_w, fc2_b):
        import jax, jax.numpy as jnp
        import numpy as np
        D = 128
        H = 16
        HD = D // H
        MLP = 4 * D
        EPS = 1e-06
        SCALE = HD ** (-0.5)

        def _p(key, shape, s=0.02):
            return jax.random.normal(key, shape, dtype=jnp.float32) * s

        def _ln(x):
            mu = jnp.mean(x, axis=-1, keepdims=True)
            var = jnp.var(x, axis=-1, keepdims=True)
            return (x - mu) * jax.lax.rsqrt(var + EPS)

        def _heads(t):
            B, L, _ = t.shape
            return t.reshape(B, L, H, HD).transpose(0, 2, 1, 3)

        def _attend(q, k, v):
            attn = jnp.einsum('bhnd,bhsd->bhns', q, k) * SCALE
            attn = jax.nn.softmax(attn, axis=-1)
            o = jnp.einsum('bhns,bhsd->bhnd', attn, v)
            B, _, N, _ = q.shape
            return o.transpose(0, 2, 1, 3).reshape(B, N, D)
        B, N, _ = x.shape
        S = context.shape[1]
        mod = jax.nn.silu(t_emb) @ adaln_w + adaln_b
        sh_sa, sc_sa, g_sa, sh_ff, sc_ff, g_ff = jnp.split(mod[:, None, :], 6, axis=-1)
        xm = _ln(x) * (1.0 + sc_sa) + sh_sa
        qkv = (xm @ qkv_w + qkv_b).reshape(B, N, 3, H, HD)
        q = qkv[:, :, 0].transpose(0, 2, 1, 3)
        k = qkv[:, :, 1].transpose(0, 2, 1, 3)
        v = qkv[:, :, 2].transpose(0, 2, 1, 3)
        x_sa = _attend(q, k, v) @ sa_proj_w + sa_proj_b
        x = x + g_sa * x_sa
        xn = _ln(x)
        q = _heads(xn @ q_w + q_b)
        kv = (context @ kv_w + kv_b).reshape(B, S, 2, H, HD)
        k = kv[:, :, 0].transpose(0, 2, 1, 3)
        v = kv[:, :, 1].transpose(0, 2, 1, 3)
        x_ca = _attend(q, k, v) @ ca_proj_w + ca_proj_b
        x = x + x_ca
        xm = _ln(x) * (1.0 + sc_ff) + sh_ff
        h = jax.nn.gelu(xm @ fc1_w + fc1_b, approximate=True)
        x_ff = h @ fc2_w + fc2_b
        x = x + g_ff * x_ff
        return x

    def _L3_xcond_ref(x_q, x_kv, t_vec, Wq, bq, Wkv, bkv, Wp, bp, Wss_q, bss_q, Wss_kv, bss_kv):
        import jax, jax.numpy as jnp
        import numpy as np
        EPS = 1e-05

        def _ada_ln(x, c, W_ss, b_ss):
            mu = jnp.mean(x, axis=-1, keepdims=True)
            var = jnp.mean((x - mu) ** 2, axis=-1, keepdims=True)
            h = (x - mu) / jnp.sqrt(var + EPS)
            ss = jax.nn.silu(c) @ W_ss + b_ss
            scale, bias = jnp.split(ss, 2, axis=-1)
            return (1.0 + scale)[:, None, :] * h + bias[:, None, :]
        B, Lq, H = x_q.shape
        Lkv = x_kv.shape[1]
        nh = 16
        dh = H // nh
        xq = _ada_ln(x_q, t_vec, Wss_q, bss_q)
        xkv = _ada_ln(x_kv, t_vec, Wss_kv, bss_kv)
        q = (xq @ Wq + bq).reshape(B, Lq, nh, dh)
        kv = (xkv @ Wkv + bkv).reshape(B, Lkv, 2, nh, dh)
        k = kv[:, :, 0]
        v = kv[:, :, 1]
        scores = jnp.einsum('bqhd,bkhd->bhqk', q, k) / jnp.sqrt(jnp.float32(dh))
        attn = jax.nn.softmax(scores, axis=-1)
        out = jnp.einsum('bhqk,bkhd->bqhd', attn, v).reshape(B, Lq, H)
        return x_q + (out @ Wp + bp)
    x = _L0_xcond_ref(x, cond_1024, ctx_1024, L0_xcond_ln_gamma, L0_xcond_ln_beta, L0_xcond_Wq, L0_xcond_Wk, L0_xcond_Wv, L0_xcond_router_W, L0_xcond_router_b, L0_xcond_e_w1, L0_xcond_e_b1, L0_xcond_e_w2, L0_xcond_e_b2, L0_xcond_gate_w1, L0_xcond_gate_b1, L0_xcond_gate_w2, L0_xcond_gate_b2, L0_xcond_out_w, L0_xcond_out_b)
    x = _L1_xcond_ref(x, cond_1024, ctx_1024, L1_xcond_w_ada, L1_xcond_b_ada, L1_xcond_w_qkv, L1_xcond_b_qkv, L1_xcond_w_so, L1_xcond_b_so, L1_xcond_w_q, L1_xcond_b_q, L1_xcond_w_kv, L1_xcond_b_kv, L1_xcond_w_co, L1_xcond_b_co, L1_xcond_w_m1, L1_xcond_b_m1, L1_xcond_w_m2, L1_xcond_b_m2)
    x = _L2_xcond_ref(x, cond_1024, ctx_1024, L2_xcond_adaln_w, L2_xcond_adaln_b, L2_xcond_qkv_w, L2_xcond_qkv_b, L2_xcond_sa_proj_w, L2_xcond_sa_proj_b, L2_xcond_q_w, L2_xcond_q_b, L2_xcond_kv_w, L2_xcond_kv_b, L2_xcond_ca_proj_w, L2_xcond_ca_proj_b, L2_xcond_fc1_w, L2_xcond_fc1_b, L2_xcond_fc2_w, L2_xcond_fc2_b)
    x = _L3_xcond_ref(x, ctx_1024, cond_1024, L3_xcond_Wq, L3_xcond_bq, L3_xcond_Wkv, L3_xcond_bkv, L3_xcond_Wp, L3_xcond_bp, L3_xcond_Wss_q, L3_xcond_bss_q, L3_xcond_Wss_kv, L3_xcond_bss_kv)
    return x

_drawn_inputs = setup_inputs


def setup_inputs(seed=0):
    import zlib

    import numpy as np

    out = dict(_drawn_inputs(seed))
    spreads = {'L0_xcond_ln_gamma': (1.0, 0.2),
     'L0_xcond_ln_beta': (0.0, 0.617),
     'L0_xcond_router_b': (0.0, 0.8),
     'L0_xcond_e_b1': (0.0, 0.38),
     'L0_xcond_e_b2': (0.0, 0.1),
     'L0_xcond_gate_b1': (0.0, 0.8),
     'L0_xcond_gate_b2': (0.0, 0.8),
     'L0_xcond_out_b': (0.0, 0.1),
     'L1_xcond_b_ada': (0.0, 0.566),
     'L1_xcond_b_qkv': (0.0, 0.8),
     'L1_xcond_b_so': (0.0, 0.538),
     'L1_xcond_b_q': (0.0, 0.8),
     'L1_xcond_b_kv': (0.0, 0.8),
     'L1_xcond_b_co': (0.0, 0.546),
     'L1_xcond_b_m1': (0.0, 0.8),
     'L1_xcond_b_m2': (0.0, 0.569),
     'L3_xcond_bq': (0.0, 2.0),
     'L3_xcond_bkv': (0.0, 2.0),
     'L3_xcond_bp': (0.0, 2.0),
     'L3_xcond_bss_q': (0.0, 2.0),
     'L3_xcond_bss_kv': (0.0, 2.0)}
    factors = {'L1_xcond_w_qkv': 8.0,
     'L1_xcond_w_so': 8.0,
     'L1_xcond_w_q': 8.0,
     'L1_xcond_w_kv': 7.675,
     'L1_xcond_w_co': 6.5,
     'L1_xcond_w_m1': 8.0,
     'L1_xcond_w_m2': 8.0,
     'L2_xcond_adaln_w': 6.967,
     'L2_xcond_adaln_b': 8.0,
     'L2_xcond_qkv_w': 8.0,
     'L2_xcond_qkv_b': 8.0,
     'L2_xcond_sa_proj_w': 8.0,
     'L2_xcond_sa_proj_b': 32.323,
     'L2_xcond_q_w': 64.0,
     'L2_xcond_q_b': 64.0,
     'L2_xcond_kv_b': 64.0,
     'L2_xcond_ca_proj_b': 23.384,
     'L2_xcond_fc1_w': 8.0,
     'L2_xcond_fc1_b': 8.0,
     'L2_xcond_fc2_w': 7.938,
     'L2_xcond_fc2_b': 39.658,
     'L3_xcond_Wq': 64.0,
     'L3_xcond_Wss_q': 64.0,
     'L3_xcond_Wss_kv': 57.776,
     'L2_xcond_kv_w': 8.0,
     'L2_xcond_ca_proj_w': 8.0,
     'L3_xcond_Wkv': 8.0,
     'L3_xcond_Wp': 6.151}
    for name, (base, spread) in spreads.items():
        noise = np.random.default_rng([zlib.crc32(name.encode()), seed]).standard_normal(out[name].shape)
        drawn = base * np.exp(spread * noise) if base else spread * noise
        out[name] = jnp.asarray(drawn.astype(out[name].dtype))
    for name, factor in factors.items():
        out[name] = (out[name] * factor).astype(out[name].dtype)
    return out
```

```python
from contextlib import ExitStack, contextmanager

import concourse.bass as bass
from concourse import mybir
from concourse.alu_op_type import AluOpType as ALU

ACT = mybir.ActivationFunctionType
AX = mybir.AxisListType
F32 = mybir.dt.float32
BF16 = mybir.dt.bfloat16

B, T, C = 16, 256, 128
LC = 1601
H, D = 16, 8
HQ = 4
QUADS = H // HQ
QT = T // 128
NTILE = B * QT
BANK = 512
PARTS = 3
ROWS_QK = PARTS * PARTS * D
WINDOW, SHIFT = 64, 32
NWIN = T // WINDOW
ROW_MASK = ROWS_QK
ROW_SHIFT = ROW_MASK + NWIN
ROW_END = ROW_SHIFT + PARTS
EXP_BIAS = -40.0
EXP_SPAN = 104.0
TIE_MARGIN = 2.0 ** -21


@contextmanager
def phase(nc, tag):
    made = []
    with ExitStack() as ctx:
        def sb(name, shape, dt=F32):
            return ctx.enter_context(nc.sbuf_tensor(f"{tag}_{name}", shape, dt))

        def ps(name, shape=(128, BANK), dt=F32):
            return ctx.enter_context(nc.psum_tensor(f"{tag}_{name}", list(shape), dt))

        def sem(name):
            made.append(ctx.enter_context(nc.semaphore(f"{tag}_{name}")))
            return made[-1]

        yield sb, ps, sem
        with nc.Block() as block:
            @block.gpsimd
            def _(pool):
                for s in made:
                    pool.sem_clear(s)


def stand_alone(eng, passed):
    eng.sem_inc(passed, 1)


def modulation(nc, tag, cond_t, silu_t, cond_sb, columns, blocks):
    n = len(blocks)
    plus_one = sum(1 for x in blocks if x[3])
    with phase(nc, tag) as (sb, ps, sem):
        w = sb("w", [128, n, C])
        bias = sb("bias", [128, n, 1])
        out_ps = ps("out")
        loaded, silu_ready, out_ready, added = sem("loaded"), sem("silu_ready"), sem("out_ready"), sem("added")
        out3 = out_ps[:, 0:n * B].rearrange("p (k b) -> p k b", k=n)
        with nc.Block() as block:
            @block.sync
            def _(sp):
                sp.dma_start(cond_sb[:, :], cond_t).then_inc(loaded, 16)
                for k, (wk, bk, _, _) in enumerate(blocks):
                    sp.dma_start(w[:, k, :], wk).then_inc(loaded, 16)
                    sp.dma_start(bias[:, k, :], bk.rearrange("(p o) -> p o", o=1)).then_inc(loaded, 16)

            @block.scalar
            def _(act):
                act.wait_ge(loaded, 16 * (2 * n + 1))
                act.activation(silu_t[:, :], cond_sb[:, :], ACT.Silu).then_inc(silu_ready, 1)

            @block.tensor
            def _(pe):
                pe.wait_ge(loaded, 16 * (2 * n + 1))
                pe.wait_ge(silu_ready, 1)
                for k, (_, _, of_silu, _) in enumerate(blocks):
                    src = silu_t if of_silu else cond_sb
                    last = pe.matmul(out3[:, k, :], w[:, k, :], src[:, :], start=True, stop=True)
                last.then_inc(out_ready, 1)

            @block.vector
            def _(dve):
                dve.wait_ge(out_ready, 1)
                dve.tensor_tensor(columns[:, :, :], out3, bias[:, :, :].broadcast_to([128, n, B]), ALU.add
                                  ).then_inc(added, 1)
                dve.wait_ge(added, 1)
                dve.tensor_scalar(columns[:, 0:plus_one, :], columns[:, 0:plus_one, :], 1.0, None, ALU.add
                                  ).then_inc(added, 1)


def gate_rows(nc, tag, silu_t, gate, w_block, bias):
    PER_BANK = BANK // C
    with phase(nc, tag) as (sb, ps, sem):
        w = sb("w", [128, C])
        bias_row = sb("bias_row", [1, C])
        ones = sb("ones", [1, 128])
        banks = [ps(f"rows{i}") for i in range(B // PER_BANK)]
        loaded, ones_ready, rows_ready, copied = sem("loaded"), sem("ones_ready"), sem("rows_ready"), sem("copied")
        with nc.Block() as block:
            @block.sync
            def _(sp):
                sp.dma_start(w[:, :], w_block).then_inc(loaded, 16)
                sp.dma_start(bias_row[:, :], bias.rearrange("(o n) -> o n", o=1)).then_inc(loaded, 16)

            @block.tensor
            def _(pe):
                pe.wait_ge(loaded, 32)
                pe.wait_ge(ones_ready, 1)
                for b in range(B):
                    out = banks[b // PER_BANK][:, b % PER_BANK * C:(b % PER_BANK + 1) * C]
                    pe.matmul(out, silu_t[:, b:b + 1].broadcast_to([128, 128]), w[:, :], start=True, stop=False)
                    last = pe.matmul(out, ones[:, :], bias_row[:, :], start=False, stop=True)
                    if b % PER_BANK == PER_BANK - 1:
                        last.then_inc(rows_ready, 1)

            @block.vector
            def _(dve):
                dve.memset(ones[:, :], 1.0).then_inc(ones_ready, 1)

            @block.scalar
            def _(act):
                for i in range(B // PER_BANK):
                    act.wait_ge(rows_ready, i + 1)
                    act.activation(gate[:, i * BANK:(i + 1) * BANK], banks[i][:, :], ACT.Copy).then_inc(copied, 1)


def prepare(nc, tag, X, items, columns, eps, raw_outs, norm_outs, norm_cols, const, ctx_dram=None, turned_dram=None):
    NI = len(items)
    STEP = 1 + max(i[0] for i in items)
    MAXT = max((i[2] + 127) // 128 for i in items)
    outs = [("raw", *o) for o in raw_outs] + [("norm", *o) for o in norm_outs]
    NO = len(outs)
    sources = (["raw"] if raw_outs else []) + (["norm"] if norm_outs else [])
    n_split = sum(o[1] == "split" for o in outs)
    n_rows = NO - n_split
    tiles_of = [[(i * 128, min(128, r - i * 128)) for i in range((r + 127) // 128)] for _, _, r in items]
    TILES = sum(len(t) for t in tiles_of)
    before = [sum(len(t) for t in tiles_of[:u]) for u in range(NI + 1)]
    with phase(nc, tag) as (sb, ps, sem):
        w = sb("w", [128, NO, C])
        bias_col = sb("bias_col", [128, NO, 1])
        bias_scaled = sb("bias_scaled", [128, NO, 1])
        bias_row = sb("bias_row", [1, NO, C])
        ones = sb("ones", [1, 128])
        eps_col = sb("eps_col", [128, 1])
        ident = sb("ident", [128, 128])
        raw = [sb(f"raw{i}", [128, MAXT, C]) for i in range(2)]
        normed = [sb(f"normed{i}", [128, MAXT, C]) for i in range(2)]
        stats = [sb(f"stats{i}", [128, MAXT, 6]) for i in range(2)]
        mean_var = [sb(f"mean_var{i}", [128, MAXT, 2]) for i in range(2)]
        deviation = [sb(f"deviation{i}", [128, MAXT]) for i in range(2)]
        inverse = [sb(f"inverse{i}", [128, MAXT]) for i in range(2)]
        turned = {s: [sb(f"turned_{s}{i}", [128, MAXT * 128]) for i in range(2)] for s in sources}
        value = [[sb(f"value{k}_{i}", [128, MAXT * 128]) for i in range(2)] for k in range(NO)]
        parts = [[sb(f"parts{k}_{i}", [128, PARTS, MAXT * 128], BF16) if outs[k][1] == "split" else None
                  for i in range(2)] for k in range(NO)]
        remains = [sb(f"remains{k}", [128, MAXT * 128]) for k in range(NO)]
        turned_ps = {s: ps(f"turned_{s}") for s in sources}
        out_ps = [ps(f"out{k}") for k in range(NO)]

        loaded, set_once, bias_done = sem("loaded"), sem("set_once"), sem("bias_done")
        passed_sp, passed_pool, passed_act, passed_dve = (sem(f"passed_{e}") for e in ("sp", "pool", "act", "dve"))
        raw_loaded = [sem(f"raw_loaded{i}") for i in range(2)]
        stats_ready, aggregated, dev_ready, inv_ready = (
            sem("stats_ready"), sem("aggregated"), sem("dev_ready"), sem("inv_ready"))
        normed_ready = sem("normed_ready")
        turned_ready = {s: sem(f"turned_ready_{s}") for s in sources}
        turned_copied = {s: sem(f"turned_copied_{s}") for s in sources}
        out_ready = [sem(f"out_ready{k}") for k in range(NO)]
        value_ready = [sem(f"value_ready{k}") for k in range(NO)]
        remain_ready = [sem(f"remain_ready{k}") for k in range(NO)]
        middle_ready = [sem(f"middle_ready{k}") for k in range(NO)]
        split_ready = [sem(f"split_ready{k}") for k in range(NO)]
        stored = [[sem(f"stored{k}_{i}") for i in range(2)] for k in range(NO)]

        turned_stored = [sem(f"turned_stored{i}") for i in range(2)]

        def count(it, u, per=1, c=0):
            return it * (NI * per) + (u * per + c)

        def loop(eng, body):
            for u in range(NI):
                body(0, 0, u, u < 2)
            with eng.Fori(1, B // STEP) as it:
                for u in range(NI):
                    body(it, it * STEP if STEP > 1 else it, u, False)

        with nc.Block() as block:
            @block.sync
            def _(sp):
                sp.dma_start(ident[:, :], const["ident_f"]).then_inc(loaded, 16)
                for k, (_, kind, wk, bk, _, _) in enumerate(outs):
                    sp.dma_start(w[:, k, :], wk).then_inc(loaded, 16)
                    sp.dma_start(bias_col[:, k, :], bk.rearrange("(p o) -> p o", o=1)).then_inc(loaded, 16)
                    sp.dma_start(bias_row[:, k, :], bk.rearrange("(o n) -> o n", o=1)).then_inc(loaded, 16)

                def load(it, b, u, first):
                    db, r0, rows = items[u]
                    p = min(128, rows)
                    if not first:
                        if raw_outs:
                            sp.wait_ge(turned_ready["raw"], count(it, u, 1, -1))
                            stand_alone(sp, passed_sp)
                        if norm_outs:
                            sp.wait_ge(normed_ready, it * TILES + (before[u - 1] if u else before[NI - 1] - TILES))
                        stand_alone(sp, passed_sp)
                    sp.dma_start(raw[u % 2][0:p, 0:(rows + 127) // 128, :],
                                 ctx_dram[b, r0:r0 + rows, :].rearrange("(c p) n -> p c n", p=p)
                                 ).then_inc(raw_loaded[u % 2], 16)

                def store(it, b, u, first):
                    db, r0, rows = items[u]
                    for k, (_, kind, _, _, _, dest) in enumerate(outs):
                        if kind == "split":
                            sp.wait_ge(split_ready[k], count(it, u, 1, 1))
                            stand_alone(sp, passed_sp)
                            for j in range(PARTS):
                                sp.dma_start(dest[bass.ds(b + db, 1), :, j * D:j * D + D, r0:r0 + rows].rearrange("o h d n -> (o h) d n"),
                                             parts[k][u % 2][:, j, 0:rows]).then_inc(stored[k][u % 2], 16)
                        else:
                            p = min(128, rows)
                            sp.wait_ge(value_ready[k], count(it, u, 1, 1))
                            stand_alone(sp, passed_sp)
                            sp.dma_start(dest[bass.ds(b + db, 1), r0:r0 + rows, :].rearrange("o (c p) n -> p (o c) n", p=p),
                                         value[k][u % 2][0:p, 0:(rows + 127) // 128 * C].rearrange("p (c n) -> p c n", n=C)
                                         ).then_inc(stored[k][u % 2], 16)

                    if turned_dram is not None:
                        db, r0, rows = items[u]
                        sp.wait_ge(turned_copied["raw"], count(it, u, 1, 1))
                        stand_alone(sp, passed_sp)
                        sp.dma_start(turned_dram[bass.ds(b + db, 1), :, r0:r0 + rows].rearrange("o p n -> (o p) n"),
                                     turned["raw"][u % 2][:, 0:rows]).then_inc(turned_stored[u % 2], 16)

                def both(it, b, u, first):
                    if ctx_dram is not None:
                        load(it, b, u, first)
                    store(it, b, u, first)
                loop(sp, both)
                if turned_dram is not None:
                    for i in range(2):
                        sp.wait_ge(turned_stored[i], 16 * (NI // 2) * (B // STEP))
                for k in range(NO):
                    for i in range(2):
                        sp.wait_ge(stored[k][i], 16 * (PARTS if outs[k][1] == "split" else 1) * (NI // 2) * (B // STEP))

            @block.gpsimd
            def _(pool):
                pool.memset(ones[:, :], 1.0).then_inc(set_once, 1)
                pool.memset(eps_col[:, :], eps).then_inc(set_once, 1)
                pool.wait_ge(loaded, 16 * (1 + 3 * NO))
                for k in range(NO):
                    pool.tensor_scalar(bias_scaled[:, k, :], bias_col[:, k, :], outs[k][4], None, ALU.mult
                                       ).then_inc(bias_done, 1)
                pool.wait_ge(bias_done, NO)
                def split(it, b, u, first):
                    n = items[u][2]
                    for k, (_, kind, _, _, _, _) in enumerate(outs):
                        if kind == "split":
                            pool.wait_ge(remain_ready[k], count(it, u, 1, 1))
                            stand_alone(pool, passed_pool)
                            pool.tensor_copy(parts[k][u % 2][:, 1, 0:n], remains[k][:, 0:n]).then_inc(middle_ready[k], 1)
                            pool.wait_ge(middle_ready[k], count(it, u, 1, 1))
                            pool.tensor_tensor(parts[k][u % 2][:, 2, 0:n], remains[k][:, 0:n],
                                               parts[k][u % 2][:, 1, 0:n], ALU.subtract).then_inc(split_ready[k], 1)
                loop(pool, split)

            @block.tensor
            def _(pe):
                pe.wait_ge(loaded, 16 * (1 + 3 * NO))
                pe.wait_ge(set_once, 2)

                def body(it, b, u, first):
                    rows = items[u][2]
                    for s in sources:
                        if s == "raw":
                            pe.wait_ge(raw_loaded[u % 2], it * (16 * NI // 2) + 16 * (u // 2 + 1))
                        else:
                            pe.wait_ge(normed_ready, it * TILES + before[u + 1])
                        if not (first and u == 0):
                            pe.wait_ge(turned_copied[s], count(it, u))
                        src = raw if s == "raw" else normed
                        for i, (c0, p) in enumerate(tiles_of[u]):
                            last = pe.transpose(turned_ps[s][:, c0:c0 + p], src[u % 2][0:p, i, :], ident[0:p, 0:p])
                        last.then_inc(turned_ready[s], 1)
                    for k, (s, kind, _, _, _, _) in enumerate(outs):
                        pe.wait_ge(turned_copied[s], count(it, u, 1, 1))
                        if not (first and u == 0):
                            if kind == "split":
                                pe.wait_ge(value_ready[k], count(it, u, 2))
                            else:
                                pe.wait_ge(value_ready[k], count(it, u))
                        if kind == "split":
                            last = pe.matmul(out_ps[k][:, 0:rows], w[:, k, :], turned[s][u % 2][:, 0:rows],
                                             start=True, stop=True)
                        else:
                            for c0, p in tiles_of[u]:
                                pe.matmul(out_ps[k][0:p, c0:c0 + C], turned[s][u % 2][:, c0:c0 + p], w[:, k, :],
                                          start=True, stop=False)
                                last = pe.matmul(out_ps[k][0:p, c0:c0 + C], ones[:, 0:p], bias_row[:, k, :],
                                                 start=False, stop=True)
                        last.then_inc(out_ready[k], 1)
                loop(pe, body)

            @block.scalar
            def _(act):
                act.wait_ge(set_once, 2)
                act.wait_ge(bias_done, NO)
                def body(it, b, u, first):
                    db, _, rows = items[u]
                    p, nt = min(128, rows), (rows + 127) // 128
                    if norm_outs:
                        act.wait_ge(aggregated, it * TILES + before[u + 1])
                        act.activation(deviation[u % 2][0:p, 0:nt], mean_var[u % 2][0:p, 0:nt, 1], ACT.Sqrt,
                                       bias=eps_col[0:p, :]).then_inc(dev_ready, 1)
                    for s in sources:
                        act.wait_ge(turned_ready[s], count(it, u, 1, 1))
                        if not first:
                            for k in range(NO):
                                if outs[k][0] == s:
                                    act.wait_ge(out_ready[k], count(it, u, 1, -1))
                            if s == "raw" and turned_dram is not None:
                                act.wait_ge(turned_stored[u % 2], it * (16 * (NI // 2)) + 16 * (u // 2))
                        if s == "norm" and norm_cols is not None:
                            sc, sh = (columns[:, c, bass.ds(b + db, 1)] if len(columns.shape) == 3 else columns[:, c:c + 1]
                                      for c in norm_cols)
                            stand_alone(act, passed_act)
                            ins = act.activation(turned[s][u % 2][:, 0:rows], turned_ps[s][:, 0:rows], ACT.Identity,
                                                 bias=sh, scale=sc)
                        else:
                            ins = act.activation(turned[s][u % 2][:, 0:rows], turned_ps[s][:, 0:rows], ACT.Copy)
                        ins.then_inc(turned_copied[s], 1)
                    for k, (s, kind, _, _, scale, _) in enumerate(outs):
                        act.wait_ge(out_ready[k], count(it, u, 1, 1))
                        if kind == "split":
                            if not first:
                                stores = it * (16 * PARTS * (NI // 2)) + 16 * PARTS * (u // 2)
                                act.wait_ge(stored[k][u % 2], stores)
                            act.activation(parts[k][u % 2][:, 0, 0:rows], out_ps[k][:, 0:rows], ACT.Identity,
                                           bias=bias_scaled[:, k, :], scale=scale).then_inc(value_ready[k], 1)
                            act.activation(value[k][u % 2][:, 0:rows], out_ps[k][:, 0:rows], ACT.Identity,
                                           bias=bias_scaled[:, k, :], scale=scale).then_inc(value_ready[k], 1)
                        else:
                            if not first:
                                act.wait_ge(stored[k][u % 2], it * (16 * (NI // 2)) + 16 * (u // 2))
                            act.activation(value[k][u % 2][0:p, 0:nt * C], out_ps[k][0:p, 0:nt * C], ACT.Copy
                                           ).then_inc(value_ready[k], 1)
                loop(act, body)

            @block.vector
            def _(dve):
                def norm(it, b, u, first):
                    db, _, rows = items[u]
                    p, nt = min(128, rows), (rows + 127) // 128
                    if ctx_dram is not None:
                        dve.wait_ge(raw_loaded[u % 2], it * (16 * NI // 2) + 16 * (u // 2 + 1))

                    def src(i):
                        if ctx_dram is not None:
                            return raw[u % 2][0:p, i, :]
                        return X[:, bass.ds((b + db) * QT + i, 1), :].rearrange("p o n -> p (o n)")
                    for i in range(nt):
                        dve.bn_stats(stats[u % 2][0:p, i, :], src(i)).then_inc(stats_ready, 1)
                    for i in range(nt):
                        dve.wait_ge(stats_ready, it * TILES + before[u] + i + 1)
                        stand_alone(dve, passed_dve)
                        dve.bn_aggr(mean_var[u % 2][0:p, i, :], stats[u % 2][0:p, i, :]).then_inc(aggregated, 1)
                    dve.wait_ge(dev_ready, count(it, u, 1, 1))
                    dve.reciprocal(inverse[u % 2][0:p, 0:nt], deviation[u % 2][0:p, 0:nt]).then_inc(inv_ready, 1)
                    dve.wait_ge(inv_ready, count(it, u, 1, 1))
                    if not first:
                        dve.wait_ge(turned_ready["norm"], count(it, u, 1, -1))
                    for i in range(nt):
                        dve.tensor_scalar(normed[u % 2][0:p, i, :], src(i), mean_var[u % 2][0:p, i, 0:1],
                                          inverse[u % 2][0:p, i:i + 1], ALU.subtract, ALU.mult
                                          ).then_inc(normed_ready, 1)

                def body(it, b, u, first):
                    n = items[u][2]
                    if norm_outs:
                        norm(it, b, u, first)
                    for k, (_, kind, _, _, _, _) in enumerate(outs):
                        if kind == "split":
                            dve.wait_ge(value_ready[k], count(it, u, 2, 2))
                            if not (first and u == 0):
                                dve.wait_ge(split_ready[k], count(it, u))
                            dve.tensor_tensor(remains[k][:, 0:n], value[k][u % 2][:, 0:n],
                                              parts[k][u % 2][:, 0, 0:n], ALU.subtract).then_inc(remain_ready[k], 1)
                loop(dve, body)


def attention(nc, tag, X, q_parts, k_parts, v_rows, nk, w_out, out_bias, gate, const, topk=False):
    NCH = (nk + 127) // 128
    full = nk // 128
    size = [min(128, nk - c * 128) for c in range(NCH)]
    cross = nk > T
    NT = HQ * QT if cross else QT
    UNITS = 2 * NCH
    ST_RING, P_RING = 2, 3
    LOADS = 16 * (PARTS + PARTS * PARTS + 1)
    V_LOADS = 16 * (1 if full == NCH else 2)
    NCOL = HQ * QT
    NSTEP = 4 + (4 + 2 * NT if topk else 0)

    if cross:
        order, c = ["T0", "shift", "T1", "sum", 0], 1
        for t in range(2, NT):
            order.append(f"T{t}")
            if t == 3:
                order.append("project")
            order += list(range(c, min(c + 2, NCH)))
            c = min(c + 2, NCH)
        order += list(range(c, NCH))
    else:
        order = ["T0", "shift", "sum", 0, "T1", "project", 1]

    with phase(nc, tag) as (sb, ps, sem):
        ks = [sb(f"ks{g}", [128, HQ, nk], BF16) for g in range(QUADS)]
        qs = [sb(f"qs{g}", [128, HQ, T], BF16) for g in range(QUADS)]
        v_nat = sb("v_nat", [128, NCH, C], F32)
        v_pad = [sb(f"v_pad{i}", [128, NCH, HQ, 32], F32) for i in range(2)]
        probs = sb("probs", [128, P_RING, HQ * T], F32)
        below = sb("below", [128, ST_RING, 2 * T], BF16)
        rest = sb("rest", [128, nk if topk else 8], F32)
        top_a = sb("top_a", [128, NCOL, 8], F32)
        top_b = sb("top_b", [128, NCOL, 8], F32)
        stat = sb("stat", [128, 8, NCOL], F32)
        shift_parts = sb("shift_parts", [128, PARTS, NCOL], BF16)
        shift_rows = sb("shift_rows", [PARTS * NCOL, 128], BF16)
        o_t = sb("o_t", [128, T], F32)
        inv = sb("inv", [128, T], F32)
        o_norm = [sb(f"o_norm{g}", [128, T], F32) for g in range(QUADS)]
        gated = sb("gated", [128, QT, C], F32)
        w_sb = sb("w_sb", [128, QUADS, C], F32)
        bias_row = sb("bias_row", [1, C], F32)
        ones_row = sb("ones_row", [1, 128], F32)
        ident = sb("ident", [128, 128], BF16)
        neg_ident = sb("neg_ident", [128, 128], BF16)
        spread = sb("spread", [128, 128], F32)
        exp_bias = sb("exp_bias", [128, 1], F32)

        s_ps = ps("s_ps", [128, 4 * BANK])
        st_ps = ps("st_ps", [128, ST_RING, BANK])
        pv_ps = ps("pv_ps")[:, 0:T]
        misc_ps = ps("misc_ps")
        shift_ps = misc_ps[0:PARTS * NCOL, 0:64].bitcast(BF16)
        den_ps = misc_ps[:, BANK - T:BANK]
        y_ps = den_ps.rearrange("p (q n) -> p q n", q=QT)

        const_ready = sem("const_ready")
        rows_ready = sem("rows_ready")
        cleared = sem("cleared")
        set_once = sem("set_once")
        passed_pool, passed_dve = sem("passed_pool"), sem("passed_dve")
        load_ready = [sem(f"load_ready{g}") for g in range(QUADS)]
        v_ready = sem("v_ready")
        v_full_padded = sem("v_full_padded")
        v_padded = sem("v_padded")
        s_ready = sem("s_ready")
        s_free = sem("s_free")
        dve_step = sem("dve_step")
        parts_ready = sem("parts_ready")
        shift_t_ready = sem("shift_t_ready")
        shift_copied = sem("shift_copied")
        shift_ready = [sem(f"shift_ready{g}") for g in range(QUADS)]
        st_ready = sem("st_ready")
        below_ready = sem("below_ready")
        masked_ready = sem("masked_ready")
        p_ready = sem("p_ready")
        pv_done = sem("pv_done")
        o_copied = sem("o_copied")
        den_ready = sem("den_ready")
        inv_ready = sem("inv_ready")
        norm_ready = sem("norm_ready")
        y_ready = sem("y_ready")
        gated_ready = sem("gated_ready")
        y_used = sem("y_used")

        def count(b, g, per, c=0):
            return b * (QUADS * per) + (g * per + c)

        with nc.Block() as block:

            @block.sync
            def _(sp):
                sp.dma_start(w_sb[:, :, :], w_out).then_inc(const_ready, 16)
                sp.dma_start(bias_row[:, :], out_bias).then_inc(const_ready, 16)
                sp.dma_start(ident[:, :], const["ident_bf"]).then_inc(const_ready, 16)
                sp.dma_start(neg_ident[:, :], const["neg_ident_bf"]).then_inc(const_ready, 16)
                sp.dma_start(spread[:, :], const["spread"]).then_inc(const_ready, 16)
                sp.wait_ge(cleared, 2 * QUADS)
                for g in range(QUADS):
                    sp.dma_start(ks[g][ROW_MASK:ROW_END, :, :], const["k_rows"]).then_inc(rows_ready, 16)
                    sp.dma_start(qs[g][ROW_MASK:ROW_SHIFT, :, :], const["q_rows"]).then_inc(rows_ready, 16)

                def load(b, g):
                    for j in range(PARTS):
                        r = j * PARTS * D
                        sp.dma_start(ks[g][r:r + PARTS * D, :, :],
                                     k_parts[b, HQ * g:HQ * g + HQ, :, :].rearrange("h r n -> r h n")
                                     ).then_inc(load_ready[g], 16)
                        for i in range(PARTS):
                            sp.dma_start(qs[g][r + i * D:r + i * D + D, :, :],
                                         q_parts[b, HQ * g:HQ * g + HQ, j * D:j * D + D, :].rearrange("h d t -> d h t")
                                         ).then_inc(load_ready[g], 16)
                    sp.dma_start(qs[g][ROW_SHIFT:ROW_END, :, :], const["zero_rows"]).then_inc(load_ready[g], 16)

                def load_v(b):
                    sp.dma_start(v_nat[:, 0:full, :],
                                 v_rows[b, 0:full * 128, :].rearrange("(c p) n -> p c n", p=128)).then_inc(v_ready, 16)
                    if full < NCH:
                        sp.dma_start(v_nat[0:size[-1], full, :], v_rows[b, full * 128:nk, :]).then_inc(v_ready, 16)

                def send_shift(b, g):
                    sp.wait_ge(shift_copied, count(b, g, 1, 1))
                    for i in range(PARTS):
                        sp.dma_start(qs[g][ROW_SHIFT + i:ROW_SHIFT + i + 1, :, :],
                                     shift_rows[i * NCOL:(i + 1) * NCOL, :]).then_inc(shift_ready[g], 16)

                def reload(b, g):
                    sp.wait_ge(pv_done, count(b - 1, g, NCH, NCH))
                    load(b, g)

                load_v(0)
                for g in range(QUADS):
                    load(0, g)
                with sp.Fori(0, B - 1) as b:
                    for g in range(QUADS):
                        send_shift(b, g)
                        if g > 0:
                            reload(b + 1, g - 1)
                        if g == QUADS - 1:
                            sp.wait_ge(v_padded, b * QUADS + QUADS)
                            load_v(b + 1)
                    reload(b + 1, QUADS - 1)
                for g in range(QUADS):
                    send_shift(B - 1, g)

            @block.gpsimd
            def _(pool):
                for g in range(QUADS):
                    pool.memset(ks[g][:, :, :], 0.0).then_inc(cleared, 1)
                    pool.memset(qs[g][:, :, :], 0.0).then_inc(cleared, 1)
                for i in range(2):
                    pool.memset(v_pad[i][:, :, :, :], 1.0).then_inc(set_once, 1)
                pool.memset(ones_row[:, :], 1.0).then_inc(set_once, 1)
                pool.memset(exp_bias[:, :], EXP_BIAS if topk else 0.0).then_inc(set_once, 1)
                pool.wait_ge(set_once, 4)
                v_heads = v_nat[:, :, :].rearrange("p c (h d) -> p c h d", d=D)

                def pad(b, g, wait=True):
                    if g == 0:
                        pool.wait_ge(v_ready, b * V_LOADS + V_LOADS)
                    if wait:
                        pool.wait_ge(pv_done, count(b, g, NCH, -NCH))
                        stand_alone(pool, passed_pool)
                    for c0, c1, p in [(0, full, 128), (full, NCH, size[-1])]:
                        if c0 < c1:
                            last = pool.tensor_copy(v_pad[g % 2][0:p, c0:c1, :, 0:D],
                                                    v_heads[0:p, c0:c1, HQ * g:HQ * g + HQ, :])
                            if c1 == NCH:
                                last.then_inc(v_padded, 1)
                            else:
                                last.then_inc(v_full_padded, 1)

                for g in range(QUADS):
                    pad(0, g, wait=g >= 2)
                with pool.Fori(1, B) as b:
                    for g in range(QUADS):
                        pad(b, g)

            @block.tensor
            def _(pe):
                pe.wait_ge(const_ready, 5 * 16)
                pe.wait_ge(rows_ready, 2 * QUADS * 16)
                pe.wait_ge(set_once, 4)

                def tile(b, g, t, first=False):
                    if t == 0:
                        pe.wait_ge(load_ready[g], b * LOADS + LOADS)
                    if not first:
                        pe.wait_ge(s_free, count(b, g, NT, t))
                    heads = [t // QT] if cross else range(HQ)
                    qt = t % QT
                    for i, h in enumerate(heads):
                        for c0 in range(0, nk, BANK):
                            c1 = min(nk, c0 + BANK)
                            last = pe.matmul(s_ps[:, i * nk + c0:i * nk + c1], qs[g][:, h, qt * 128:qt * 128 + 128],
                                             ks[g][:, h, c0:c1], start=True, stop=True)
                    last.then_inc(s_ready, 1)

                def shift(b, g, first=False):
                    pe.wait_ge(parts_ready, count(b, g, 1, 1))
                    if not first:
                        pe.wait_ge(inv_ready, count(b, g, 1, -1))
                        if g == 1:
                            pe.wait_ge(y_used, b)
                    pe.transpose(shift_ps, shift_parts[:, :, :].rearrange("p i n -> p (i n)"), ident[:, :]
                                 ).then_inc(shift_t_ready, 1)

                def unit_scores(b, g, u, first=False):
                    c = u // 2
                    if u == 0:
                        pe.wait_ge(shift_ready[g], b * (16 * PARTS) + 16 * PARTS)
                    if u >= ST_RING:
                        pe.wait_ge(p_ready, count(b, g, UNITS, u - ST_RING + 1))
                    elif not first:
                        pe.wait_ge(p_ready, count(b, g, UNITS, -UNITS + 1 + max(
                            v for v in range(UNITS) if v % ST_RING == u % ST_RING)))
                    for i in range(2):
                        h = 2 * (u % 2) + i
                        last = pe.matmul(st_ps[0:size[c], u % ST_RING, i * T:(i + 1) * T],
                                         ks[g][:, h, c * 128:c * 128 + size[c]], qs[g][:, h, :],
                                         start=(i == 0), stop=not topk, skip_group_check=True)
                    last.then_inc(st_ready, 1)

                def unit_mask(b, g, u):
                    pe.wait_ge(below_ready, count(b, g, UNITS, u + 1))
                    n = size[u // 2]
                    pe.matmul(st_ps[0:n, u % ST_RING, :], neg_ident[:, 0:n],
                              below[:, u % ST_RING, :], start=False, stop=True, skip_group_check=True
                              ).then_inc(masked_ready, 1)

                def weigh(b, g, c, first=False):
                    if c == 0:
                        pe.wait_ge(v_padded, count(b, g, 1, 1))
                        if not first:
                            pe.wait_ge(o_copied, count(b, g, 1))
                    pe.wait_ge(p_ready, count(b, g, UNITS, 2 * c + 2))
                    for h in range(HQ):
                        last = pe.matmul(pv_ps[32 * h:32 * h + 32, :], v_pad[g % 2][0:size[c], c, h, :],
                                         probs[0:size[c], c % P_RING, h * T:(h + 1) * T],
                                         start=(c == 0), stop=(c == NCH - 1))
                    last.then_inc(pv_done, 1)

                def sum_rows(b, g, last=False):
                    pe.wait_ge(o_copied, count(b, g, 1, 1))
                    if not last:
                        pe.wait_ge(shift_copied, count(b, g, 1, 2))
                    pe.matmul(den_ps, spread[:, :], o_t[:, :], start=True, stop=True).then_inc(den_ready, 1)

                def project(b):
                    pe.wait_ge(norm_ready, b * QUADS + QUADS)
                    for qt in range(QT):
                        for g in range(QUADS):
                            pe.matmul(y_ps[:, qt, :], o_norm[g][:, qt * 128:qt * 128 + 128], w_sb[:, g, :],
                                      start=(g == 0), stop=False)
                        last = pe.matmul(y_ps[:, qt, :], ones_row[:, :], bias_row[:, :], start=False, stop=True)
                    last.then_inc(y_ready, 1)

                def step(b, g, start=False, end=False):
                    nb, ng = (b, g + 1) if g < QUADS - 1 else (b + 1, 0)
                    lb, lg = (b, g - 1) if g > 0 else (b - 1, QUADS - 1)
                    for what in order:
                        if what == "shift":
                            shift(b, g, first=start and g < 2)
                        elif what == "sum":
                            if not (start and g == 0):
                                sum_rows(lb, lg)
                        elif what == "project":
                            if g == 0 and not start:
                                project(lb)
                        elif isinstance(what, str):
                            if not (end and g == QUADS - 1):
                                tile(nb, ng, int(what[1:]))
                        else:
                            for u in (2 * what, 2 * what + 1):
                                unit_scores(b, g, u, first=start and g == 0)
                                if topk and u > 0:
                                    unit_mask(b, g, u - 1)
                                if u % 2 and u >= 3:
                                    weigh(b, g, (u - 3) // 2, first=start and g == 0)
                    if topk:
                        unit_mask(b, g, UNITS - 1)
                    weigh(b, g, NCH - 1, first=start and g == 0)

                for t in range(NT):
                    tile(0, 0, t, first=t == 0)
                for g in range(QUADS):
                    step(0, g, start=True)
                with pe.Fori(1, B - 1) as b:
                    for g in range(QUADS):
                        step(b, g)
                for g in range(QUADS):
                    step(B - 1, g, end=True)
                sum_rows(B - 1, QUADS - 1, last=True)
                project(B - 1)

            @block.scalar
            def _(act):
                act.wait_ge(set_once, 4)

                def copy_shift(b, g, first=False):
                    act.wait_ge(shift_t_ready, count(b, g, 1, 1))
                    if not first:
                        lb, lg = (b, g - 1) if g > 0 else (b - 1, QUADS - 1)
                        act.wait_ge(shift_ready[lg], lb * (16 * PARTS) + 16 * PARTS)
                    act.activation(shift_rows[:, :], shift_ps, ACT.Copy).then_inc(shift_copied, 1)

                def exp_unit(b, g, u, first=False):
                    c, n = u // 2, size[u // 2]
                    if topk:
                        act.wait_ge(masked_ready, count(b, g, UNITS, u + 1))
                    else:
                        act.wait_ge(st_ready, count(b, g, UNITS, u + 1))
                    if u % 2 == 0:
                        if c >= P_RING:
                            act.wait_ge(pv_done, count(b, g, NCH, c - P_RING + 1))
                        elif not first:
                            act.wait_ge(pv_done, count(b, g, NCH, -NCH + 1 + max(
                                v for v in range(NCH) if v % P_RING == c % P_RING)
                                if NCH > c % P_RING else 0))
                    half = u % 2
                    act.activation(probs[0:n, c % P_RING, half * 2 * T:(half + 1) * 2 * T],
                                   st_ps[0:n, u % ST_RING, :], ACT.Exp, bias=exp_bias[0:n, :]).then_inc(p_ready, 1)

                def copy_sums(b, g, first=False):
                    act.wait_ge(pv_done, count(b, g, NCH, NCH))
                    if not first:
                        act.wait_ge(norm_ready, count(b, g, 1))
                    act.activation(o_t[:, :], pv_ps, ACT.Copy).then_inc(o_copied, 1)

                def step(b, g, start=False):
                    first = start and g == 0
                    copy_shift(b, g, first)
                    for u in range(UNITS):
                        if topk:
                            n = size[u // 2]
                            act.wait_ge(st_ready, count(b, g, UNITS, u + 1))
                            act.activation(below[0:n, u % ST_RING, :], st_ps[0:n, u % ST_RING, :], ACT.Relu,
                                           scale=-1e20).then_inc(below_ready, 1)
                            if u > 0:
                                exp_unit(b, g, u - 1, first)
                        else:
                            exp_unit(b, g, u, first)
                    if topk:
                        exp_unit(b, g, UNITS - 1, first)
                    copy_sums(b, g, first)

                for g in range(QUADS):
                    step(0, g, start=True)
                with act.Fori(1, B) as b:
                    for g in range(QUADS):
                        step(b, g)

            @block.vector
            def _(dve):
                def link(ins, b, g, k):
                    ins.then_inc(dve_step, 1)
                    dve.wait_ge(dve_step, count(b, g, NSTEP, k + 1))

                def tile(b, g, t):
                    dve.wait_ge(s_ready, count(b, g, NT, t + 1))
                    if topk:
                        stand_alone(dve, passed_dve)
                        link(dve.max(top_a[:, t, :], s_ps[:, 0:nk]), b, g, 2 * t)
                        stand_alone(dve, passed_dve)
                        dve.match_replace(rest[:, :], top_a[:, t, :], s_ps[:, 0:nk], -3e38).then_inc(s_free, 1)
                        dve.wait_ge(s_free, count(b, g, NT, t + 1))
                        stand_alone(dve, passed_dve)
                        link(dve.max(top_b[:, t, :], rest[:, :]), b, g, 2 * t + 1)
                    elif cross:
                        dve.tensor_reduce(stat[:, 0, t:t + 1], s_ps[:, 0:nk], AX.X, ALU.max, negate=True).then_inc(s_free, 1)
                    else:
                        dve.tensor_reduce(stat[:, 0, t:NCOL:QT], s_ps[:, 0:HQ * nk].rearrange("p (h n) -> p h n", h=HQ),
                                          AX.X, ALU.max, negate=True).then_inc(s_free, 1)

                def split_shift(b, g, first=False):
                    k = 2 * NT if topk else 0
                    if topk:
                        biggest, least = top_a[:, :, 0], top_b[:, :, 7]
                        link(dve.tensor_scalar(stat[:, 1, :], biggest, -1.0, EXP_SPAN, ALU.mult, ALU.add), b, g, k)
                        link(dve.scalar_tensor_tensor(stat[:, 2, :], least, -1.0, biggest, ALU.mult, ALU.max), b, g, k + 1)
                        link(dve.scalar_tensor_tensor(stat[:, 3, :], stat[:, 2, :], TIE_MARGIN, least,
                                                      ALU.mult, ALU.subtract), b, g, k + 2)
                        ins = dve.tensor_tensor(stat[:, 0, :], stat[:, 1, :], stat[:, 3, :], ALU.min)
                        k += 3
                        link(ins, b, g, k)
                        k += 1
                    else:
                        dve.wait_ge(s_free, count(b, g, NT, NT))
                    if not first:
                        dve.wait_ge(shift_t_ready, count(b, g, 1))
                    link(dve.tensor_copy(shift_parts[:, 0, :], stat[:, 0, :]), b, g, k)
                    link(dve.tensor_tensor(stat[:, 4, :], stat[:, 0, :], shift_parts[:, 0, :], ALU.subtract), b, g, k + 1)
                    link(dve.tensor_copy(shift_parts[:, 1, :], stat[:, 4, :]), b, g, k + 2)
                    link(dve.tensor_tensor(stat[:, 5, :], stat[:, 4, :], shift_parts[:, 1, :], ALU.subtract), b, g, k + 3)
                    dve.tensor_copy(shift_parts[:, 2, :], stat[:, 5, :]).then_inc(parts_ready, 1)

                def normalise(b, g):
                    dve.wait_ge(den_ready, count(b, g, 1, 1))
                    dve.reciprocal(inv[:, :], den_ps).then_inc(inv_ready, 1)
                    dve.wait_ge(inv_ready, count(b, g, 1, 1))
                    dve.tensor_tensor(o_norm[g][:, :], o_t[:, :], inv[:, :], ALU.mult).then_inc(norm_ready, 1)

                def add_to_x(b):
                    dve.wait_ge(y_ready, b + 1)
                    x = X[:, bass.ds(b * QT, QT), :]
                    if gate is None:
                        dve.tensor_tensor(x, x, y_ps, ALU.add).then_inc(y_used, 1)
                    else:
                        for qt in range(QT):
                            dve.tensor_tensor(gated[:, qt, :], y_ps[:, qt, :], gate[:, bass.ds(b * C, C)], ALU.mult
                                              ).then_inc(gated_ready, 1)
                        dve.wait_ge(gated_ready, b * QT + QT)
                        dve.tensor_tensor(x, x, gated[:, :, :], ALU.add).then_inc(y_used, 1)

                def step(b, g, start=False, end=False):
                    nb, ng = (b, g + 1) if g < QUADS - 1 else (b + 1, 0)
                    lb, lg = (b, g - 1) if g > 0 else (b - 1, QUADS - 1)
                    for what in order:
                        if what == "sum":
                            if not (start and g == 0):
                                normalise(lb, lg)
                        elif what == "project":
                            if g == 0 and not start:
                                add_to_x(lb)
                        elif what != "shift" and isinstance(what, str):
                            if not (end and g == QUADS - 1):
                                tile(nb, ng, int(what[1:]))
                    if not (end and g == QUADS - 1):
                        split_shift(nb, ng)

                for t in range(NT):
                    tile(0, 0, t)
                split_shift(0, 0, first=True)
                for g in range(QUADS):
                    step(0, g, start=True)
                with dve.Fori(1, B - 1) as b:
                    for g in range(QUADS):
                        step(b, g)
                for g in range(QUADS):
                    step(B - 1, g, end=True)
                normalise(B - 1, QUADS - 1)
                add_to_x(B - 1)
def row_stats(nc, tag, X, negative_mean, inverse, eps):
    with phase(nc, tag) as (sb, ps, sem):
        stats = sb("stats", [128, NTILE, 6])
        mean_var = sb("mean_var", [128, NTILE, 2])
        deviation = sb("deviation", [128, NTILE])
        eps_col = sb("eps_col", [128, 1])
        eps_ready, stats_ready, aggregated, dev_ready, done = (
            sem("eps_ready"), sem("stats_ready"), sem("aggregated"), sem("dev_ready"), sem("done"))
        with nc.Block() as block:
            @block.vector
            def _(dve):
                dve.memset(eps_col[:, :], eps).then_inc(eps_ready, 1)
                for i in range(NTILE):
                    dve.bn_stats(stats[:, i, :], X[:, i, :]).then_inc(stats_ready, 1)
                for i in range(NTILE):
                    dve.wait_ge(stats_ready, i + 1)
                    dve.bn_aggr(mean_var[:, i, :], stats[:, i, :]).then_inc(aggregated, 1)
                dve.wait_ge(aggregated, NTILE)
                dve.tensor_scalar(negative_mean[:, :], mean_var[:, :, 0], -1.0, None, ALU.mult).then_inc(done, 1)
                dve.wait_ge(dev_ready, 1)
                dve.reciprocal(inverse[:, :], deviation[:, :]).then_inc(done, 1)

            @block.scalar
            def _(act):
                act.wait_ge(eps_ready, 1)
                act.wait_ge(aggregated, NTILE)
                act.activation(deviation[:, :], mean_var[:, :, 1], ACT.Sqrt, bias=eps_col[:, :]).then_inc(dev_ready, 1)


def evidence(nc, tag, X, negative_mean, inverse, cond_sb, probs_out, p, ctx, ctx_turned, nx_dram, ev_dram, const):
    NCH = (LC + 127) // 128
    FULL = LC // 128
    size = [min(128, LC - c * 128) for c in range(NCH)]
    E = 3
    GROUPS = [list(range(c, min(c + 4, NCH))) for c in range(0, NCH, 4)]
    NG = len(GROUPS)
    with phase(nc, tag) as (sb, ps, sem):
        wq, wk_t, wv = sb("wq", [128, C]), sb("wk_t", [128, C]), sb("wv", [128, C])
        router = sb("router", [128, 3, E])
        router_bias = sb("router_bias", [1, E])
        gamma, beta = sb("gamma", [128, 1]), sb("beta", [128, 1])
        ident = sb("ident", [128, 128])
        ones = sb("ones", [1, 128])
        rows = [sb(f"rows{i}", [128, NCH, C]) for i in range(2)]
        turned = [sb(f"turned{i}", [128, LC]) for i in range(2)]
        normed = [sb(f"normed{i}", [128, QT, C]) for i in range(2)]
        anchor = [sb(f"anchor{i}", [128, 128]) for i in range(2)]
        nx = [sb(f"nx{i}", [128, T]) for i in range(2)]
        q1 = [sb(f"q1_{i}", [128, T]) for i in range(2)]
        q2 = [sb(f"q2_{i}", [128, T]) for i in range(2)]
        weights = [sb(f"weights{i}", [128, LC]) for i in range(2)]
        w_turned = [sb(f"w_turned{i}", [128, NCH, 128]) for i in range(2)]
        top = sb("top", [128, 2])
        sums = sb("sums", [128, 2])
        inv_sums = sb("inv_sums", [128, 2])
        mixed = [sb(f"mixed{i}", [128, QT, C]) for i in range(2)]
        mixed_t = [sb(f"mixed_t{i}", [128, T]) for i in range(2)]
        ev = [sb(f"ev{i}", [128, T]) for i in range(2)]
        logits_top = sb("logits_top", [128, QT])
        exps = sb("exps", [128, QT, E])
        exp_sums = sb("exp_sums", [128, QT])
        exp_inv = sb("exp_inv", [128, QT])

        s_ps = ps("s_ps", [128, 4 * BANK])
        turn_ps = [ps(f"turn_ps{i}") for i in range(2)]
        small_ps, mix_ps = ps("small_ps"), ps("mix_ps")

        loaded, set_once = sem("loaded"), sem("set_once")
        ctx_loaded = [sem(f"ctx_loaded{i}") for i in range(2)]
        normed_ready, anchor_ready, nx_turned, nx_ready = (
            sem("normed_ready"), sem("anchor_ready"), sem("nx_turned"), sem("nx_ready"))
        q1_made, q1_ready, q2_made, q2_ready = sem("q1_made"), sem("q1_ready"), sem("q2_made"), sem("q2_ready")
        s_ready, top_ready, w_ready, inv_ready = sem("s_ready"), sem("top_ready"), sem("w_ready"), sem("inv_ready")
        w_turn_ready, w_turn_copied = sem("w_turn_ready"), sem("w_turn_copied")
        mix_ready, mixed_ready, mixed_turned, mixed_copied = (
            sem("mix_ready"), sem("mixed_ready"), sem("mixed_turned"), sem("mixed_copied"))
        ev_made, ev_ready, logits_made, logits_max, exps_ready, exps_inv, probs_done = (
            sem("ev_made"), sem("ev_ready"), sem("logits_made"), sem("logits_max"), sem("exps_ready"),
            sem("exps_inv"), sem("probs_done"))
        stored = [sem(f"stored{i}") for i in range(2)]
        passed_sp, passed_dve = sem("passed_sp"), sem("passed_dve")

        def count(it, u, per=1, c=0):
            return it * (2 * per) + (u * per + c)

        def loop(eng, body):
            body(0, 0, 0, True)
            body(0, 0, 1, True)
            with eng.Fori(1, B // 2) as it:
                body(it, it * 2, 0, False)
                body(it, it * 2, 1, False)

        with nc.Block() as block:
            @block.sync
            def _(sp):
                for dst, src in [(wq[:, :], p["Wq"]), (wk_t[:, :], p["Wk_t"]), (wv[:, :], p["Wv"]),
                                 (router[:, :, :], p["router_W"].rearrange("(k p) e -> p k e", p=128)),
                                 (router_bias[:, :], p["router_b"].rearrange("(o n) -> o n", o=1)),
                                 (gamma[:, :], p["ln_gamma"].rearrange("(p o) -> p o", o=1)),
                                 (beta[:, :], p["ln_beta"].rearrange("(p o) -> p o", o=1)),
                                 (ident[:, :], const["ident_f"])]:
                    sp.dma_start(dst, src).then_inc(loaded, 16)

                def load(b, u):
                    one = bass.ds(b + u, 1)
                    sp.dma_start(rows[u][:, 0:FULL, :],
                                 ctx[one, 0:FULL * 128, :].rearrange("o (c p) n -> p (o c) n", p=128)
                                 ).then_inc(ctx_loaded[u], 16)
                    sp.dma_start(rows[u][0:size[-1], FULL, :],
                                 ctx[one, FULL * 128:LC, :].rearrange("o p n -> (o p) n")).then_inc(ctx_loaded[u], 16)
                    sp.dma_start(turned[u][:, :], ctx_turned[one, :, :].rearrange("o p n -> (o p) n")
                                 ).then_inc(ctx_loaded[u], 16)

                def body(it, b, u, first):
                    one = bass.ds(b + u, 1)
                    sp.wait_ge(ev_ready, count(it, u, 1, 1))
                    stand_alone(sp, passed_sp)
                    sp.dma_start(nx_dram[one, :, :].rearrange("o p n -> (o p) n"), nx[u][:, :]).then_inc(stored[u], 16)
                    sp.dma_start(ev_dram[one, :, :].rearrange("o p n -> (o p) n"), ev[u][:, :]).then_inc(stored[u], 16)
                load(0, 0)
                load(0, 1)
                with sp.Fori(0, B // 2 - 1) as it:
                    for u in range(2):
                        body(it, it * 2, u, False)
                        sp.wait_ge(mix_ready, count(it, u, QT, QT))
                        stand_alone(sp, passed_sp)
                        load(it * 2 + 2, u)
                for u in range(2):
                    body(B // 2 - 1, B - 2, u, False)
                for u in range(2):
                    sp.wait_ge(stored[u], 32 * (B // 2))

            @block.tensor
            def _(pe):
                pe.wait_ge(loaded, 8 * 16)
                pe.wait_ge(set_once, 1)

                def turn_rows(it, u, first):
                    pe.wait_ge(normed_ready, count(it, u, 1, 1))
                    if not (first and u == 0):
                        pe.wait_ge(probs_done, count(it, u))
                    for qt in range(QT):
                        last = pe.transpose(small_ps[:, qt * 128:qt * 128 + 128], normed[u][:, qt, :], ident[:, :])
                    last.then_inc(nx_turned, 1)

                def query1(it, u):
                    pe.wait_ge(nx_ready, count(it, u, 1, 1))
                    pe.matmul(small_ps[:, 0:T], wq[:, :], nx[u][:, :], start=True, stop=True).then_inc(q1_made, 1)

                def query2(it, u):
                    pe.wait_ge(q1_ready, count(it, u, 1, 1))
                    pe.matmul(small_ps[:, 0:T], wk_t[:, :], q1[u][:, :], start=True, stop=True).then_inc(q2_made, 1)

                def scores(it, u, qt, first):
                    if qt == 0:
                        pe.wait_ge(q2_ready, count(it, u, 1, 1))
                        pe.wait_ge(ctx_loaded[u], it * 48 + 48)
                    if not (first and u == 0 and qt == 0):
                        pe.wait_ge(w_ready, count(it, u, QT, qt))
                    for c0 in range(0, LC, BANK):
                        c1 = min(LC, c0 + BANK)
                        last = pe.matmul(s_ps[:, c0:c1], q2[u][:, qt * 128:qt * 128 + 128], turned[u][:, c0:c1],
                                         start=True, stop=True)
                    last.then_inc(s_ready, 1)

                def mix(it, u, qt, first):
                    pe.wait_ge(w_ready, count(it, u, QT, qt + 1))
                    for n, group in enumerate(GROUPS):
                        if not (first and u == 0 and qt == 0 and n < 2):
                            pe.wait_ge(w_turn_copied, it * (2 * QT * NG) + (u * QT + qt) * NG + n - 1)
                        for i, c in enumerate(group):
                            last = pe.transpose(turn_ps[n % 2][0:size[c], i * 128:i * 128 + 128],
                                                weights[qt][:, c * 128:c * 128 + size[c]], ident[:, :])
                        last.then_inc(w_turn_ready, 1)
                    if not (first and u == 0 and qt == 0):
                        pe.wait_ge(mixed_ready, count(it, u, QT, qt))
                    for n, group in enumerate(GROUPS):
                        pe.wait_ge(w_turn_copied, it * (2 * QT * NG) + (u * QT + qt) * NG + n + 1)
                        for c in group:
                            last = pe.matmul(mix_ps[:, 0:C], w_turned[qt][0:size[c], c, :], rows[u][0:size[c], c, :],
                                             start=(c == 0), stop=(c == NCH - 1))
                    last.then_inc(mix_ready, 1)

                def finish(it, u):
                    pe.wait_ge(mixed_ready, count(it, u, QT, QT))
                    for qt in range(QT):
                        last = pe.transpose(small_ps[:, qt * 128:qt * 128 + 128], mixed[u][:, qt, :], ident[:, :])
                    last.then_inc(mixed_turned, 1)
                    pe.wait_ge(mixed_copied, count(it, u, 1, 1))
                    pe.matmul(small_ps[:, 0:T], wv[:, :], mixed_t[u][:, :], start=True, stop=True).then_inc(ev_made, 1)
                    pe.wait_ge(ev_ready, count(it, u, 1, 1))
                    pe.wait_ge(anchor_ready, count(it, u, 1, 1))
                    for qt in range(QT):
                        out = small_ps[:, qt * E:qt * E + E]
                        q = slice(qt * 128, qt * 128 + 128)
                        pe.matmul(out, nx[u][:, q], router[:, 0, :], start=True, stop=False)
                        pe.matmul(out, ev[u][:, q], router[:, 1, :], start=False, stop=False)
                        pe.matmul(out, anchor[u][:, :], router[:, 2, :], start=False, stop=False)
                        last = pe.matmul(out, ones[:, :], router_bias[:, :], start=False, stop=True)
                    last.then_inc(logits_made, 1)

                def body(it, b, u, first):
                    turn_rows(it, u, first)
                    query1(it, u)
                    query2(it, u)
                    scores(it, u, 0, first)
                    scores(it, u, 1, first)
                    mix(it, u, 0, first)
                    mix(it, u, 1, first)
                    finish(it, u)
                loop(pe, body)

            @block.scalar
            def _(act):
                act.wait_ge(loaded, 8 * 16)

                def body(it, b, u, first):
                    act.wait_ge(nx_turned, count(it, u, 1, 1))
                    if not first:
                        act.wait_ge(stored[u], it * 32)
                    act.activation(nx[u][:, :], small_ps[:, 0:T], ACT.Identity, bias=beta[:, :], scale=gamma[:, :]
                                   ).then_inc(nx_ready, 1)
                    act.wait_ge(q1_made, count(it, u, 1, 1))
                    act.activation(q1[u][:, :], small_ps[:, 0:T], ACT.Copy, scale=float(C) ** -0.5).then_inc(q1_ready, 1)
                    act.wait_ge(q2_made, count(it, u, 1, 1))
                    act.activation(q2[u][:, :], small_ps[:, 0:T], ACT.Copy).then_inc(q2_ready, 1)
                    for qt in range(QT):
                        act.wait_ge(top_ready, count(it, u, QT, qt + 1))
                        if not (first and u == 0):
                            act.wait_ge(w_turn_ready, it * (2 * QT * NG) + (u * QT + qt) * NG - (QT - 1) * NG)
                            act.wait_ge(inv_ready, count(it, u, QT, qt - 1))
                        act.activation(weights[qt][:, :], s_ps[:, 0:LC], ACT.Exp, bias=top[:, qt:qt + 1],
                                       accum_out=sums[:, qt:qt + 1]).then_inc(w_ready, 1)
                    for qt in range(QT):
                        act.wait_ge(mix_ready, count(it, u, QT, qt + 1))
                        act.wait_ge(inv_ready, count(it, u, QT, qt + 1))
                        act.activation(mixed[u][:, qt, :], mix_ps[:, 0:C], ACT.Copy, scale=inv_sums[:, qt:qt + 1]
                                       ).then_inc(mixed_ready, 1)
                    act.wait_ge(mixed_turned, count(it, u, 1, 1))
                    act.activation(mixed_t[u][:, :], small_ps[:, 0:T], ACT.Copy).then_inc(mixed_copied, 1)
                    act.wait_ge(ev_made, count(it, u, 1, 1))
                    act.activation(ev[u][:, :], small_ps[:, 0:T], ACT.Copy).then_inc(ev_ready, 1)
                    for qt in range(QT):
                        act.wait_ge(logits_max, count(it, u, QT, QT))
                        if not (first and u == 0):
                            act.wait_ge(probs_done, count(it, u))
                        act.activation(exps[:, qt, :], small_ps[:, qt * E:qt * E + E], ACT.Exp,
                                       bias=logits_top[:, qt:qt + 1], accum_out=exp_sums[:, qt:qt + 1]
                                       ).then_inc(exps_ready, 1)
                loop(act, body)

            @block.vector
            def _(dve):
                dve.memset(ones[:, :], 1.0).then_inc(set_once, 1)

                def norm(it, b, u, first):
                    if not first:
                        dve.wait_ge(nx_turned, count(it, u, 1, -1))
                        dve.wait_ge(logits_made, count(it, u, 1, -1))
                        stand_alone(dve, passed_dve)
                    dve.tensor_copy(anchor[u][:, :], cond_sb[:, bass.ds(b + u, 1)].broadcast_to([128, 128])
                                    ).then_inc(anchor_ready, 1)
                    tile = (b + u) * QT
                    for qt in range(QT):
                        ins = dve.tensor_scalar(normed[u][:, qt, :], X[:, bass.ds(tile + qt, 1), :].rearrange("p o n -> p (o n)"),
                                                negative_mean[:, bass.ds(tile + qt, 1)], inverse[:, bass.ds(tile + qt, 1)],
                                                ALU.add, ALU.mult)
                    ins.then_inc(normed_ready, 1)

                def body(it, b, u, first):
                    norm(it, b, u, first)
                    for qt in range(QT):
                        dve.wait_ge(s_ready, count(it, u, QT, qt + 1))
                        dve.tensor_reduce(top[:, qt:qt + 1], s_ps[:, 0:LC], AX.X, ALU.max, negate=True
                                          ).then_inc(top_ready, 1)
                    for qt in range(QT):
                        dve.wait_ge(w_ready, count(it, u, QT, qt + 1))
                        if not (first and u == 0):
                            dve.wait_ge(mixed_ready, count(it, u, QT, qt - 1))
                        dve.reciprocal(inv_sums[:, qt:qt + 1], sums[:, qt:qt + 1]).then_inc(inv_ready, 1)
                        for n, group in enumerate(GROUPS):
                            dve.wait_ge(w_turn_ready, it * (2 * QT * NG) + (u * QT + qt) * NG + n + 1)
                            p_, k = size[group[-1]], len(group)
                            dve.tensor_copy(w_turned[qt][0:p_, group[0]:group[0] + k, :],
                                            turn_ps[n % 2][0:p_, 0:k * 128].rearrange("p (c n) -> p c n", n=128)
                                            ).then_inc(w_turn_copied, 1)
                    dve.wait_ge(logits_made, count(it, u, 1, 1))
                    for qt in range(QT):
                        dve.tensor_reduce(logits_top[:, qt:qt + 1], small_ps[:, qt * E:qt * E + E], AX.X, ALU.max,
                                          negate=True).then_inc(logits_max, 1)
                    dve.wait_ge(exps_ready, count(it, u, QT, QT))
                    dve.reciprocal(exp_inv[:, :], exp_sums[:, :]).then_inc(exps_inv, 1)
                    dve.wait_ge(exps_inv, count(it, u, 1, 1))
                    stand_alone(dve, passed_dve)
                    for qt in range(QT):
                        ins = dve.tensor_scalar(probs_out[:, bass.ds((b + u) * QT + qt, 1), :].rearrange("p o e -> p (o e)"),
                                                exps[:, qt, :], exp_inv[:, qt:qt + 1], None, ALU.mult)
                    ins.then_inc(probs_done, 1)
                loop(dve, body)


def experts(nc, tag, X, probs, columns, cols, p, nx_dram, ev_dram, const):
    E, RB = 3, 2
    NB = E * RB + 1
    with phase(nc, tag) as (sb, ps, sem):
        w1 = sb("w1", [128, NB, 2, 128])
        w2 = sb("w2", [128, E * RB, C])
        b2 = sb("b2", [1, E, C])
        gate_w2, out_w = sb("gate_w2", [128, C]), sb("out_w", [128, C])
        gate_b2, out_b = sb("gate_b2", [1, C]), sb("out_b", [1, C])
        ones, ident = sb("ones", [1, 128]), sb("ident", [128, 128])
        nx = [sb(f"nx{i}", [128, T]) for i in range(2)]
        ev = [sb(f"ev{i}", [128, T]) for i in range(2)]
        hidden = [sb(f"hidden{i}", [128, NB, T]) for i in range(2)]
        tanh = [sb(f"tanh{i}", [128, QT, C]) for i in range(2)]
        routed = sb("routed", [128, QT, C])
        routed_t = sb("routed_t", [128, T])
        product = sb("product", [128, QT, C])
        hidden_ps = [ps(f"hidden_ps{i}") for i in range(2)]
        y_ps = [ps(f"y_ps{i}") for i in range(QT)]
        gate_ps, turned_ps, out_ps = ps("gate_ps"), ps("turned_ps"), ps("out_ps")

        loaded, set_once = sem("loaded"), sem("set_once")
        in_loaded = [sem(f"in_loaded{i}") for i in range(2)]
        hidden_made, hidden_ready, y_made, y_taken = sem("hidden_made"), sem("hidden_ready"), sem("y_made"), sem("y_taken")
        gate_made, tanh_ready, routed_step = sem("gate_made"), sem("tanh_ready"), sem("routed_step")
        turned_made, turned_ready, out_made, product_ready, x_done = (
            sem("turned_made"), sem("turned_ready"), sem("out_made"), sem("product_ready"), sem("x_done"))
        passed_sp, passed_act, passed_dve = sem("passed_sp"), sem("passed_act"), sem("passed_dve")
        NLOAD = 5 + E * (1 + 2 * RB) + 1

        def count(it, u, per=1, c=0):
            return it * (2 * per) + (u * per + c)

        def loop(eng, body):
            body(0, 0, 0, True)
            body(0, 0, 1, True)
            with eng.Fori(1, B // 2) as it:
                body(it, it * 2, 0, False)
                body(it, it * 2, 1, False)

        with nc.Block() as block:
            @block.sync
            def _(sp):
                row = lambda a: a.rearrange("(o n) -> o n", o=1)
                weights = [(gate_w2[:, :], p["gate_w2"]), (out_w[:, :], p["out_w"]), (gate_b2[:, :], row(p["gate_b2"])),
                           (out_b[:, :], row(p["out_b"])), (ident[:, :], const["ident_f"])]
                for e in range(E):
                    weights.append((b2[:, e, :], p["e_b2"][e:e + 1, :]))
                    for r in range(RB):
                        k = e * RB + r
                        weights.append((w2[:, k, :], p["e_w2"][e, r * 128:r * 128 + 128, :]))
                        weights.append((w1[:, k, :, :], p["e_w1"][e, 0:2 * C, r * 128:r * 128 + 128]
                                        .rearrange("(s c) n -> c s n", s=2)))
                weights.append((w1[:, NB - 1, :, :], p["gate_w1"][0:2 * C, :].rearrange("(s c) n -> c s n", s=2)))
                for dst, src in weights:
                    sp.dma_start(dst, src).then_inc(loaded, 16)
                assert len(weights) == NLOAD

                def body(it, b, u, first):
                    if not first:
                        sp.wait_ge(hidden_made, count(it, u, NB, -NB))
                        stand_alone(sp, passed_sp)
                    one = bass.ds(b + u, 1)
                    sp.dma_start(nx[u][:, :], nx_dram[one, :, :].rearrange("o p n -> (o p) n")).then_inc(in_loaded[u], 16)
                    sp.dma_start(ev[u][:, :], ev_dram[one, :, :].rearrange("o p n -> (o p) n")).then_inc(in_loaded[u], 16)
                loop(sp, body)

            @block.tensor
            def _(pe):
                pe.wait_ge(loaded, 16 * NLOAD)
                pe.wait_ge(set_once, 1)

                def first_part(it, b, u, first):
                    pe.wait_ge(in_loaded[u], it * 32 + 32)
                    for k in range(NB):
                        if not (first and u == 0 and k < 2):
                            pe.wait_ge(hidden_ready, count(it, u, NB, k - 1))
                        pe.matmul(hidden_ps[k % 2][:, 0:T], w1[:, k, 0, :], nx[u][:, :], start=True, stop=False)
                        pe.matmul(hidden_ps[k % 2][:, 0:T], w1[:, k, 1, :], ev[u][:, :], start=False, stop=True
                                  ).then_inc(hidden_made, 1)

                def second_part(it, b, u, first):
                    for qt in range(QT):
                        q = slice(qt * 128, qt * 128 + 128)
                        if qt == 0:
                            pe.wait_ge(hidden_ready, count(it, u, NB, NB))
                        if not (first and u == 0):
                            pe.wait_ge(y_taken, count(it, u, QT, qt - 1))
                        for e in range(E):
                            out = y_ps[qt][:, e * C:e * C + C]
                            for r in range(RB):
                                pe.matmul(out, hidden[u][:, e * RB + r, q], w2[:, e * RB + r, :], start=(r == 0), stop=False)
                            last = pe.matmul(out, ones[:, :], b2[:, e, :], start=False, stop=True)
                        last.then_inc(y_made, 1)
                    if not (first and u == 0):
                        pe.wait_ge(tanh_ready, count(it, u))
                    for qt in range(QT):
                        out = gate_ps[:, qt * C:qt * C + C]
                        pe.matmul(out, hidden[u][:, NB - 1, qt * 128:qt * 128 + 128], gate_w2[:, :], start=True, stop=False)
                        last = pe.matmul(out, ones[:, :], gate_b2[:, :], start=False, stop=True)
                    last.then_inc(gate_made, 1)

                def third_part(it, b, u, first):
                    pe.wait_ge(routed_step, count(it, u, QT * E, QT * E))
                    if not (first and u == 0):
                        pe.wait_ge(turned_ready, count(it, u))
                    for qt in range(QT):
                        last = pe.transpose(turned_ps[:, qt * 128:qt * 128 + 128], routed[:, qt, :], ident[:, :])
                    last.then_inc(turned_made, 1)
                    pe.wait_ge(turned_ready, count(it, u, 1, 1))
                    if not (first and u == 0):
                        pe.wait_ge(product_ready, count(it, u))
                    for qt in range(QT):
                        out = out_ps[:, qt * C:qt * C + C]
                        pe.matmul(out, routed_t[:, qt * 128:qt * 128 + 128], out_w[:, :], start=True, stop=False)
                        last = pe.matmul(out, ones[:, :], out_b[:, :], start=False, stop=True)
                    last.then_inc(out_made, 1)

                def body(it, b, u, first):
                    first_part(it, b, u, first)
                    second_part(it, b, u, first)
                    third_part(it, b, u, first)
                loop(pe, body)

            @block.scalar
            def _(act):
                def body(it, b, u, first):
                    for k in range(NB):
                        act.wait_ge(hidden_made, count(it, u, NB, k + 1))
                        if not first and k == 0:
                            act.wait_ge(gate_made, count(it, u, 1, -1))
                        if k == 0:
                            stand_alone(act, passed_act)
                        act.activation(hidden[u][:, k, :], hidden_ps[k % 2][:, 0:T], ACT.Silu,
                                       bias=columns[:, cols + k, bass.ds(b + u, 1)]).then_inc(hidden_ready, 1)
                    act.wait_ge(gate_made, count(it, u, 1, 1))
                    if not first:
                        act.wait_ge(product_ready, count(it, u, 1, -1))
                    act.activation(tanh[u][:, :, :], gate_ps[:, 0:QT * C].rearrange("p (q n) -> p q n", q=QT), ACT.Tanh,
                                   scale=0.5).then_inc(tanh_ready, 1)
                    act.wait_ge(turned_made, count(it, u, 1, 1))
                    act.activation(routed_t[:, :], turned_ps[:, 0:T], ACT.Copy).then_inc(turned_ready, 1)
                loop(act, body)

            @block.vector
            def _(dve):
                dve.memset(ones[:, :], 1.0).then_inc(set_once, 1)

                def body(it, b, u, first):
                    tile = (b + u) * QT
                    for qt in range(QT):
                        dve.wait_ge(y_made, count(it, u, QT, qt + 1))
                        if qt == 0 and not (first and u == 0):
                            dve.wait_ge(turned_made, count(it, u))
                        stand_alone(dve, passed_dve)
                        for e in range(E):
                            y = y_ps[qt][:, e * C:e * C + C]
                            pr = probs[:, bass.ds(tile + qt, 1), e]
                            if e == 0:
                                ins = dve.tensor_scalar(routed[:, qt, :], y, pr, None, ALU.mult)
                            else:
                                ins = dve.scalar_tensor_tensor(routed[:, qt, :], y, pr, routed[:, qt, :], ALU.mult, ALU.add)
                            ins.then_inc(routed_step, 1)
                            dve.wait_ge(routed_step, count(it, u, QT * E, qt * E + e + 1))
                            if e == E - 1:
                                dve.sem_inc(y_taken, 1)
                    dve.wait_ge(out_made, count(it, u, 1, 1))
                    dve.wait_ge(tanh_ready, count(it, u, 1, 1))
                    dve.scalar_tensor_tensor(product[:, :, :], tanh[u][:, :, :], 1.0,
                                             out_ps[:, 0:QT * C].rearrange("p (q n) -> p q n", q=QT), ALU.add, ALU.mult
                                             ).then_inc(product_ready, 1)
                    dve.wait_ge(product_ready, count(it, u, 1, 1))
                    stand_alone(dve, passed_dve)
                    x = X[:, bass.ds(tile, QT), :]
                    dve.scalar_tensor_tensor(x, product[:, :, :], 0.5, x, ALU.mult, ALU.add).then_inc(x_done, 1)
                loop(dve, body)


def mlp(nc, tag, X, negative_mean, inverse, columns, norm_cols, w1_d, b1_d, w2_d, b2_d, gate, swiglu, const):
    NK = w2_d.shape[0] // 128
    with phase(nc, tag) as (sb, ps, sem):
        NW = NK * (2 if swiglu else 1)
        w1 = sb("w1", [128, NW, 128])
        b1 = sb("b1", [128, NW, 1])
        w2 = sb("w2", [128, NK, C])
        b2, ones, ident = sb("b2", [1, C]), sb("ones", [1, 128]), sb("ident", [128, 128])
        normed = [sb(f"normed{i}", [128, QT, C]) for i in range(2)]
        x_t = [sb(f"x_t{i}", [128, T]) for i in range(2)]
        silu = [sb(f"silu{i}", [128, T]) for i in range(2)]
        hidden = [sb(f"hidden{i}", [128, NK, T]) for i in range(2)]
        gated = sb("gated", [128, QT, C])
        turned_ps = ps("turned_ps")
        a_ps = [ps(f"a_ps{i}") for i in range(2)]
        b_ps = [ps(f"b_ps{i}") for i in range(2)] if swiglu else None
        out_ps = [ps(f"out_ps{i}") for i in range(2)]
        loaded, set_once = sem("loaded"), sem("set_once")
        normed_ready, turned_made, turned_ready = sem("normed_ready"), sem("turned_made"), sem("turned_ready")
        a_made, b_made, silu_ready, hidden_ready = sem("a_made"), sem("b_made"), sem("silu_ready"), sem("hidden_ready")
        out_made, gated_ready, x_done = sem("out_made"), sem("gated_ready"), sem("x_done")
        passed_act, passed_dve = sem("passed_act"), sem("passed_dve")

        def count(it, u, per=1, c=0):
            return it * (2 * per) + (u * per + c)

        def loop(eng, body):
            body(0, 0, 0, True)
            body(0, 0, 1, True)
            with eng.Fori(1, B // 2) as it:
                body(it, it * 2, 0, False)
                body(it, it * 2, 1, False)

        with nc.Block() as block:
            @block.sync
            def _(sp):
                for dst, src in [(w1[:, :, :], w1_d.rearrange("c (k n) -> c k n", n=128)),
                                 (w2[:, :, :], w2_d.rearrange("(k p) n -> p k n", p=128)),
                                 (b2[:, :], b2_d.rearrange("(o n) -> o n", o=1)), (ident[:, :], const["ident_f"])]:
                    sp.dma_start(dst, src).then_inc(loaded, 16)
                for k in range(NW):
                    sp.dma_start(b1[:, k, :], b1_d[k * 128:(k + 1) * 128].rearrange("(p o) -> p o", o=1)
                                 ).then_inc(loaded, 16)

            @block.tensor
            def _(pe):
                pe.wait_ge(loaded, (4 + NW) * 16)
                pe.wait_ge(set_once, 1)

                def body(it, b, u, first):
                    pe.wait_ge(normed_ready, count(it, u, 1, 1))
                    if not (first and u == 0):
                        pe.wait_ge(turned_ready, count(it, u))
                    for qt in range(QT):
                        last = pe.transpose(turned_ps[:, qt * 128:qt * 128 + 128], normed[u][:, qt, :], ident[:, :])
                    last.then_inc(turned_made, 1)
                    pe.wait_ge(turned_ready, count(it, u, 1, 1))
                    for k in range(NK):
                        if not (first and u == 0 and k < 2):
                            pe.wait_ge(silu_ready if swiglu else hidden_ready, count(it, u, NK, k - 1))
                        pe.matmul(a_ps[k % 2][:, 0:T], w1[:, k, :], x_t[u][:, :], start=True, stop=True).then_inc(a_made, 1)
                        if swiglu:
                            if not (first and u == 0 and k < 2):
                                pe.wait_ge(hidden_ready, count(it, u, NK, k - 1))
                            pe.matmul(b_ps[k % 2][:, 0:T], w1[:, NK + k, :], x_t[u][:, :], start=True, stop=True
                                      ).then_inc(b_made, 1)
                    pe.wait_ge(hidden_ready, count(it, u, NK, NK))
                    if not first:
                        pe.wait_ge(gated_ready, count(it, u, QT, -QT))
                    for qt in range(QT):
                        out = out_ps[u][:, qt * C:qt * C + C]
                        for k in range(NK):
                            pe.matmul(out, hidden[u][:, k, qt * 128:qt * 128 + 128], w2[:, k, :], start=(k == 0), stop=False)
                        last = pe.matmul(out, ones[:, :], b2[:, :], start=False, stop=True)
                    last.then_inc(out_made, 1)
                loop(pe, body)

            @block.scalar
            def _(act):
                act.wait_ge(loaded, (4 + NW) * 16)

                def body(it, b, u, first):
                    act.wait_ge(turned_made, count(it, u, 1, 1))
                    stand_alone(act, passed_act)
                    if not first:
                        act.wait_ge(b_made if swiglu else a_made, count(it, u, NK, -NK))
                        stand_alone(act, passed_act)
                    sc, sh = (columns[:, c, bass.ds(b + u, 1)] for c in norm_cols)
                    act.activation(x_t[u][:, :], turned_ps[:, 0:T], ACT.Identity, bias=sh, scale=sc
                                   ).then_inc(turned_ready, 1)
                    for k in range(NK):
                        act.wait_ge(a_made, count(it, u, NK, k + 1))
                        if swiglu:
                            if not (first and u == 0 and k < 2):
                                act.wait_ge(hidden_ready, count(it, u, NK, k - 1))
                            act.activation(silu[k % 2][:, :], a_ps[k % 2][:, 0:T], ACT.Silu, bias=b1[:, k, :]
                                           ).then_inc(silu_ready, 1)
                        else:
                            if k == 0 and not first:
                                act.wait_ge(out_made, count(it, u, 1, -1))
                            act.activation(hidden[u][:, k, :], a_ps[k % 2][:, 0:T], ACT.Gelu_apprx_tanh,
                                           bias=b1[:, k, :]).then_inc(hidden_ready, 1)
                loop(act, body)

            @block.vector
            def _(dve):
                dve.wait_ge(loaded, (4 + NW) * 16)
                dve.memset(ones[:, :], 1.0).then_inc(set_once, 1)

                def body(it, b, u, first):
                    tile = (b + u) * QT
                    if not first:
                        dve.wait_ge(turned_made, count(it, u, 1, -1))
                        stand_alone(dve, passed_dve)
                    for qt in range(QT):
                        ins = dve.tensor_scalar(normed[u][:, qt, :], X[:, bass.ds(tile + qt, 1), :].rearrange("p o n -> p (o n)"),
                                                negative_mean[:, bass.ds(tile + qt, 1)], inverse[:, bass.ds(tile + qt, 1)],
                                                ALU.add, ALU.mult)
                    ins.then_inc(normed_ready, 1)
                    if swiglu:
                        for k in range(NK):
                            dve.wait_ge(silu_ready, count(it, u, NK, k + 1))
                            dve.wait_ge(b_made, count(it, u, NK, k + 1))
                            if k == 0 and not first:
                                dve.wait_ge(out_made, count(it, u, 1, -1))
                            dve.scalar_tensor_tensor(hidden[u][:, k, :], b_ps[k % 2][:, 0:T], b1[:, NK + k, :],
                                                     silu[k % 2][:, :], ALU.add, ALU.mult).then_inc(hidden_ready, 1)
                    dve.wait_ge(out_made, count(it, u, 1, 1))
                    stand_alone(dve, passed_dve)
                    for qt in range(QT):
                        dve.tensor_tensor(gated[:, qt, :], out_ps[u][:, qt * C:qt * C + C], gate[:, bass.ds((b + u) * C, C)],
                                          ALU.mult).then_inc(gated_ready, 1)
                    dve.wait_ge(gated_ready, count(it, u, QT, QT))
                    stand_alone(dve, passed_dve)
                    x = X[:, bass.ds(tile, QT), :]
                    dve.tensor_tensor(x, x, gated[:, :, :], ALU.add).then_inc(x_done, 1)
                loop(dve, body)




def network(nc, p, x_in, x_out):
    def dram(name, shape, dt=F32):
        return nc.dram_tensor(name, shape, dt).ap()

    def block_of(w, k):
        return w[:, k * C:(k + 1) * C]

    def bias_of(b, k):
        return b[k * C:(k + 1) * C]

    const = {"ident_f": p["ident_f"], "ident_bf": p["ident_bf"], "neg_ident_bf": p["neg_ident_bf"],
             "spread": p["spread"], "zero_rows": p["zero_rows"]}
    plain = {True: {**const, "k_rows": p["k_rows_cross"], "q_rows": p["q_rows_plain"]},
             False: {**const, "k_rows": p["k_rows_self"], "q_rows": p["q_rows_plain"]}}
    windows = {**const, "k_rows": p["k_rows_window"], "q_rows": p["q_rows_window"]}
    ctx, n1, n2, n3, n0 = p["ctx_1024"], "L1_xcond_", "L2_xcond_", "L3_xcond_", "L0_xcond_"
    l0 = {k[len(n0):]: v for k, v in p.items() if k.startswith(n0)}

    nx_dram, ev_dram = dram("nx_rows", [B, 128, T]), dram("ev_rows", [B, 128, T])
    ctx_turned = dram("ctx_turned", [B, 128, LC])
    q_parts = dram("q_parts", [B, H, PARTS * D, T], BF16)
    k_self, v_self = dram("k_self", [B, H, PARTS * D, T], BF16), dram("v_self", [B, T, C])
    k_cross = [dram(f"k_cross{i}", [B, H, PARTS * D, LC], BF16) for i in range(3)]
    v_cross = [dram(f"v_cross{i}", [B, LC, C]) for i in range(3)]

    ada1, b_ada1, ada2, b_ada2 = p[n1 + "w_ada"], p[n1 + "b_ada"], p[n2 + "adaln_w"], p[n2 + "adaln_b"]
    ss_q, b_ss_q, ss_kv, b_ss_kv = p[n3 + "Wss_q"], p[n3 + "bss_q"], p[n3 + "Wss_kv"], p[n3 + "bss_kv"]
    blocks = [(block_of(ada1, k), bias_of(b_ada1, k), True, True) for k in (1, 4, 7)]
    blocks += [(block_of(ada2, k), bias_of(b_ada2, k), True, True) for k in (1, 4)]
    blocks += [(block_of(ss_q, 0), bias_of(b_ss_q, 0), True, True), (block_of(ss_kv, 0), bias_of(b_ss_kv, 0), True, True)]
    blocks += [(block_of(ada1, k), bias_of(b_ada1, k), True, False) for k in (0, 3, 6)]
    blocks += [(block_of(ada2, k), bias_of(b_ada2, k), True, False) for k in (0, 3)]
    blocks += [(block_of(ss_q, 1), bias_of(b_ss_q, 1), True, False), (block_of(ss_kv, 1), bias_of(b_ss_kv, 1), True, False)]
    NSC = 7
    MSA, MCA, MLP, SA2, FF2, Q3, KV3 = ((k, k + NSC) for k in range(NSC))
    EXPERT_COLS = len(blocks)
    for e in range(3):
        for r in range(2):
            blocks.append((l0["e_w1"][e, 2 * C:3 * C, r * 128:(r + 1) * 128],
                           l0["e_b1"][e, r * 128:(r + 1) * 128], False, False))
    blocks.append((l0["gate_w1"][2 * C:3 * C, :], l0["gate_b1"], False, False))
    scale = float(D) ** -0.5
    tokens = [(0, 0, T), (1, 0, T)]
    ctx_items = [(0, r, min(BANK, LC - r)) for r in range(0, LC, BANK)]

    with ExitStack() as stack:
        def sb(name, shape):
            return stack.enter_context(nc.sbuf_tensor(name, shape, F32))
        X = sb("X", [128, NTILE, C])
        silu_t, cond_sb = sb("silu_t", [128, B]), sb("cond_sb", [128, B])
        columns = sb("columns", [128, len(blocks), B])
        gate = sb("gate", [128, B * C])
        negative_mean, inverse = sb("negative_mean", [128, NTILE]), sb("inverse", [128, NTILE])
        probs = sb("probs", [128, NTILE, 3])
        x_loaded = stack.enter_context(nc.semaphore("x_loaded"))
        x_stored = stack.enter_context(nc.semaphore("x_stored"))

        with nc.Block() as block:
            @block.sync
            def _(sp):
                for b in range(B):
                    sp.dma_start(X[:, b * QT:(b + 1) * QT, :], x_in[b].rearrange("(q p) c -> p q c", p=128)
                                 ).then_inc(x_loaded, 16)
                sp.wait_ge(x_loaded, 16 * B)

        modulation(nc, "modulation", p["cond_t"], silu_t, cond_sb, columns, blocks)
        prepare(nc, "ctx", X, ctx_items, columns, 1e-5,
                [("split", block_of(p[n1 + "w_kv"], 0), bias_of(p[n1 + "b_kv"], 0), 1.0, k_cross[0]),
                 ("rows", block_of(p[n1 + "w_kv"], 1), bias_of(p[n1 + "b_kv"], 1), 1.0, v_cross[0]),
                 ("split", block_of(p[n2 + "kv_w"], 0), bias_of(p[n2 + "kv_b"], 0), 1.0, k_cross[1]),
                 ("rows", block_of(p[n2 + "kv_w"], 1), bias_of(p[n2 + "kv_b"], 1), 1.0, v_cross[1])],
                [("split", block_of(p[n3 + "Wkv"], 0), bias_of(p[n3 + "bkv"], 0), 1.0, k_cross[2]),
                 ("rows", block_of(p[n3 + "Wkv"], 1), bias_of(p[n3 + "bkv"], 1), 1.0, v_cross[2])],
                KV3, const, ctx, ctx_turned)

        row_stats(nc, "stats0", X, negative_mean, inverse, 1e-5)
        evidence(nc, "evidence", X, negative_mean, inverse, cond_sb, probs, l0, ctx, ctx_turned, nx_dram, ev_dram, const)
        experts(nc, "experts", X, probs, columns, EXPERT_COLS, l0, nx_dram, ev_dram, const)

        def self_attention(tag, w_qkv, b_qkv, cols, w_out, b_out, g, consts):
            prepare(nc, tag + "_qkv", X, tokens, columns, 1e-6, [],
                    [("split", block_of(w_qkv, 0), bias_of(b_qkv, 0), scale, q_parts),
                     ("split", block_of(w_qkv, 1), bias_of(b_qkv, 1), 1.0, k_self),
                     ("rows", block_of(w_qkv, 2), bias_of(b_qkv, 2), 1.0, v_self)], cols, const)
            attention(nc, tag, X, q_parts, k_self, v_self, T, w_out, b_out, g, consts)

        def cross_attention(tag, w_q, b_q, cols, eps, kv, w_out, b_out, g, topk=False):
            prepare(nc, tag + "_q", X, tokens, columns, eps, [], [("split", w_q, b_q, scale, q_parts)], cols, const)
            attention(nc, tag, X, q_parts, k_cross[kv], v_cross[kv], LC, w_out, b_out, g, plain[True], topk)

        gate_rows(nc, "gate_msa", silu_t, gate, block_of(ada1, 2), bias_of(b_ada1, 2))
        self_attention("self1", p[n1 + "w_qkv"], p[n1 + "b_qkv"], MSA, p["w_so_quads"], p["b_so_row"], gate, windows)
        gate_rows(nc, "gate_mca", silu_t, gate, block_of(ada1, 5), bias_of(b_ada1, 5))
        cross_attention("cross1", p[n1 + "w_q"], p[n1 + "b_q"], MCA, 1e-6, 0, p["w_co_quads"], p["b_co_row"], gate, True)
        gate_rows(nc, "gate_mlp", silu_t, gate, block_of(ada1, 8), bias_of(b_ada1, 8))
        row_stats(nc, "stats1", X, negative_mean, inverse, 1e-6)
        mlp(nc, "mlp1", X, negative_mean, inverse, columns, MLP, p[n1 + "w_m1"], p[n1 + "b_m1"], p[n1 + "w_m2"],
            p[n1 + "b_m2"], gate, True, const)

        gate_rows(nc, "gate_sa", silu_t, gate, block_of(ada2, 2), bias_of(b_ada2, 2))
        self_attention("self2", p[n2 + "qkv_w"], p[n2 + "qkv_b"], SA2, p["sa_proj_quads"], p["sa_proj_b_row"], gate,
                       plain[False])
        cross_attention("cross2", p[n2 + "q_w"], p[n2 + "q_b"], None, 1e-6, 1, p["ca_proj_quads"], p["ca_proj_b_row"], None)
        gate_rows(nc, "gate_ff", silu_t, gate, block_of(ada2, 5), bias_of(b_ada2, 5))
        row_stats(nc, "stats2", X, negative_mean, inverse, 1e-6)
        mlp(nc, "mlp2", X, negative_mean, inverse, columns, FF2, p[n2 + "fc1_w"], p[n2 + "fc1_b"], p[n2 + "fc2_w"],
            p[n2 + "fc2_b"], gate, False, const)

        cross_attention("cross3", p[n3 + "Wq"], p[n3 + "bq"], Q3, 1e-5, 2, p["Wp_quads"], p["bp_row"], None)

        with nc.Block() as block:
            @block.sync
            def _(sp):
                for b in range(B):
                    sp.dma_start(x_out[b].rearrange("(q p) c -> p q c", p=128), X[:, b * QT:(b + 1) * QT, :]
                                 ).then_inc(x_stored, 16)
                sp.wait_ge(x_stored, 16 * B)


def layout(inputs):
    import numpy as np
    bf16 = np.dtype("bfloat16")
    arrays = {k: np.ascontiguousarray(v) for k, v in inputs.items()}
    arrays["cond_t"] = np.ascontiguousarray(arrays.pop("cond_1024").T)
    arrays["L0_xcond_Wk_t"] = np.ascontiguousarray(arrays.pop("L0_xcond_Wk").T)
    for name in ("L1_xcond_w_so", "L1_xcond_w_co", "L2_xcond_sa_proj_w", "L2_xcond_ca_proj_w", "L3_xcond_Wp"):
        w = arrays.pop(name)
        padded = np.zeros((HQ, 32, QUADS, C), w.dtype)
        padded[:, 0:D] = w.reshape(QUADS, HQ, D, C).transpose(1, 2, 0, 3)
        short = name.split("xcond_")[1]
        arrays[(short[:-2] if short.endswith("_w") else short) + "_quads"] = padded.reshape(128, QUADS, C)
    for name in ("L1_xcond_b_so", "L1_xcond_b_co", "L2_xcond_sa_proj_b", "L2_xcond_ca_proj_b", "L3_xcond_bp"):
        arrays[name.split("xcond_")[1] + "_row"] = arrays.pop(name).reshape(1, C)
    arrays["ident_f"] = np.eye(128, dtype=np.float32)
    arrays["ident_bf"] = np.eye(128).astype(bf16)
    arrays["neg_ident_bf"] = (-np.eye(128)).astype(bf16)
    m = np.arange(128)
    spread = np.zeros((128, 128), np.float32)
    spread[32 * (m // 32) + D, m] = 1
    arrays["spread"] = spread
    arrays["zero_rows"] = np.zeros((PARTS, HQ, T), bf16)
    window = (np.arange(T) - SHIFT) % T // WINDOW
    for name, n in (("cross", LC), ("self", T), ("window", T)):
        k_rows = np.zeros((NWIN + PARTS, HQ, n), np.float32)
        k_rows[NWIN:] = 1
        if name == "window":
            k_rows[0:NWIN] = (window == np.arange(NWIN)[:, None])[:, None, :]
        arrays["k_rows_" + name] = k_rows.astype(bf16)
    q_rows = np.zeros((NWIN, HQ, T), np.float32)
    arrays["q_rows_plain"] = q_rows.astype(bf16)
    q_rows[:] = np.where(window == np.arange(NWIN)[:, None], 0.0, -30000.0)[:, None, :]
    arrays["q_rows_window"] = q_rows.astype(bf16)
    return arrays


def kernel(**inputs):
    import concourse.bacc as bacc
    import numpy as np
    from concourse.bass_utils import run_bass_kernel_spmd

    nc = bacc.Bacc("TRN2", target_bir_lowering=False, num_devices=1)
    arrays = layout(inputs)
    p = {k: nc.dram_tensor(k, list(a.shape), mybir.dt.from_np(a.dtype), kind="ExternalInput").ap()
         for k, a in arrays.items()}
    out = nc.dram_tensor("out", [B, T, C], F32, kind="ExternalOutput").ap()
    network(nc, p, p["x"], out)
    result = run_bass_kernel_spmd(nc, [arrays], core_ids=[0])
    return np.array(result.results[0]["out"])
```

```python
from contextlib import ExitStack, contextmanager

import concourse.bass as bass
from concourse import mybir
from concourse.alu_op_type import AluOpType as ALU

ACT = mybir.ActivationFunctionType
AX = mybir.AxisListType
F32 = mybir.dt.float32
BF16 = mybir.dt.bfloat16

B, T, C = 16, 256, 128
LC = 1601
H, D = 16, 8
HQ = 4
QUADS = H // HQ
QT = T // 128
NTILE = B * QT
BANK = 512
PARTS = 3
ROWS_QK = PARTS * PARTS * D
WINDOW, SHIFT = 64, 32
NWIN = T // WINDOW
ROW_SHIFT = ROWS_QK
ROW_MASK = ROW_SHIFT + PARTS
ROW_END = ROW_MASK + NWIN
PACE = {"topk": (4, 8, 1, 6, 11), "cross": (9, 3, 1, 3, 6), "self": (2, 2, 0, 1, 1)}
EXP_BIAS = -40.0
EXP_SPAN = 104.0
TIE_MARGIN = 2.0 ** -21


@contextmanager
def phase(nc, tag):
    made = []
    with ExitStack() as ctx:
        def sb(name, shape, dt=F32):
            return ctx.enter_context(nc.sbuf_tensor(f"{tag}_{name}", shape, dt))

        def ps(name, shape=(128, BANK), dt=F32):
            return ctx.enter_context(nc.psum_tensor(f"{tag}_{name}", list(shape), dt))

        def sem(name):
            made.append(ctx.enter_context(nc.semaphore(f"{tag}_{name}")))
            return made[-1]

        yield sb, ps, sem
        with nc.Block() as block:
            @block.gpsimd
            def _(pool):
                for s in made:
                    pool.sem_clear(s)


def stand_alone(eng, passed):
    eng.sem_inc(passed, 1)


def modulation(nc, tag, cond_t, silu_t, cond_sb, columns, blocks):
    n = len(blocks)
    plus_one = sum(1 for x in blocks if x[3])
    with phase(nc, tag) as (sb, ps, sem):
        w = sb("w", [128, n, C])
        bias = sb("bias", [128, n, 1])
        out_ps = ps("out")
        loaded, silu_ready, out_ready, added = sem("loaded"), sem("silu_ready"), sem("out_ready"), sem("added")
        out3 = out_ps[:, 0:n * B].rearrange("p (k b) -> p k b", k=n)
        with nc.Block() as block:
            @block.sync
            def _(sp):
                sp.dma_start(cond_sb[:, :], cond_t).then_inc(loaded, 16)
                for k, (wk, bk, _, _) in enumerate(blocks):
                    sp.dma_start(w[:, k, :], wk).then_inc(loaded, 16)
                    sp.dma_start(bias[:, k, :], bk.rearrange("(p o) -> p o", o=1)).then_inc(loaded, 16)

            @block.scalar
            def _(act):
                act.wait_ge(loaded, 16 * (2 * n + 1))
                act.activation(silu_t[:, :], cond_sb[:, :], ACT.Silu).then_inc(silu_ready, 1)

            @block.tensor
            def _(pe):
                pe.wait_ge(loaded, 16 * (2 * n + 1))
                pe.wait_ge(silu_ready, 1)
                for k, (_, _, of_silu, _) in enumerate(blocks):
                    src = silu_t if of_silu else cond_sb
                    last = pe.matmul(out3[:, k, :], w[:, k, :], src[:, :], start=True, stop=True)
                last.then_inc(out_ready, 1)

            @block.vector
            def _(dve):
                dve.wait_ge(out_ready, 1)
                dve.tensor_tensor(columns[:, :, :], out3, bias[:, :, :].broadcast_to([128, n, B]), ALU.add
                                  ).then_inc(added, 1)
                dve.wait_ge(added, 1)
                dve.tensor_scalar(columns[:, 0:plus_one, :], columns[:, 0:plus_one, :], 1.0, None, ALU.add
                                  ).then_inc(added, 1)


def gate_rows(nc, tag, silu_t, gate, w_block, bias):
    PER_BANK = BANK // C
    with phase(nc, tag) as (sb, ps, sem):
        w = sb("w", [128, C])
        bias_row = sb("bias_row", [1, C])
        ones = sb("ones", [1, 128])
        banks = [ps(f"rows{i}") for i in range(B // PER_BANK)]
        loaded, ones_ready, rows_ready, copied = sem("loaded"), sem("ones_ready"), sem("rows_ready"), sem("copied")
        with nc.Block() as block:
            @block.sync
            def _(sp):
                sp.dma_start(w[:, :], w_block).then_inc(loaded, 16)
                sp.dma_start(bias_row[:, :], bias.rearrange("(o n) -> o n", o=1)).then_inc(loaded, 16)

            @block.tensor
            def _(pe):
                pe.wait_ge(loaded, 32)
                pe.wait_ge(ones_ready, 1)
                for b in range(B):
                    out = banks[b // PER_BANK][:, b % PER_BANK * C:(b % PER_BANK + 1) * C]
                    pe.matmul(out, silu_t[:, b:b + 1].broadcast_to([128, 128]), w[:, :], start=True, stop=False)
                    last = pe.matmul(out, ones[:, :], bias_row[:, :], start=False, stop=True)
                    if b % PER_BANK == PER_BANK - 1:
                        last.then_inc(rows_ready, 1)

            @block.vector
            def _(dve):
                dve.memset(ones[:, :], 1.0).then_inc(ones_ready, 1)

            @block.scalar
            def _(act):
                for i in range(B // PER_BANK):
                    act.wait_ge(rows_ready, i + 1)
                    act.activation(gate[:, i * BANK:(i + 1) * BANK], banks[i][:, :], ACT.Copy).then_inc(copied, 1)


def prepare(nc, tag, X, items, columns, eps, raw_outs, norm_outs, norm_cols, const, ctx_dram=None, turned_dram=None):
    NI = len(items)
    STORES = {"split": 1, "split_q": PARTS, "rows": 1}
    STEP = 1 + max(i[0] for i in items)
    MAXT = max((i[2] + 127) // 128 for i in items)
    outs = [("raw", *o) for o in raw_outs] + [("norm", *o) for o in norm_outs]
    NO = len(outs)
    sources = (["raw"] if raw_outs else []) + (["norm"] if norm_outs else [])
    n_split = sum(o[1] != "rows" for o in outs)
    n_rows = NO - n_split
    tiles_of = [[(i * 128, min(128, r - i * 128)) for i in range((r + 127) // 128)] for _, _, r in items]
    TILES = sum(len(t) for t in tiles_of)
    before = [sum(len(t) for t in tiles_of[:u]) for u in range(NI + 1)]
    with phase(nc, tag) as (sb, ps, sem):
        w = sb("w", [128, NO, C])
        bias_col = sb("bias_col", [128, NO, 1])
        bias_scaled = sb("bias_scaled", [128, NO, 1])
        bias_row = sb("bias_row", [1, NO, C])
        ones = sb("ones", [1, 128])
        eps_col = sb("eps_col", [128, 1])
        ident = sb("ident", [128, 128])
        raw = [sb(f"raw{i}", [128, MAXT, C]) for i in range(NI if ctx_dram is not None else 0)]
        normed = [sb(f"normed{i}", [128, MAXT, C]) for i in range(2)]
        stats = [sb(f"stats{i}", [128, MAXT, 6]) for i in range(2)]
        mean_var = [sb(f"mean_var{i}", [128, MAXT, 2]) for i in range(2)]
        deviation = [sb(f"deviation{i}", [128, MAXT]) for i in range(2)]
        inverse = [sb(f"inverse{i}", [128, MAXT]) for i in range(2)]
        turned = {s: [sb(f"turned_{s}{i}", [128, MAXT * 128]) for i in range(2)] for s in sources}
        value = [[sb(f"value{k}_{i}", [128, MAXT * 128]) for i in range(2)] for k in range(NO)]
        parts = [[sb(f"parts{k}_{i}", [128, PARTS, MAXT * 128], BF16) if outs[k][1] != "rows" else None
                  for i in range(2)] for k in range(NO)]
        remains = [sb(f"remains{k}", [128, MAXT * 128]) for k in range(NO)]
        turned_ps = {s: ps(f"turned_{s}") for s in sources}
        out_ps = [ps(f"out{k}") for k in range(NO)]

        loaded, set_once, bias_done = sem("loaded"), sem("set_once"), sem("bias_done")
        passed_sp, passed_pool, passed_act, passed_dve = (sem(f"passed_{e}") for e in ("sp", "pool", "act", "dve"))
        raw_loaded = [sem(f"raw_loaded{i}") for i in range(NI)]
        stats_ready, aggregated, dev_ready, inv_ready = (
            sem("stats_ready"), sem("aggregated"), sem("dev_ready"), sem("inv_ready"))
        normed_ready = sem("normed_ready")
        turned_ready = {s: sem(f"turned_ready_{s}") for s in sources}
        turned_copied = {s: sem(f"turned_copied_{s}") for s in sources}
        out_ready = [sem(f"out_ready{k}") for k in range(NO)]
        value_ready = [sem(f"value_ready{k}") for k in range(NO)]
        remain_ready = [sem(f"remain_ready{k}") for k in range(NO)]
        middle_ready = [sem(f"middle_ready{k}") for k in range(NO)]
        split_ready = [sem(f"split_ready{k}") for k in range(NO)]
        stored = [[sem(f"stored{k}_{i}") for i in range(2)] for k in range(NO)]

        turned_stored = [sem(f"turned_stored{i}") for i in range(2)]

        def count(it, u, per=1, c=0):
            return it * (NI * per) + (u * per + c)

        def nothing(it, b, u, first):
            pass

        def loop(eng, early=nothing, late=nothing, last=nothing):
            def body(it, b, start=False, end=False):
                for u in range(NI):
                    more = not (end and u == NI - 1)
                    following = (it, b, u + 1, start and u == 0) if u + 1 < NI else (it + 1, b + STEP, 0, False)
                    if more:
                        early(*following)
                    late(it, b, u, start and u < 2)
                    if more:
                        last(*following)
            early(0, 0, 0, True)
            last(0, 0, 0, True)
            body(0, 0, start=True)
            with eng.Fori(1, B // STEP - 1) as it:
                body(it, it * STEP if STEP > 1 else it)
            body(B // STEP - 1, B - STEP, end=True)

        with nc.Block() as block:
            @block.sync
            def _(sp):
                sp.dma_start(ident[:, :], const["ident_f"]).then_inc(loaded, 16)
                for k, (_, kind, wk, bk, _, _) in enumerate(outs):
                    sp.dma_start(w[:, k, :], wk).then_inc(loaded, 16)
                    sp.dma_start(bias_col[:, k, :], bk.rearrange("(p o) -> p o", o=1)).then_inc(loaded, 16)
                    sp.dma_start(bias_row[:, k, :], bk.rearrange("(o n) -> o n", o=1)).then_inc(loaded, 16)

                def load(it, b, u, first):
                    db, r0, rows = items[u]
                    p = min(128, rows)
                    if not first:
                        if raw_outs:
                            sp.wait_ge(turned_ready["raw"], count(it, u, 1, 1 - NI))
                            stand_alone(sp, passed_sp)
                        if norm_outs:
                            sp.wait_ge(normed_ready, it * TILES + (before[u + 1] - TILES))
                        stand_alone(sp, passed_sp)
                    sp.dma_start(raw[u][0:p, 0:(rows + 127) // 128, :],
                                 ctx_dram[b, r0:r0 + rows, :].rearrange("(c p) n -> p c n", p=p)
                                 ).then_inc(raw_loaded[u], 16)

                def store(it, b, u, first):
                    db, r0, rows = items[u]
                    if turned_dram is not None:
                        sp.wait_ge(turned_copied["raw"], count(it, u, 1, 1))
                        stand_alone(sp, passed_sp)
                        sp.dma_start(turned_dram[bass.ds(b + db, 1), :, r0:r0 + rows].rearrange("o p n -> (o p) n"),
                                     turned["raw"][u % 2][:, 0:rows]).then_inc(turned_stored[u % 2], 16)
                    for k, (_, kind, _, _, _, dest) in sorted(enumerate(outs), key=lambda out: out[1][1] != "rows"):
                        if kind != "rows":
                            sp.wait_ge(split_ready[k], count(it, u, 1, 1))
                            stand_alone(sp, passed_sp)
                        if kind == "split":
                            sp.dma_start(dest[bass.ds(b + db, 1), :, :, r0:r0 + rows]
                                         .rearrange("o (i d) h n -> (o d h) i n", i=PARTS),
                                         parts[k][u % 2][:, :, 0:rows]).then_inc(stored[k][u % 2], 16)
                        elif kind == "split_q":
                            for j in range(PARTS):
                                rj = j * PARTS * D
                                sp.dma_start(dest[bass.ds(b + db, 1), rj:rj + PARTS * D, :, r0:r0 + rows]
                                             .rearrange("o (i d) h n -> (o d h) i n", i=PARTS),
                                             parts[k][u % 2][:, j:j + 1, 0:rows].broadcast_to([128, PARTS, rows])
                                             ).then_inc(stored[k][u % 2], 16)
                        else:
                            p = min(128, rows)
                            sp.wait_ge(value_ready[k], count(it, u, 1, 1))
                            stand_alone(sp, passed_sp)
                            sp.dma_start(dest[bass.ds(b + db, 1), r0:r0 + rows, :].rearrange("o (c p) n -> p (o c) n", p=p),
                                         value[k][u % 2][0:p, 0:(rows + 127) // 128 * C].rearrange("p (c n) -> p c n", n=C)
                                         ).then_inc(stored[k][u % 2], 16)

                def body(it, b, start=False, end=False):
                    for u in range(NI):
                        if ctx_dram is not None:
                            if u == 0:
                                load(it, b, NI - 1, start)
                            elif not end:
                                load(it + 1, b + STEP, u - 1, False)
                        store(it, b, u, start and u < 2)
                if ctx_dram is not None:
                    for u in range(NI - 1):
                        load(0, 0, u, True)
                body(0, 0, start=True)
                with sp.Fori(1, B // STEP - 1) as it:
                    body(it, it * STEP if STEP > 1 else it)
                body(B // STEP - 1, B - STEP, end=True)
                if turned_dram is not None:
                    for i in range(2):
                        sp.wait_ge(turned_stored[i], 16 * (NI // 2) * (B // STEP))
                for k in range(NO):
                    for i in range(2):
                        sp.wait_ge(stored[k][i], 16 * STORES[outs[k][1]] * (NI // 2) * (B // STEP))

            @block.gpsimd
            def _(pool):
                pool.memset(ones[:, :], 1.0).then_inc(set_once, 1)
                pool.memset(eps_col[:, :], eps).then_inc(set_once, 1)
                pool.wait_ge(loaded, 16 * (1 + 3 * NO))
                for k in range(NO):
                    pool.tensor_scalar(bias_scaled[:, k, :], bias_col[:, k, :], outs[k][4], None, ALU.mult
                                       ).then_inc(bias_done, 1)
                pool.wait_ge(bias_done, NO)
                def split(it, b, u, first):
                    n = items[u][2]
                    for k, (_, kind, _, _, _, _) in enumerate(outs):
                        if kind != "rows":
                            pool.wait_ge(middle_ready[k], count(it, u, 1, 1))
                            stand_alone(pool, passed_pool)
                            pool.tensor_tensor(parts[k][u % 2][:, 2, 0:n], remains[k][:, 0:n],
                                               parts[k][u % 2][:, 1, 0:n], ALU.subtract).then_inc(split_ready[k], 1)
                loop(pool, late=split)

            @block.tensor
            def _(pe):
                pe.wait_ge(loaded, 16 * (1 + 3 * NO))
                pe.wait_ge(set_once, 2)

                def turn(s, it, b, u, first):
                    if s in sources:
                        if s == "raw":
                            pe.wait_ge(raw_loaded[u], it * 16 + 16)
                        else:
                            pe.wait_ge(normed_ready, it * TILES + before[u + 1])
                        if not (first and u == 0):
                            pe.wait_ge(turned_copied[s], count(it, u))
                        src = raw[u] if s == "raw" else normed[u % 2]
                        for i, (c0, p) in enumerate(tiles_of[u]):
                            last = pe.transpose(turned_ps[s][:, c0:c0 + p], src[0:p, i, :], ident[0:p, 0:p])
                        last.then_inc(turned_ready[s], 1)

                def project(it, b, u, first):
                    rows = items[u][2]
                    for k, (s, kind, _, _, _, _) in enumerate(outs):
                        pe.wait_ge(turned_copied[s], count(it, u, 1, 1))
                        if not (first and u == 0):
                            if kind != "rows":
                                pe.wait_ge(value_ready[k], count(it, u, 2))
                            else:
                                pe.wait_ge(value_ready[k], count(it, u))
                        if kind != "rows":
                            last = pe.matmul(out_ps[k][:, 0:rows], w[:, k, :], turned[s][u % 2][:, 0:rows],
                                             start=True, stop=True)
                        else:
                            for c0, p in tiles_of[u]:
                                pe.matmul(out_ps[k][0:p, c0:c0 + C], turned[s][u % 2][:, c0:c0 + p], w[:, k, :],
                                          start=True, stop=False)
                                last = pe.matmul(out_ps[k][0:p, c0:c0 + C], ones[:, 0:p], bias_row[:, k, :],
                                                 start=False, stop=True)
                        last.then_inc(out_ready[k], 1)
                loop(pe, early=lambda *item: turn("raw", *item), late=project, last=lambda *item: turn("norm", *item))

            @block.scalar
            def _(act):
                act.wait_ge(set_once, 2)
                act.wait_ge(bias_done, NO)
                def early(it, b, u, first):
                    _, _, rows = items[u]
                    p, nt = min(128, rows), (rows + 127) // 128
                    if norm_outs:
                        act.wait_ge(aggregated, it * TILES + before[u + 1])
                        act.activation(deviation[u % 2][0:p, 0:nt], mean_var[u % 2][0:p, 0:nt, 1], ACT.Sqrt,
                                       bias=eps_col[0:p, :]).then_inc(dev_ready, 1)
                    copy("raw", it, b, u, first)

                def copy(s, it, b, u, first):
                    db, _, rows = items[u]
                    if s in sources:
                        act.wait_ge(turned_ready[s], count(it, u, 1, 1))
                        if not first:
                            for k in range(NO):
                                if outs[k][0] == s:
                                    act.wait_ge(out_ready[k], count(it, u, 1, -1))
                            if s == "raw" and turned_dram is not None:
                                act.wait_ge(turned_stored[u % 2], it * (16 * (NI // 2)) + 16 * (u // 2))
                        if s == "norm" and norm_cols is not None:
                            sc, sh = (columns[:, c, bass.ds(b + db, 1)] if len(columns.shape) == 3 else columns[:, c:c + 1]
                                      for c in norm_cols)
                            stand_alone(act, passed_act)
                            ins = act.activation(turned[s][u % 2][:, 0:rows], turned_ps[s][:, 0:rows], ACT.Identity,
                                                 bias=sh, scale=sc)
                        else:
                            ins = act.activation(turned[s][u % 2][:, 0:rows], turned_ps[s][:, 0:rows], ACT.Copy)
                        ins.then_inc(turned_copied[s], 1)

                def values(it, b, u, first):
                    _, _, rows = items[u]
                    p, nt = min(128, rows), (rows + 127) // 128
                    for k, (s, kind, _, _, scale, _) in enumerate(outs):
                        act.wait_ge(out_ready[k], count(it, u, 1, 1))
                        if kind != "rows":
                            if not first:
                                stores = it * (16 * STORES[kind] * (NI // 2)) + 16 * STORES[kind] * (u // 2)
                                act.wait_ge(stored[k][u % 2], stores)
                            act.activation(parts[k][u % 2][:, 0, 0:rows], out_ps[k][:, 0:rows], ACT.Identity,
                                           bias=bias_scaled[:, k, :], scale=scale).then_inc(value_ready[k], 1)
                            act.activation(value[k][u % 2][:, 0:rows], out_ps[k][:, 0:rows], ACT.Identity,
                                           bias=bias_scaled[:, k, :], scale=scale).then_inc(value_ready[k], 1)
                        else:
                            if not first:
                                act.wait_ge(stored[k][u % 2], it * (16 * (NI // 2)) + 16 * (u // 2))
                            act.activation(value[k][u % 2][0:p, 0:nt * C], out_ps[k][0:p, 0:nt * C], ACT.Copy
                                           ).then_inc(value_ready[k], 1)
                loop(act, early=early, late=values, last=lambda *item: copy("norm", *item))

            @block.vector
            def _(dve):
                def norm(it, b, u, first):
                    db, _, rows = items[u]
                    p, nt = min(128, rows), (rows + 127) // 128
                    if ctx_dram is not None:
                        dve.wait_ge(raw_loaded[u], it * 16 + 16)

                    def src(i):
                        if ctx_dram is not None:
                            return raw[u][0:p, i, :]
                        return X[:, bass.ds((b + db) * QT + i, 1), :].rearrange("p o n -> p (o n)")
                    for i in range(nt):
                        dve.bn_stats(stats[u % 2][0:p, i, :], src(i)).then_inc(stats_ready, 1)
                    for i in range(nt):
                        dve.wait_ge(stats_ready, it * TILES + before[u] + i + 1)
                        stand_alone(dve, passed_dve)
                        dve.bn_aggr(mean_var[u % 2][0:p, i, :], stats[u % 2][0:p, i, :]).then_inc(aggregated, 1)
                    dve.wait_ge(dev_ready, count(it, u, 1, 1))
                    dve.reciprocal(inverse[u % 2][0:p, 0:nt], deviation[u % 2][0:p, 0:nt]).then_inc(inv_ready, 1)
                    dve.wait_ge(inv_ready, count(it, u, 1, 1))
                    if not first:
                        dve.wait_ge(turned_ready["norm"], count(it, u, 1, -1))
                    for i in range(nt):
                        dve.tensor_scalar(normed[u % 2][0:p, i, :], src(i), mean_var[u % 2][0:p, i, 0:1],
                                          inverse[u % 2][0:p, i:i + 1], ALU.subtract, ALU.mult
                                          ).then_inc(normed_ready, 1)

                def remain(it, b, u, first):
                    n = items[u][2]
                    for k, (_, kind, _, _, _, _) in enumerate(outs):
                        if kind != "rows":
                            dve.wait_ge(value_ready[k], count(it, u, 2, 2))
                            if not (first and u == 0):
                                dve.wait_ge(split_ready[k], count(it, u))
                            dve.tensor_tensor(remains[k][:, 0:n], value[k][u % 2][:, 0:n],
                                              parts[k][u % 2][:, 0, 0:n], ALU.subtract).then_inc(remain_ready[k], 1)
                            dve.wait_ge(remain_ready[k], count(it, u, 1, 1))
                            dve.tensor_copy(parts[k][u % 2][:, 1, 0:n], remains[k][:, 0:n]).then_inc(middle_ready[k], 1)
                loop(dve, early=norm if norm_outs else nothing, late=remain)


def attention(nc, tag, X, q_parts, k_parts, v_rows, nk, w_out, out_bias, gate, const, topk=False):
    NCH = (nk + 127) // 128
    full = nk // 128
    size = [min(128, nk - c * 128) for c in range(NCH)]
    cross = nk > T
    UNITS = 2 * NCH
    NCOL = HQ * QT
    tail = 3 * BANK
    if topk:
        fills = [[(n, c0, min(nk, c0 + BANK), c0) for c0 in range(0, nk, BANK)] for n in range(NCOL)]
        SLOT, SLOTS = 4 * BANK, 1
    elif cross:
        fills = [[(n, c0, c0 + BANK, 0)] for n in range(NCOL) for c0 in range(0, tail, BANK)]
        fills += [[(n, tail, nk, (n - n0) * (nk - tail)) for n in range(n0, min(n0 + 3, NCOL))]
                  for n0 in range(0, NCOL, 3)]
        SLOT, SLOTS = BANK, 3
    else:
        fills = [[(h * QT + qt, 0, nk, h * nk) for h in range(HQ)] for qt in range(QT)]
        SLOT, SLOTS = 2 * BANK, 2
    NF = len(fills)
    assert NF % SLOTS == 0
    ST_RING = 3 if cross and not topk else 2
    P_RING = 4
    LOADS = 16 * (PARTS + 1)
    V_LOADS = 16 * (1 if full == NCH else 2)
    NSTEP = 4 + (4 if topk else 1 if cross else 0)

    early, lag, sum_at, turn_at, project_at = PACE["topk" if topk else "cross" if cross else "self"]
    flow = [("fill", i, 1) for i in range(early, NF)] + [("fill", i, 2) for i in range(early)]
    order, done, shift_at = ([("split",)], 0, lag) if early == NF else ([], 0, None)
    for u in range(UNITS + 1):
        upto = u * len(flow) // UNITS if topk else min(len(flow), -(-(u + 1) * len(flow) // UNITS))
        for item in flow[done:upto]:
            order.append(item)
            if item == ("fill", NF - 1, 1):
                order.append(("split",))
                shift_at = min(u + lag, UNITS - 1)
        done = upto
        if u < UNITS:
            order.append(("unit", u))
            for what, at in (("sum", sum_at), ("turn", turn_at), ("project", project_at), ("shift", shift_at)):
                if u == at:
                    order.append((what,))

    with phase(nc, tag) as (sb, ps, sem):
        ks = [sb(f"ks{g}", [128, HQ, nk], BF16) for g in range(QUADS)]
        qs = [sb(f"qs{g}", [128, HQ, T], BF16) for g in range(QUADS)]
        v_nat = sb("v_nat", [128, NCH, C], F32)
        v_pad = [sb(f"v_pad{i}", [128, NCH, HQ, 32], F32) for i in range(2)]
        probs = sb("probs", [128, P_RING, HQ * T], F32)
        below = sb("below", [128, ST_RING, 2 * T], BF16)
        rest = sb("rest", [128, 2, nk if topk else 8], F32)
        top_a = sb("top_a", [128, NCOL, 8], F32)
        top_b = sb("top_b", [128, NCOL, 8], F32)
        stat = sb("stat", [128, 8, NCOL], F32)
        partial = sb("partial", [128, 4, NCOL], F32)
        shift_parts = sb("shift_parts", [128, PARTS, NCOL], BF16)
        shift_rows = sb("shift_rows", [PARTS * NCOL, 128], BF16)
        o_t = sb("o_t", [128, T], F32)
        inv = sb("inv", [128, QT, HQ, 1], F32)
        o_norm = sb("o_norm", [128, QT, C], F32)
        o_norm_t = sb("o_norm_t", [128, T], F32)
        gated = sb("gated", [128, QT, C], F32)
        w_sb = sb("w_sb", [128, C], F32)
        bias_row = sb("bias_row", [1, C], F32)
        ones_row = sb("ones_row", [1, 128], F32)
        ident = sb("ident", [128, 128], BF16)
        neg_ident = sb("neg_ident", [128, 128], BF16)
        ident_f = sb("ident_f", [128, 128], F32)
        exp_bias = sb("exp_bias", [128, 1], F32)

        s_ps = ps("s_ps", [128, SLOTS * SLOT])
        st_ps = ps("st_ps", [128, ST_RING, BANK])
        pv_ps = ps("pv_ps")[:, 0:T]
        misc_ps = ps("misc_ps")
        shift_ps = misc_ps[0:PARTS * NCOL, 0:64].bitcast(BF16)
        turned_ps = misc_ps[:, BANK - T:BANK]
        turned_heads = turned_ps.rearrange("p (q h r) -> p q h r", q=QT, h=HQ)
        y_ps = turned_ps.rearrange("p (q n) -> p q n", q=QT)

        const_ready = sem("const_ready")
        rows_ready = sem("rows_ready")
        cleared = sem("cleared")
        set_once = sem("set_once")
        passed_pool, passed_dve = sem("passed_pool"), sem("passed_dve")
        load_ready = [sem(f"load_ready{g}") for g in range(QUADS)]
        v_ready = sem("v_ready")
        v_full_padded = sem("v_full_padded")
        v_padded = sem("v_padded")
        s_ready = sem("s_ready")
        s_free = sem("s_free")
        dve_step = sem("dve_step")
        top_a_ready, top_b_ready = sem("top_a_ready"), sem("top_b_ready")
        parts_ready = sem("parts_ready")
        shift_t_ready = sem("shift_t_ready")
        shift_copied = sem("shift_copied")
        shift_ready = [sem(f"shift_ready{g}") for g in range(QUADS)]
        st_ready = sem("st_ready")
        below_ready = sem("below_ready")
        masked_ready = sem("masked_ready")
        p_ready = sem("p_ready")
        pv_done = sem("pv_done")
        o_copied = sem("o_copied")
        sums_turned = sem("sums_turned")
        inv_ready = sem("inv_ready")
        out_turned = sem("out_turned")
        out_copied = sem("out_copied")
        norm_ready = sem("norm_ready")
        y_ready = sem("y_ready")
        gated_ready = sem("gated_ready")
        y_used = sem("y_used")

        def count(b, g, per, c=0):
            return b * (QUADS * per) + (g * per + c)

        def ahead(b, g, n):
            return b + (g + n) // QUADS, (g + n) % QUADS

        with nc.Block() as block:

            @block.sync
            def _(sp):
                sp.dma_start(w_sb[:, :], w_out).then_inc(const_ready, 16)
                sp.dma_start(bias_row[:, :], out_bias).then_inc(const_ready, 16)
                sp.dma_start(ident[:, :], const["ident_bf"]).then_inc(const_ready, 16)
                sp.dma_start(neg_ident[:, :], const["neg_ident_bf"]).then_inc(const_ready, 16)
                sp.dma_start(ident_f[:, :], const["ident_f"]).then_inc(const_ready, 16)
                sp.wait_ge(cleared, 2 * QUADS)
                for g in range(QUADS):
                    sp.dma_start(ks[g][ROW_SHIFT:ROW_END, :, :], const["k_rows"]).then_inc(rows_ready, 16)
                    sp.dma_start(qs[g][ROW_MASK:ROW_END, :, :], const["q_rows"]).then_inc(rows_ready, 16)

                def load(b, g):
                    heads = slice(HQ * g, HQ * g + HQ)
                    for j in range(PARTS):
                        sp.dma_start(ks[g][j * PARTS * D:(j + 1) * PARTS * D, :, :], k_parts[b, :, heads, :]
                                     ).then_inc(load_ready[g], 16)
                    sp.dma_start(qs[g][0:ROW_MASK, :, :], q_parts[b, :, heads, :]).then_inc(load_ready[g], 16)

                def load_v(b):
                    sp.dma_start(v_nat[:, 0:full, :],
                                 v_rows[b, 0:full * 128, :].rearrange("(c p) n -> p c n", p=128)).then_inc(v_ready, 16)
                    if full < NCH:
                        sp.dma_start(v_nat[0:size[-1], full, :], v_rows[b, full * 128:nk, :]).then_inc(v_ready, 16)

                def send_shift(b, g):
                    sp.wait_ge(shift_copied, count(b, g, 1, 1))
                    sp.dma_start(qs[g][ROW_SHIFT:ROW_MASK, :, :], shift_rows[:, :]).then_inc(shift_ready[g], 16)

                def reload(b, g):
                    sp.wait_ge(pv_done, count(b - 1, g, NCH, NCH))
                    load(b, g)

                def step(b, g, end=False):
                    nb, ng = ahead(b, g, 1)
                    if not (end and g == QUADS - 1):
                        send_shift(nb, ng)
                    if not end:
                        if g == QUADS - 1:
                            sp.wait_ge(v_padded, b * QUADS + QUADS)
                            load_v(b + 1)
                        reload(b + 1, g)

                load(0, 0)
                load(0, 1)
                load_v(0)
                load(0, 2)
                load(0, 3)
                send_shift(0, 0)
                with sp.Fori(0, B - 1) as b:
                    for g in range(QUADS):
                        step(b, g)
                for g in range(QUADS):
                    step(B - 1, g, end=True)

            @block.gpsimd
            def _(pool):
                for g in range(QUADS):
                    pool.memset(ks[g][:, :, :], 0.0).then_inc(cleared, 1)
                    pool.memset(qs[g][:, :, :], 0.0).then_inc(cleared, 1)
                for i in range(2):
                    pool.memset(v_pad[i][:, :, :, :], 1.0).then_inc(set_once, 1)
                pool.memset(ones_row[:, :], 1.0).then_inc(set_once, 1)
                pool.memset(exp_bias[:, :], EXP_BIAS if topk else 0.0).then_inc(set_once, 1)
                pool.wait_ge(set_once, 4)
                v_heads = v_nat[:, :, :].rearrange("p c (h d) -> p c h d", d=D)

                def pad(b, g, wait=True):
                    if g == 0:
                        pool.wait_ge(v_ready, b * V_LOADS + V_LOADS)
                    if wait:
                        pool.wait_ge(pv_done, count(b, g, NCH, -NCH))
                        stand_alone(pool, passed_pool)
                    for c0, c1, p in [(0, full, 128), (full, NCH, size[-1])]:
                        if c0 < c1:
                            last = pool.tensor_copy(v_pad[g % 2][0:p, c0:c1, :, 0:D],
                                                    v_heads[0:p, c0:c1, HQ * g:HQ * g + HQ, :])
                            if c1 == NCH:
                                last.then_inc(v_padded, 1)
                            else:
                                last.then_inc(v_full_padded, 1)

                for g in range(QUADS):
                    pad(0, g, wait=g >= 2)
                with pool.Fori(1, B) as b:
                    for g in range(QUADS):
                        pad(b, g)

            @block.tensor
            def _(pe):
                pe.wait_ge(const_ready, 5 * 16)
                pe.wait_ge(rows_ready, 2 * QUADS * 16)
                pe.wait_ge(set_once, 4)

                def fill(b, g, i, first=False):
                    if i == 0:
                        pe.wait_ge(load_ready[g], b * LOADS + LOADS)
                    if not (first and i < SLOTS):
                        pe.wait_ge(s_free, count(b, g, NF, i + 1 - SLOTS))
                    for n, c0, c1, at in fills[i]:
                        at += i % SLOTS * SLOT
                        h, qt = n // QT, n % QT
                        last = pe.matmul(s_ps[:, at:at + c1 - c0], qs[g][:, h, qt * 128:qt * 128 + 128],
                                         ks[g][:, h, c0:c1], start=True, stop=True)
                    last.then_inc(s_ready, 1)

                def shift(b, g, lb, lg, start=False):
                    pe.wait_ge(parts_ready, count(b, g, 1, 1))
                    if not start:
                        pe.wait_ge(norm_ready, count(lb, lg, 1))
                        if lg == 0:
                            pe.wait_ge(y_used, lb)
                    pe.transpose(shift_ps, shift_parts[:, :, :].rearrange("p i n -> p (i n)"), ident[:, :]
                                 ).then_inc(shift_t_ready, 1)

                def unit_scores(b, g, u, first=False):
                    c = u // 2
                    if u == 0:
                        pe.wait_ge(shift_ready[g], b * 16 + 16)
                    if u >= ST_RING:
                        pe.wait_ge(p_ready, count(b, g, UNITS, u - ST_RING + 1))
                    elif not first:
                        pe.wait_ge(p_ready, count(b, g, UNITS, -UNITS + 1 + max(
                            v for v in range(UNITS) if v % ST_RING == u % ST_RING)))
                    for i in range(2):
                        h = 2 * (u % 2) + i
                        last = pe.matmul(st_ps[0:size[c], u % ST_RING, i * T:(i + 1) * T],
                                         ks[g][:, h, c * 128:c * 128 + size[c]], qs[g][:, h, :],
                                         start=(i == 0), stop=not topk, skip_group_check=True)
                    last.then_inc(st_ready, 1)

                def unit_mask(b, g, u):
                    pe.wait_ge(below_ready, count(b, g, UNITS, u + 1))
                    n = size[u // 2]
                    pe.matmul(st_ps[0:n, u % ST_RING, :], neg_ident[:, 0:n],
                              below[:, u % ST_RING, :], start=False, stop=True, skip_group_check=True
                              ).then_inc(masked_ready, 1)

                def weigh(b, g, c, first=False):
                    if c == 0:
                        pe.wait_ge(v_padded, count(b, g, 1, 1))
                        if not first:
                            pe.wait_ge(o_copied, count(b, g, 1))
                    pe.wait_ge(p_ready, count(b, g, UNITS, 2 * c + 2))
                    for h in range(HQ):
                        last = pe.matmul(pv_ps[32 * h:32 * h + 32, :], v_pad[g % 2][0:size[c], c, h, :],
                                         probs[0:size[c], c % P_RING, h * T:(h + 1) * T],
                                         start=(c == 0), stop=(c == NCH - 1))
                    last.then_inc(pv_done, 1)

                def turn_sums(b, g, last=False):
                    pe.wait_ge(o_copied, count(b, g, 1, 1))
                    if not last:
                        pe.wait_ge(shift_copied, count(b, g, 1, 2))
                    for qt in range(QT):
                        q = slice(qt * 128, qt * 128 + 128)
                        last_of = pe.transpose(turned_ps[:, q], o_t[:, q], ident_f[:, :])
                    last_of.then_inc(sums_turned, 1)

                def turn_out(b):
                    pe.wait_ge(norm_ready, b * QUADS + QUADS)
                    for qt in range(QT):
                        last = pe.transpose(turned_ps[:, qt * 128:qt * 128 + 128], o_norm[:, qt, :], ident_f[:, :])
                    last.then_inc(out_turned, 1)

                def project(b):
                    pe.wait_ge(out_copied, b + 1)
                    for qt in range(QT):
                        pe.matmul(y_ps[:, qt, :], o_norm_t[:, qt * 128:qt * 128 + 128], w_sb[:, :], start=True, stop=False)
                        last = pe.matmul(y_ps[:, qt, :], ones_row[:, :], bias_row[:, :], start=False, stop=True)
                    last.then_inc(y_ready, 1)

                def step(b, g, start=False, end=False):
                    nb, ng = ahead(b, g, 1)
                    lb, lg = (b, g - 1) if g > 0 else (b - 1, QUADS - 1)
                    first = start and g == 0
                    for what, *n in order:
                        if what == "fill":
                            i, quads = n
                            if not (end and g + quads >= QUADS):
                                fill(*ahead(b, g, quads), i)
                        elif what == "shift":
                            if not (end and g == QUADS - 1):
                                shift(nb, ng, b, g, start=first)
                        elif what == "sum":
                            if not first:
                                turn_sums(lb, lg)
                        elif what == "turn":
                            if g == 0 and not start:
                                turn_out(lb)
                        elif what == "project":
                            if g == 0 and not start:
                                project(lb)
                        elif what == "unit":
                            u = n[0]
                            unit_scores(b, g, u, first=first)
                            if topk and u > 0:
                                unit_mask(b, g, u - 1)
                            if u % 2 and u >= 3:
                                weigh(b, g, (u - 3) // 2, first=first)
                    if topk:
                        unit_mask(b, g, UNITS - 1)
                    weigh(b, g, NCH - 1, first=first)

                for i in range(NF):
                    fill(0, 0, i, first=True)
                for i in range(early):
                    fill(0, 1, i)
                    if i == 0:
                        shift(0, 0, 0, 0, start=True)
                for g in range(QUADS):
                    step(0, g, start=True)
                with pe.Fori(1, B - 1) as b:
                    for g in range(QUADS):
                        step(b, g)
                for g in range(QUADS):
                    step(B - 1, g, end=True)
                turn_sums(B - 1, QUADS - 1, last=True)
                turn_out(B - 1)
                project(B - 1)

            @block.scalar
            def _(act):
                act.wait_ge(set_once, 4)

                def copy_shift(b, g, first=False):
                    act.wait_ge(shift_t_ready, count(b, g, 1, 1))
                    if not first:
                        lb, lg = (b, g - 1) if g > 0 else (b - 1, QUADS - 1)
                        act.wait_ge(shift_ready[lg], lb * 16 + 16)
                    act.activation(shift_rows[:, :], shift_ps, ACT.Copy).then_inc(shift_copied, 1)

                def exp_unit(b, g, u, first=False):
                    c, n = u // 2, size[u // 2]
                    if topk:
                        act.wait_ge(masked_ready, count(b, g, UNITS, u + 1))
                    else:
                        act.wait_ge(st_ready, count(b, g, UNITS, u + 1))
                    if u % 2 == 0:
                        if c >= P_RING:
                            act.wait_ge(pv_done, count(b, g, NCH, c - P_RING + 1))
                        elif not first:
                            act.wait_ge(pv_done, count(b, g, NCH, -NCH + 1 + max(
                                v for v in range(NCH) if v % P_RING == c % P_RING)
                                if NCH > c % P_RING else 0))
                    half = u % 2
                    act.activation(probs[0:n, c % P_RING, half * 2 * T:(half + 1) * 2 * T],
                                   st_ps[0:n, u % ST_RING, :], ACT.Exp, bias=exp_bias[0:n, :]).then_inc(p_ready, 1)

                def copy_sums(b, g, first=False):
                    act.wait_ge(pv_done, count(b, g, NCH, NCH))
                    if not first:
                        act.wait_ge(norm_ready, count(b, g, 1))
                    act.activation(o_t[:, :], pv_ps, ACT.Copy).then_inc(o_copied, 1)

                def step(b, g, start=False, end=False):
                    first = start and g == 0
                    for what, *n in order:
                        if what == "shift" and not (end and g == QUADS - 1):
                            copy_shift(*ahead(b, g, 1))
                        elif what == "unit":
                            u = n[0]
                            if topk:
                                n = size[u // 2]
                                act.wait_ge(st_ready, count(b, g, UNITS, u + 1))
                                act.activation(below[0:n, u % ST_RING, :], st_ps[0:n, u % ST_RING, :], ACT.Relu,
                                               scale=-1e20).then_inc(below_ready, 1)
                                if u > 0:
                                    exp_unit(b, g, u - 1, first)
                            else:
                                exp_unit(b, g, u, first)
                    if topk:
                        exp_unit(b, g, UNITS - 1, first)
                    copy_sums(b, g, first)

                copy_shift(0, 0, first=True)
                for g in range(QUADS):
                    step(0, g, start=True)
                with act.Fori(1, B - 1) as b:
                    for g in range(QUADS):
                        step(b, g)
                for g in range(QUADS):
                    step(B - 1, g, end=True)

            @block.vector
            def _(dve):
                def link(ins, b, g, k):
                    ins.then_inc(dve_step, 1)
                    dve.wait_ge(dve_step, count(b, g, NSTEP, k + 1))

                def second_max(b, g, i):
                    dve.wait_ge(s_free, count(b, g, NF, i + 1))
                    stand_alone(dve, passed_dve)
                    dve.max(top_b[:, i, :], rest[:, i % 2, :]).then_inc(top_b_ready, 1)

                def tile(b, g, i, first=False):
                    dve.wait_ge(s_ready, count(b, g, NF, i + 1))
                    at = i % SLOTS * SLOT
                    if topk:
                        stand_alone(dve, passed_dve)
                        dve.max(top_a[:, i, :], s_ps[:, 0:nk]).then_inc(top_a_ready, 1)
                        dve.wait_ge(top_a_ready, count(b, g, NF, i + 1))
                        stand_alone(dve, passed_dve)
                        if not (first and i < 2):
                            dve.wait_ge(top_b_ready, count(b, g, NF, i - 1))
                            stand_alone(dve, passed_dve)
                        dve.match_replace(rest[:, i % 2, :], top_a[:, i, :], s_ps[:, 0:nk], -3e38).then_inc(s_free, 1)
                        if i > 0:
                            second_max(b, g, i - 1)
                        return
                    if cross:
                        n, c0, c1, _ = fills[i][0]
                        k, width = len(fills[i]), c1 - c0
                        out = partial[:, min(c0 // BANK, PARTS), n:n + k]
                    else:
                        k, width = HQ, nk
                        out = stat[:, 0, i:NCOL:QT]
                    dve.tensor_reduce(out, s_ps[:, at:at + k * width].rearrange("p (k n) -> p k n", k=k),
                                      AX.X, ALU.max, negate=True).then_inc(s_free, 1)

                def split_shift(b, g, first=False):
                    k = 0
                    if topk:
                        second_max(b, g, NF - 1)
                        dve.wait_ge(top_b_ready, count(b, g, NF, NF))
                        biggest, least = top_a[:, :, 0], top_b[:, :, 7]
                        link(dve.tensor_scalar(stat[:, 1, :], biggest, -1.0, EXP_SPAN, ALU.mult, ALU.add), b, g, k)
                        link(dve.scalar_tensor_tensor(stat[:, 2, :], least, -1.0, biggest, ALU.mult, ALU.max), b, g, k + 1)
                        link(dve.scalar_tensor_tensor(stat[:, 3, :], stat[:, 2, :], TIE_MARGIN, least,
                                                      ALU.mult, ALU.subtract), b, g, k + 2)
                        ins = dve.tensor_tensor(stat[:, 0, :], stat[:, 1, :], stat[:, 3, :], ALU.min)
                        k += 3
                        link(ins, b, g, k)
                        k += 1
                    else:
                        dve.wait_ge(s_free, count(b, g, NF, NF))
                        if cross:
                            link(dve.tensor_reduce(stat[:, 0, :], partial[:, :, :].rearrange("p k n -> p n k"),
                                                   AX.X, ALU.min), b, g, k)
                            k += 1
                    if not first:
                        dve.wait_ge(shift_t_ready, count(b, g, 1))
                    link(dve.tensor_copy(shift_parts[:, 0, :], stat[:, 0, :]), b, g, k)
                    link(dve.tensor_tensor(stat[:, 4, :], stat[:, 0, :], shift_parts[:, 0, :], ALU.subtract), b, g, k + 1)
                    link(dve.tensor_copy(shift_parts[:, 1, :], stat[:, 4, :]), b, g, k + 2)
                    link(dve.tensor_tensor(stat[:, 5, :], stat[:, 4, :], shift_parts[:, 1, :], ALU.subtract), b, g, k + 3)
                    dve.tensor_copy(shift_parts[:, 2, :], stat[:, 5, :]).then_inc(parts_ready, 1)

                def normalise(b, g):
                    dve.wait_ge(sums_turned, count(b, g, 1, 1))
                    dve.reciprocal(inv[:, :, :, :], turned_heads[:, :, :, D:D + 1]).then_inc(inv_ready, 1)
                    dve.wait_ge(inv_ready, count(b, g, 1, 1))
                    dve.tensor_tensor(o_norm[:, :, g * HQ * D:(g + 1) * HQ * D].rearrange("p q (h d) -> p q h d", d=D),
                                      turned_heads[:, :, :, 0:D], inv[:, :, :, :].broadcast_to([128, QT, HQ, D]), ALU.mult
                                      ).then_inc(norm_ready, 1)

                def copy_out(b):
                    dve.wait_ge(out_turned, b + 1)
                    dve.tensor_copy(o_norm_t[:, :], turned_ps).then_inc(out_copied, 1)

                def add_to_x(b):
                    dve.wait_ge(y_ready, b + 1)
                    x = X[:, bass.ds(b * QT, QT), :]
                    if gate is None:
                        dve.tensor_tensor(x, x, y_ps, ALU.add).then_inc(y_used, 1)
                    else:
                        for qt in range(QT):
                            dve.tensor_tensor(gated[:, qt, :], y_ps[:, qt, :], gate[:, bass.ds(b * C, C)], ALU.mult
                                              ).then_inc(gated_ready, 1)
                        dve.wait_ge(gated_ready, b * QT + QT)
                        dve.tensor_tensor(x, x, gated[:, :, :], ALU.add).then_inc(y_used, 1)

                def step(b, g, start=False, end=False):
                    nb, ng = ahead(b, g, 1)
                    lb, lg = (b, g - 1) if g > 0 else (b - 1, QUADS - 1)
                    for what, *n in order:
                        if what == "sum":
                            if not (start and g == 0):
                                normalise(lb, lg)
                        elif what == "turn":
                            if g == 0 and not start:
                                copy_out(lb)
                        elif what == "project":
                            if g == 0 and not start:
                                add_to_x(lb)
                        elif what == "fill":
                            i, quads = n
                            if not (end and g + quads >= QUADS):
                                tile(*ahead(b, g, quads), i)
                        elif what == "split" and not (end and g == QUADS - 1):
                            split_shift(nb, ng)

                for i in range(NF):
                    tile(0, 0, i, first=True)
                split_shift(0, 0, first=True)
                for i in range(early):
                    tile(0, 1, i)
                for g in range(QUADS):
                    step(0, g, start=True)
                with dve.Fori(1, B - 1) as b:
                    for g in range(QUADS):
                        step(b, g)
                for g in range(QUADS):
                    step(B - 1, g, end=True)
                normalise(B - 1, QUADS - 1)
                copy_out(B - 1)
                add_to_x(B - 1)
def row_stats(nc, tag, X, negative_mean, inverse, eps):
    with phase(nc, tag) as (sb, ps, sem):
        stats = sb("stats", [128, NTILE, 6])
        mean_var = sb("mean_var", [128, NTILE, 2])
        deviation = sb("deviation", [128, NTILE])
        eps_col = sb("eps_col", [128, 1])
        eps_ready, stats_ready, aggregated, dev_ready, done = (
            sem("eps_ready"), sem("stats_ready"), sem("aggregated"), sem("dev_ready"), sem("done"))
        with nc.Block() as block:
            @block.vector
            def _(dve):
                dve.memset(eps_col[:, :], eps).then_inc(eps_ready, 1)
                for i in range(NTILE):
                    dve.bn_stats(stats[:, i, :], X[:, i, :]).then_inc(stats_ready, 1)
                for i in range(NTILE):
                    dve.wait_ge(stats_ready, i + 1)
                    dve.bn_aggr(mean_var[:, i, :], stats[:, i, :]).then_inc(aggregated, 1)
                dve.wait_ge(aggregated, NTILE)
                dve.tensor_scalar(negative_mean[:, :], mean_var[:, :, 0], -1.0, None, ALU.mult).then_inc(done, 1)
                dve.wait_ge(dev_ready, 1)
                dve.reciprocal(inverse[:, :], deviation[:, :]).then_inc(done, 1)

            @block.scalar
            def _(act):
                act.wait_ge(eps_ready, 1)
                act.wait_ge(aggregated, NTILE)
                act.activation(deviation[:, :], mean_var[:, :, 1], ACT.Sqrt, bias=eps_col[:, :]).then_inc(dev_ready, 1)


def evidence(nc, tag, X, negative_mean, inverse, cond_sb, probs_out, p, ctx, ctx_turned, nx_dram, ev_dram, const):
    NCH = (LC + 127) // 128
    FULL = LC // 128
    size = [min(128, LC - c * 128) for c in range(NCH)]
    E = 3
    GROUPS = [list(range(c, min(c + 4, NCH))) for c in range(0, NCH, 4)]
    NG = len(GROUPS)
    with phase(nc, tag) as (sb, ps, sem):
        wq, wk_t, wv = sb("wq", [128, C]), sb("wk_t", [128, C]), sb("wv", [128, C])
        router = sb("router", [128, 3, E])
        router_bias = sb("router_bias", [1, E])
        gamma, beta = sb("gamma", [128, 1]), sb("beta", [128, 1])
        ident = sb("ident", [128, 128])
        ones = sb("ones", [1, 128])
        rows = [sb(f"rows{i}", [128, NCH, C]) for i in range(2)]
        turned = [sb(f"turned{i}", [128, LC]) for i in range(2)]
        normed = [sb(f"normed{i}", [128, QT, C]) for i in range(2)]
        anchor = [sb(f"anchor{i}", [128, 128]) for i in range(2)]
        nx = [sb(f"nx{i}", [128, T]) for i in range(2)]
        q1 = [sb(f"q1_{i}", [128, T]) for i in range(2)]
        q2 = [sb(f"q2_{i}", [128, T]) for i in range(2)]
        weights = [sb(f"weights{i}", [128, LC]) for i in range(2)]
        w_turned = [sb(f"w_turned{i}", [128, NCH, 128]) for i in range(2)]
        top = sb("top", [128, 2])
        sums = sb("sums", [128, 2])
        inv_sums = sb("inv_sums", [128, 2])
        mixed = [sb(f"mixed{i}", [128, QT, C]) for i in range(2)]
        mixed_t = [sb(f"mixed_t{i}", [128, T]) for i in range(2)]
        ev = [sb(f"ev{i}", [128, T]) for i in range(2)]
        logits_top = sb("logits_top", [128, QT])
        exps = sb("exps", [128, QT, E])
        exp_sums = sb("exp_sums", [128, QT])
        exp_inv = sb("exp_inv", [128, QT])

        s_ps = ps("s_ps", [128, 4 * BANK])
        turn_ps = [ps(f"turn_ps{i}") for i in range(2)]
        small_ps, mix_ps = ps("small_ps"), ps("mix_ps")

        loaded, set_once = sem("loaded"), sem("set_once")
        ctx_loaded = [sem(f"ctx_loaded{i}") for i in range(2)]
        normed_ready, anchor_ready, nx_turned, nx_ready = (
            sem("normed_ready"), sem("anchor_ready"), sem("nx_turned"), sem("nx_ready"))
        q1_made, q1_ready, q2_made, q2_ready = sem("q1_made"), sem("q1_ready"), sem("q2_made"), sem("q2_ready")
        s_ready, top_ready, w_ready, inv_ready = sem("s_ready"), sem("top_ready"), sem("w_ready"), sem("inv_ready")
        w_turn_ready, w_turn_copied = sem("w_turn_ready"), sem("w_turn_copied")
        mix_ready, mixed_ready, mixed_turned, mixed_copied = (
            sem("mix_ready"), sem("mixed_ready"), sem("mixed_turned"), sem("mixed_copied"))
        ev_made, ev_ready, logits_made, logits_max, exps_ready, exps_inv, probs_done = (
            sem("ev_made"), sem("ev_ready"), sem("logits_made"), sem("logits_max"), sem("exps_ready"),
            sem("exps_inv"), sem("probs_done"))
        stored = [sem(f"stored{i}") for i in range(2)]
        passed_sp, passed_dve = sem("passed_sp"), sem("passed_dve")

        def count(it, u, per=1, c=0):
            return it * (2 * per) + (u * per + c)

        def loop(eng, begin, body, finish):
            def pair(it, b, start=False, end=False):
                zero, one = (it, b, 0, start), (it, b, 1, start)
                before = None if start else (it - 1, b - 2, 1, False)
                body(zero, one, before)
                body(one, None if end else (it + 1, b + 2, 0, False), zero)
            begin(0, 0, 0, True)
            pair(0, 0, start=True)
            with eng.Fori(1, B // 2 - 1) as it:
                pair(it, it * 2)
            pair(B // 2 - 1, B - 2, end=True)
            finish(B // 2 - 1, B - 2, 1, False)

        with nc.Block() as block:
            @block.sync
            def _(sp):
                for dst, src in [(wq[:, :], p["Wq"]), (wk_t[:, :], p["Wk_t"]), (wv[:, :], p["Wv"]),
                                 (router[:, :, :], p["router_W"].rearrange("(k p) e -> p k e", p=128)),
                                 (router_bias[:, :], p["router_b"].rearrange("(o n) -> o n", o=1)),
                                 (gamma[:, :], p["ln_gamma"].rearrange("(p o) -> p o", o=1)),
                                 (beta[:, :], p["ln_beta"].rearrange("(p o) -> p o", o=1)),
                                 (ident[:, :], const["ident_f"])]:
                    sp.dma_start(dst, src).then_inc(loaded, 16)

                def load(b, u):
                    one = bass.ds(b + u, 1)
                    sp.dma_start(rows[u][:, 0:FULL, :],
                                 ctx[one, 0:FULL * 128, :].rearrange("o (c p) n -> p (o c) n", p=128)
                                 ).then_inc(ctx_loaded[u], 16)
                    sp.dma_start(rows[u][0:size[-1], FULL, :],
                                 ctx[one, FULL * 128:LC, :].rearrange("o p n -> (o p) n")).then_inc(ctx_loaded[u], 16)
                    sp.dma_start(turned[u][:, :], ctx_turned[one, :, :].rearrange("o p n -> (o p) n")
                                 ).then_inc(ctx_loaded[u], 16)

                def store(it, b, u):
                    one = bass.ds(b + u, 1)
                    sp.wait_ge(ev_ready, count(it, u, 1, 1))
                    stand_alone(sp, passed_sp)
                    sp.dma_start(nx_dram[one, :, :].rearrange("o p n -> (o p) n"), nx[u][:, :]).then_inc(stored[u], 16)
                    sp.dma_start(ev_dram[one, :, :].rearrange("o p n -> (o p) n"), ev[u][:, :]).then_inc(stored[u], 16)
                load(0, 0)
                load(0, 1)
                with sp.Fori(0, B // 2 - 1) as it:
                    for u in range(2):
                        sp.wait_ge(mix_ready, count(it, u, QT, QT))
                        stand_alone(sp, passed_sp)
                        load(it * 2 + 2, u)
                        store(it, it * 2, u)
                for u in range(2):
                    store(B // 2 - 1, B - 2, u)
                for u in range(2):
                    sp.wait_ge(stored[u], 32 * (B // 2))

            @block.tensor
            def _(pe):
                pe.wait_ge(loaded, 8 * 16)
                pe.wait_ge(set_once, 1)

                def turn_rows(it, u, first):
                    pe.wait_ge(normed_ready, count(it, u, 1, 1))
                    if not first:
                        pe.wait_ge(exps_ready, count(it, u, QT, -QT))
                    for qt in range(QT):
                        last = pe.transpose(small_ps[:, qt * 128:qt * 128 + 128], normed[u][:, qt, :], ident[:, :])
                    last.then_inc(nx_turned, 1)

                def query1(it, u):
                    pe.wait_ge(nx_ready, count(it, u, 1, 1))
                    pe.matmul(small_ps[:, 0:T], wq[:, :], nx[u][:, :], start=True, stop=True).then_inc(q1_made, 1)

                def query2(it, u):
                    pe.wait_ge(q1_ready, count(it, u, 1, 1))
                    pe.matmul(small_ps[:, 0:T], wk_t[:, :], q1[u][:, :], start=True, stop=True).then_inc(q2_made, 1)

                def scores(it, u, qt, first):
                    if qt == 0:
                        pe.wait_ge(q2_ready, count(it, u, 1, 1))
                        pe.wait_ge(ctx_loaded[u], it * 48 + 48)
                    if not (first and u == 0 and qt == 0):
                        pe.wait_ge(w_ready, count(it, u, QT, qt))
                    for c0 in range(0, LC, BANK):
                        c1 = min(LC, c0 + BANK)
                        last = pe.matmul(s_ps[:, c0:c1], q2[u][:, qt * 128:qt * 128 + 128], turned[u][:, c0:c1],
                                         start=True, stop=True)
                    last.then_inc(s_ready, 1)

                def mix(it, u, qt, first):
                    pe.wait_ge(w_ready, count(it, u, QT, qt + 1))
                    for n, group in enumerate(GROUPS):
                        if not (first and u == 0 and qt == 0 and n < 2):
                            pe.wait_ge(w_turn_copied, it * (2 * QT * NG) + (u * QT + qt) * NG + n - 1)
                        for i, c in enumerate(group):
                            last = pe.transpose(turn_ps[n % 2][0:size[c], i * 128:i * 128 + 128],
                                                weights[qt][:, c * 128:c * 128 + size[c]], ident[:, :])
                        last.then_inc(w_turn_ready, 1)
                    if not (first and u == 0 and qt == 0):
                        pe.wait_ge(mixed_ready, count(it, u, QT, qt))
                    for n, group in enumerate(GROUPS):
                        pe.wait_ge(w_turn_copied, it * (2 * QT * NG) + (u * QT + qt) * NG + n + 1)
                        for c in group:
                            last = pe.matmul(mix_ps[:, 0:C], w_turned[qt][0:size[c], c, :], rows[u][0:size[c], c, :],
                                             start=(c == 0), stop=(c == NCH - 1))
                    last.then_inc(mix_ready, 1)

                def finish(it, u):
                    pe.wait_ge(mixed_ready, count(it, u, QT, QT))
                    for qt in range(QT):
                        last = pe.transpose(small_ps[:, qt * 128:qt * 128 + 128], mixed[u][:, qt, :], ident[:, :])
                    last.then_inc(mixed_turned, 1)
                    pe.wait_ge(mixed_copied, count(it, u, 1, 1))
                    pe.matmul(small_ps[:, 0:T], wv[:, :], mixed_t[u][:, :], start=True, stop=True).then_inc(ev_made, 1)
                    pe.wait_ge(ev_ready, count(it, u, 1, 1))
                    pe.wait_ge(anchor_ready, count(it, u, 1, 1))
                    for qt in range(QT):
                        out = small_ps[:, qt * E:qt * E + E]
                        q = slice(qt * 128, qt * 128 + 128)
                        pe.matmul(out, nx[u][:, q], router[:, 0, :], start=True, stop=False)
                        pe.matmul(out, ev[u][:, q], router[:, 1, :], start=False, stop=False)
                        pe.matmul(out, anchor[u][:, :], router[:, 2, :], start=False, stop=False)
                        last = pe.matmul(out, ones[:, :], router_bias[:, :], start=False, stop=True)
                    last.then_inc(logits_made, 1)

                def begin(it, b, u, first):
                    turn_rows(it, u, first)
                    query1(it, u)
                    query2(it, u)

                def end(it, b, u, first):
                    finish(it, u)

                def body(item, following, before):
                    it, b, u, first = item
                    scores(it, u, 0, first)
                    if before:
                        end(*before)
                    scores(it, u, 1, first)
                    mix(it, u, 0, first)
                    if following:
                        begin(*following)
                    mix(it, u, 1, first)
                loop(pe, begin, body, end)

            @block.scalar
            def _(act):
                act.wait_ge(loaded, 8 * 16)

                def begin(it, b, u, first):
                    act.wait_ge(nx_turned, count(it, u, 1, 1))
                    if not first:
                        act.wait_ge(stored[u], it * 32)
                    act.activation(nx[u][:, :], small_ps[:, 0:T], ACT.Identity, bias=beta[:, :], scale=gamma[:, :]
                                   ).then_inc(nx_ready, 1)
                    act.wait_ge(q1_made, count(it, u, 1, 1))
                    act.activation(q1[u][:, :], small_ps[:, 0:T], ACT.Copy, scale=float(C) ** -0.5).then_inc(q1_ready, 1)
                    act.wait_ge(q2_made, count(it, u, 1, 1))
                    act.activation(q2[u][:, :], small_ps[:, 0:T], ACT.Copy).then_inc(q2_ready, 1)

                def weigh(it, u, qt, first):
                    act.wait_ge(top_ready, count(it, u, QT, qt + 1))
                    if not (first and u == 0):
                        act.wait_ge(w_turn_ready, it * (2 * QT * NG) + (u * QT + qt) * NG - (QT - 1) * NG)
                        act.wait_ge(inv_ready, count(it, u, QT, qt - 1))
                    act.activation(weights[qt][:, :], s_ps[:, 0:LC], ACT.Exp, bias=top[:, qt:qt + 1],
                                   accum_out=sums[:, qt:qt + 1]).then_inc(w_ready, 1)

                def normalise(it, u, qt):
                    act.wait_ge(mix_ready, count(it, u, QT, qt + 1))
                    act.wait_ge(inv_ready, count(it, u, QT, qt + 1))
                    act.activation(mixed[u][:, qt, :], mix_ps[:, 0:C], ACT.Copy, scale=inv_sums[:, qt:qt + 1]
                                   ).then_inc(mixed_ready, 1)

                def finish(it, b, u, first):
                    act.wait_ge(mixed_turned, count(it, u, 1, 1))
                    act.activation(mixed_t[u][:, :], small_ps[:, 0:T], ACT.Copy).then_inc(mixed_copied, 1)
                    act.wait_ge(ev_made, count(it, u, 1, 1))
                    act.activation(ev[u][:, :], small_ps[:, 0:T], ACT.Copy).then_inc(ev_ready, 1)
                    for qt in range(QT):
                        act.wait_ge(logits_max, count(it, u, QT, QT))
                        if not (first and u == 0):
                            act.wait_ge(probs_done, count(it, u))
                        act.activation(exps[:, qt, :], small_ps[:, qt * E:qt * E + E], ACT.Exp,
                                       bias=logits_top[:, qt:qt + 1], accum_out=exp_sums[:, qt:qt + 1]
                                       ).then_inc(exps_ready, 1)

                def body(item, following, before):
                    it, b, u, first = item
                    weigh(it, u, 0, first)
                    if before:
                        finish(*before)
                    weigh(it, u, 1, first)
                    normalise(it, u, 0)
                    if following:
                        begin(*following)
                    normalise(it, u, 1)
                loop(act, begin, body, finish)

            @block.vector
            def _(dve):
                dve.memset(ones[:, :], 1.0).then_inc(set_once, 1)

                def norm(it, b, u, first):
                    if not first:
                        dve.wait_ge(nx_turned, count(it, u, 1, -1))
                        dve.wait_ge(logits_made, count(it, u, 1, -1))
                        stand_alone(dve, passed_dve)
                    dve.tensor_copy(anchor[u][:, :], cond_sb[:, bass.ds(b + u, 1)].broadcast_to([128, 128])
                                    ).then_inc(anchor_ready, 1)
                    tile = (b + u) * QT
                    for qt in range(QT):
                        ins = dve.tensor_scalar(normed[u][:, qt, :], X[:, bass.ds(tile + qt, 1), :].rearrange("p o n -> p (o n)"),
                                                negative_mean[:, bass.ds(tile + qt, 1)], inverse[:, bass.ds(tile + qt, 1)],
                                                ALU.add, ALU.mult)
                    ins.then_inc(normed_ready, 1)

                def top_score(it, u, qt):
                    dve.wait_ge(s_ready, count(it, u, QT, qt + 1))
                    dve.tensor_reduce(top[:, qt:qt + 1], s_ps[:, 0:LC], AX.X, ALU.max, negate=True
                                      ).then_inc(top_ready, 1)

                def copy_weights(it, u, qt, first):
                    dve.wait_ge(w_ready, count(it, u, QT, qt + 1))
                    if not (first and u == 0):
                        dve.wait_ge(mixed_ready, count(it, u, QT, qt - 1))
                    dve.reciprocal(inv_sums[:, qt:qt + 1], sums[:, qt:qt + 1]).then_inc(inv_ready, 1)
                    for n, group in enumerate(GROUPS):
                        dve.wait_ge(w_turn_ready, it * (2 * QT * NG) + (u * QT + qt) * NG + n + 1)
                        p_, k = size[group[-1]], len(group)
                        dve.tensor_copy(w_turned[qt][0:p_, group[0]:group[0] + k, :],
                                        turn_ps[n % 2][0:p_, 0:k * 128].rearrange("p (c n) -> p c n", n=128)
                                        ).then_inc(w_turn_copied, 1)

                def route(it, b, u, first):
                    dve.wait_ge(logits_made, count(it, u, 1, 1))
                    for qt in range(QT):
                        dve.tensor_reduce(logits_top[:, qt:qt + 1], small_ps[:, qt * E:qt * E + E], AX.X, ALU.max,
                                          negate=True).then_inc(logits_max, 1)
                    dve.wait_ge(exps_ready, count(it, u, QT, QT))
                    dve.reciprocal(exp_inv[:, :], exp_sums[:, :]).then_inc(exps_inv, 1)
                    dve.wait_ge(exps_inv, count(it, u, 1, 1))
                    stand_alone(dve, passed_dve)
                    for qt in range(QT):
                        ins = dve.tensor_scalar(probs_out[:, bass.ds((b + u) * QT + qt, 1), :].rearrange("p o e -> p (o e)"),
                                                exps[:, qt, :], exp_inv[:, qt:qt + 1], None, ALU.mult)
                    ins.then_inc(probs_done, 1)

                def body(item, following, before):
                    it, b, u, first = item
                    top_score(it, u, 0)
                    if before:
                        route(*before)
                    top_score(it, u, 1)
                    copy_weights(it, u, 0, first)
                    if following:
                        norm(*following)
                    copy_weights(it, u, 1, first)
                loop(dve, norm, body, route)


def experts(nc, tag, X, probs, columns, cols, p, nx_dram, ev_dram, const):
    E, RB = 3, 2
    NB = E * RB + 1
    with phase(nc, tag) as (sb, ps, sem):
        w1 = sb("w1", [128, NB, 2, 128])
        w2 = sb("w2", [128, E * RB, C])
        b2 = sb("b2", [1, E, C])
        gate_w2, out_w = sb("gate_w2", [128, C]), sb("out_w", [128, C])
        gate_b2, out_b = sb("gate_b2", [1, C]), sb("out_b", [1, C])
        ones, ident = sb("ones", [1, 128]), sb("ident", [128, 128])
        nx = [sb(f"nx{i}", [128, T]) for i in range(2)]
        ev = [sb(f"ev{i}", [128, T]) for i in range(2)]
        hidden = [sb(f"hidden{i}", [128, NB, T]) for i in range(2)]
        tanh = [sb(f"tanh{i}", [128, QT, C]) for i in range(2)]
        routed = sb("routed", [128, QT, C])
        routed_t = sb("routed_t", [128, T])
        product = sb("product", [128, QT, C])
        hidden_ps = [ps(f"hidden_ps{i}") for i in range(2)]
        y_ps = [ps(f"y_ps{i}") for i in range(QT)]
        gate_ps, turned_ps, out_ps = ps("gate_ps"), ps("turned_ps"), ps("out_ps")

        loaded, set_once = sem("loaded"), sem("set_once")
        in_loaded = [sem(f"in_loaded{i}") for i in range(2)]
        hidden_made, hidden_ready, y_made, y_taken = sem("hidden_made"), sem("hidden_ready"), sem("y_made"), sem("y_taken")
        gate_made, tanh_ready, routed_step = sem("gate_made"), sem("tanh_ready"), sem("routed_step")
        turned_made, turned_ready, out_made, product_ready, x_done = (
            sem("turned_made"), sem("turned_ready"), sem("out_made"), sem("product_ready"), sem("x_done"))
        passed_sp, passed_act, passed_dve = sem("passed_sp"), sem("passed_act"), sem("passed_dve")
        NLOAD = 5 + E * (1 + 2 * RB) + 1

        def count(it, u, per=1, c=0):
            return it * (2 * per) + (u * per + c)

        def loop(eng, body):
            body(0, 0, 0, True)
            body(0, 0, 1, True)
            with eng.Fori(1, B // 2) as it:
                body(it, it * 2, 0, False)
                body(it, it * 2, 1, False)

        with nc.Block() as block:
            @block.sync
            def _(sp):
                row = lambda a: a.rearrange("(o n) -> o n", o=1)
                weights = [(gate_w2[:, :], p["gate_w2"]), (out_w[:, :], p["out_w"]), (gate_b2[:, :], row(p["gate_b2"])),
                           (out_b[:, :], row(p["out_b"])), (ident[:, :], const["ident_f"])]
                for e in range(E):
                    weights.append((b2[:, e, :], p["e_b2"][e:e + 1, :]))
                    for r in range(RB):
                        k = e * RB + r
                        weights.append((w2[:, k, :], p["e_w2"][e, r * 128:r * 128 + 128, :]))
                        weights.append((w1[:, k, :, :], p["e_w1"][e, 0:2 * C, r * 128:r * 128 + 128]
                                        .rearrange("(s c) n -> c s n", s=2)))
                weights.append((w1[:, NB - 1, :, :], p["gate_w1"][0:2 * C, :].rearrange("(s c) n -> c s n", s=2)))
                for dst, src in weights:
                    sp.dma_start(dst, src).then_inc(loaded, 16)
                assert len(weights) == NLOAD

                def body(it, b, u, first):
                    if not first:
                        sp.wait_ge(hidden_made, count(it, u, NB, -NB))
                        stand_alone(sp, passed_sp)
                    one = bass.ds(b + u, 1)
                    sp.dma_start(nx[u][:, :], nx_dram[one, :, :].rearrange("o p n -> (o p) n")).then_inc(in_loaded[u], 16)
                    sp.dma_start(ev[u][:, :], ev_dram[one, :, :].rearrange("o p n -> (o p) n")).then_inc(in_loaded[u], 16)
                loop(sp, body)

            @block.tensor
            def _(pe):
                pe.wait_ge(loaded, 16 * NLOAD)
                pe.wait_ge(set_once, 1)

                def first_part(it, b, u, first):
                    pe.wait_ge(in_loaded[u], it * 32 + 32)
                    for k in range(NB):
                        if not (first and u == 0 and k < 2):
                            pe.wait_ge(hidden_ready, count(it, u, NB, k - 1))
                        pe.matmul(hidden_ps[k % 2][:, 0:T], w1[:, k, 0, :], nx[u][:, :], start=True, stop=False)
                        pe.matmul(hidden_ps[k % 2][:, 0:T], w1[:, k, 1, :], ev[u][:, :], start=False, stop=True
                                  ).then_inc(hidden_made, 1)

                def second_part(it, b, u, first):
                    for qt in range(QT):
                        q = slice(qt * 128, qt * 128 + 128)
                        if qt == 0:
                            pe.wait_ge(hidden_ready, count(it, u, NB, NB))
                        if not (first and u == 0):
                            pe.wait_ge(y_taken, count(it, u, QT, qt - 1))
                        for e in range(E):
                            out = y_ps[qt][:, e * C:e * C + C]
                            for r in range(RB):
                                pe.matmul(out, hidden[u][:, e * RB + r, q], w2[:, e * RB + r, :], start=(r == 0), stop=False)
                            last = pe.matmul(out, ones[:, :], b2[:, e, :], start=False, stop=True)
                        last.then_inc(y_made, 1)
                    if not (first and u == 0):
                        pe.wait_ge(tanh_ready, count(it, u))
                    for qt in range(QT):
                        out = gate_ps[:, qt * C:qt * C + C]
                        pe.matmul(out, hidden[u][:, NB - 1, qt * 128:qt * 128 + 128], gate_w2[:, :], start=True, stop=False)
                        last = pe.matmul(out, ones[:, :], gate_b2[:, :], start=False, stop=True)
                    last.then_inc(gate_made, 1)

                def third_part(it, b, u, first):
                    pe.wait_ge(routed_step, count(it, u, QT * E, QT * E))
                    if not (first and u == 0):
                        pe.wait_ge(turned_ready, count(it, u))
                    for qt in range(QT):
                        last = pe.transpose(turned_ps[:, qt * 128:qt * 128 + 128], routed[:, qt, :], ident[:, :])
                    last.then_inc(turned_made, 1)
                    pe.wait_ge(turned_ready, count(it, u, 1, 1))
                    if not (first and u == 0):
                        pe.wait_ge(product_ready, count(it, u))
                    for qt in range(QT):
                        out = out_ps[:, qt * C:qt * C + C]
                        pe.matmul(out, routed_t[:, qt * 128:qt * 128 + 128], out_w[:, :], start=True, stop=False)
                        last = pe.matmul(out, ones[:, :], out_b[:, :], start=False, stop=True)
                    last.then_inc(out_made, 1)

                def body(it, b, u, first):
                    first_part(it, b, u, first)
                    second_part(it, b, u, first)
                    third_part(it, b, u, first)
                loop(pe, body)

            @block.scalar
            def _(act):
                def body(it, b, u, first):
                    for k in range(NB):
                        act.wait_ge(hidden_made, count(it, u, NB, k + 1))
                        if not first and k == 0:
                            act.wait_ge(gate_made, count(it, u, 1, -1))
                        if k == 0:
                            stand_alone(act, passed_act)
                        act.activation(hidden[u][:, k, :], hidden_ps[k % 2][:, 0:T], ACT.Silu,
                                       bias=columns[:, cols + k, bass.ds(b + u, 1)]).then_inc(hidden_ready, 1)
                    act.wait_ge(gate_made, count(it, u, 1, 1))
                    if not first:
                        act.wait_ge(product_ready, count(it, u, 1, -1))
                    act.activation(tanh[u][:, :, :], gate_ps[:, 0:QT * C].rearrange("p (q n) -> p q n", q=QT), ACT.Tanh,
                                   scale=0.5).then_inc(tanh_ready, 1)
                    act.wait_ge(turned_made, count(it, u, 1, 1))
                    act.activation(routed_t[:, :], turned_ps[:, 0:T], ACT.Copy).then_inc(turned_ready, 1)
                loop(act, body)

            @block.vector
            def _(dve):
                dve.memset(ones[:, :], 1.0).then_inc(set_once, 1)

                def body(it, b, u, first):
                    tile = (b + u) * QT
                    for qt in range(QT):
                        dve.wait_ge(y_made, count(it, u, QT, qt + 1))
                        if qt == 0 and not (first and u == 0):
                            dve.wait_ge(turned_made, count(it, u))
                        stand_alone(dve, passed_dve)
                        for e in range(E):
                            y = y_ps[qt][:, e * C:e * C + C]
                            pr = probs[:, bass.ds(tile + qt, 1), e]
                            if e == 0:
                                ins = dve.tensor_scalar(routed[:, qt, :], y, pr, None, ALU.mult)
                            else:
                                ins = dve.scalar_tensor_tensor(routed[:, qt, :], y, pr, routed[:, qt, :], ALU.mult, ALU.add)
                            ins.then_inc(routed_step, 1)
                            dve.wait_ge(routed_step, count(it, u, QT * E, qt * E + e + 1))
                            if e == E - 1:
                                dve.sem_inc(y_taken, 1)
                    dve.wait_ge(out_made, count(it, u, 1, 1))
                    dve.wait_ge(tanh_ready, count(it, u, 1, 1))
                    dve.scalar_tensor_tensor(product[:, :, :], tanh[u][:, :, :], 1.0,
                                             out_ps[:, 0:QT * C].rearrange("p (q n) -> p q n", q=QT), ALU.add, ALU.mult
                                             ).then_inc(product_ready, 1)
                    dve.wait_ge(product_ready, count(it, u, 1, 1))
                    stand_alone(dve, passed_dve)
                    x = X[:, bass.ds(tile, QT), :]
                    dve.scalar_tensor_tensor(x, product[:, :, :], 0.5, x, ALU.mult, ALU.add).then_inc(x_done, 1)
                loop(dve, body)


def mlp(nc, tag, X, negative_mean, inverse, columns, norm_cols, w1_d, b1_d, w2_d, b2_d, gate, swiglu, const):
    NK = w2_d.shape[0] // 128
    with phase(nc, tag) as (sb, ps, sem):
        NW = NK * (2 if swiglu else 1)
        w1 = sb("w1", [128, NW, 128])
        b1 = sb("b1", [128, NW, 1])
        w2 = sb("w2", [128, NK, C])
        b2, ones, ident = sb("b2", [1, C]), sb("ones", [1, 128]), sb("ident", [128, 128])
        normed = [sb(f"normed{i}", [128, QT, C]) for i in range(2)]
        x_t = [sb(f"x_t{i}", [128, T]) for i in range(2)]
        silu = [sb(f"silu{i}", [128, T]) for i in range(2)]
        hidden = [sb(f"hidden{i}", [128, NK, T]) for i in range(2)]
        gated = sb("gated", [128, QT, C])
        turned_ps = ps("turned_ps")
        a_ps = [ps(f"a_ps{i}") for i in range(2)]
        b_ps = [ps(f"b_ps{i}") for i in range(2)] if swiglu else None
        out_ps = [ps(f"out_ps{i}") for i in range(2)]
        loaded, set_once = sem("loaded"), sem("set_once")
        normed_ready, turned_made, turned_ready = sem("normed_ready"), sem("turned_made"), sem("turned_ready")
        a_made, b_made, silu_ready, hidden_ready = sem("a_made"), sem("b_made"), sem("silu_ready"), sem("hidden_ready")
        out_made, gated_ready, x_done = sem("out_made"), sem("gated_ready"), sem("x_done")
        passed_act, passed_dve = sem("passed_act"), sem("passed_dve")

        def count(it, u, per=1, c=0):
            return it * (2 * per) + (u * per + c)

        def loop(eng, body):
            body(0, 0, 0, True)
            body(0, 0, 1, True)
            with eng.Fori(1, B // 2) as it:
                body(it, it * 2, 0, False)
                body(it, it * 2, 1, False)

        with nc.Block() as block:
            @block.sync
            def _(sp):
                for dst, src in [(w1[:, :, :], w1_d.rearrange("c (k n) -> c k n", n=128)),
                                 (w2[:, :, :], w2_d.rearrange("(k p) n -> p k n", p=128)),
                                 (b2[:, :], b2_d.rearrange("(o n) -> o n", o=1)), (ident[:, :], const["ident_f"])]:
                    sp.dma_start(dst, src).then_inc(loaded, 16)
                for k in range(NW):
                    sp.dma_start(b1[:, k, :], b1_d[k * 128:(k + 1) * 128].rearrange("(p o) -> p o", o=1)
                                 ).then_inc(loaded, 16)

            @block.tensor
            def _(pe):
                pe.wait_ge(loaded, (4 + NW) * 16)
                pe.wait_ge(set_once, 1)

                def body(it, b, u, first):
                    pe.wait_ge(normed_ready, count(it, u, 1, 1))
                    if not (first and u == 0):
                        pe.wait_ge(turned_ready, count(it, u))
                    for qt in range(QT):
                        last = pe.transpose(turned_ps[:, qt * 128:qt * 128 + 128], normed[u][:, qt, :], ident[:, :])
                    last.then_inc(turned_made, 1)
                    pe.wait_ge(turned_ready, count(it, u, 1, 1))
                    for k in range(NK):
                        if not (first and u == 0 and k < 2):
                            pe.wait_ge(silu_ready if swiglu else hidden_ready, count(it, u, NK, k - 1))
                        pe.matmul(a_ps[k % 2][:, 0:T], w1[:, k, :], x_t[u][:, :], start=True, stop=True).then_inc(a_made, 1)
                        if swiglu:
                            if not (first and u == 0 and k < 2):
                                pe.wait_ge(hidden_ready, count(it, u, NK, k - 1))
                            pe.matmul(b_ps[k % 2][:, 0:T], w1[:, NK + k, :], x_t[u][:, :], start=True, stop=True
                                      ).then_inc(b_made, 1)
                    pe.wait_ge(hidden_ready, count(it, u, NK, NK))
                    if not first:
                        pe.wait_ge(gated_ready, count(it, u, QT, -QT))
                    for qt in range(QT):
                        out = out_ps[u][:, qt * C:qt * C + C]
                        for k in range(NK):
                            pe.matmul(out, hidden[u][:, k, qt * 128:qt * 128 + 128], w2[:, k, :], start=(k == 0), stop=False)
                        last = pe.matmul(out, ones[:, :], b2[:, :], start=False, stop=True)
                    last.then_inc(out_made, 1)
                loop(pe, body)

            @block.scalar
            def _(act):
                act.wait_ge(loaded, (4 + NW) * 16)

                def body(it, b, u, first):
                    act.wait_ge(turned_made, count(it, u, 1, 1))
                    stand_alone(act, passed_act)
                    if not first:
                        act.wait_ge(b_made if swiglu else a_made, count(it, u, NK, -NK))
                        stand_alone(act, passed_act)
                    sc, sh = (columns[:, c, bass.ds(b + u, 1)] for c in norm_cols)
                    act.activation(x_t[u][:, :], turned_ps[:, 0:T], ACT.Identity, bias=sh, scale=sc
                                   ).then_inc(turned_ready, 1)
                    for k in range(NK):
                        act.wait_ge(a_made, count(it, u, NK, k + 1))
                        if swiglu:
                            if not (first and u == 0 and k < 2):
                                act.wait_ge(hidden_ready, count(it, u, NK, k - 1))
                            act.activation(silu[k % 2][:, :], a_ps[k % 2][:, 0:T], ACT.Silu, bias=b1[:, k, :]
                                           ).then_inc(silu_ready, 1)
                        else:
                            if k == 0 and not first:
                                act.wait_ge(out_made, count(it, u, 1, -1))
                            act.activation(hidden[u][:, k, :], a_ps[k % 2][:, 0:T], ACT.Gelu_apprx_tanh,
                                           bias=b1[:, k, :]).then_inc(hidden_ready, 1)
                loop(act, body)

            @block.vector
            def _(dve):
                dve.wait_ge(loaded, (4 + NW) * 16)
                dve.memset(ones[:, :], 1.0).then_inc(set_once, 1)

                def body(it, b, u, first):
                    tile = (b + u) * QT
                    if not first:
                        dve.wait_ge(turned_made, count(it, u, 1, -1))
                        stand_alone(dve, passed_dve)
                    for qt in range(QT):
                        ins = dve.tensor_scalar(normed[u][:, qt, :], X[:, bass.ds(tile + qt, 1), :].rearrange("p o n -> p (o n)"),
                                                negative_mean[:, bass.ds(tile + qt, 1)], inverse[:, bass.ds(tile + qt, 1)],
                                                ALU.add, ALU.mult)
                    ins.then_inc(normed_ready, 1)
                    if swiglu:
                        for k in range(NK):
                            dve.wait_ge(silu_ready, count(it, u, NK, k + 1))
                            dve.wait_ge(b_made, count(it, u, NK, k + 1))
                            if k == 0 and not first:
                                dve.wait_ge(out_made, count(it, u, 1, -1))
                            dve.scalar_tensor_tensor(hidden[u][:, k, :], b_ps[k % 2][:, 0:T], b1[:, NK + k, :],
                                                     silu[k % 2][:, :], ALU.add, ALU.mult).then_inc(hidden_ready, 1)
                    dve.wait_ge(out_made, count(it, u, 1, 1))
                    stand_alone(dve, passed_dve)
                    for qt in range(QT):
                        dve.tensor_tensor(gated[:, qt, :], out_ps[u][:, qt * C:qt * C + C], gate[:, bass.ds((b + u) * C, C)],
                                          ALU.mult).then_inc(gated_ready, 1)
                    dve.wait_ge(gated_ready, count(it, u, QT, QT))
                    stand_alone(dve, passed_dve)
                    x = X[:, bass.ds(tile, QT), :]
                    dve.tensor_tensor(x, x, gated[:, :, :], ALU.add).then_inc(x_done, 1)
                loop(dve, body)




def network(nc, p, x_in, x_out):
    def dram(name, shape, dt=F32):
        return nc.dram_tensor(name, shape, dt).ap()

    def block_of(w, k):
        return w[:, k * C:(k + 1) * C]

    def bias_of(b, k):
        return b[k * C:(k + 1) * C]

    const = {"ident_f": p["ident_f"], "ident_bf": p["ident_bf"], "neg_ident_bf": p["neg_ident_bf"]}
    plain = {True: {**const, "k_rows": p["k_rows_cross"], "q_rows": p["q_rows_plain"]},
             False: {**const, "k_rows": p["k_rows_self"], "q_rows": p["q_rows_plain"]}}
    windows = {**const, "k_rows": p["k_rows_window"], "q_rows": p["q_rows_window"]}
    ctx, n1, n2, n3, n0 = p["ctx_1024"], "L1_xcond_", "L2_xcond_", "L3_xcond_", "L0_xcond_"
    l0 = {k[len(n0):]: v for k, v in p.items() if k.startswith(n0)}

    nx_dram, ev_dram = dram("nx_rows", [B, 128, T]), dram("ev_rows", [B, 128, T])
    ctx_turned = dram("ctx_turned", [B, 128, LC])
    q_parts = dram("q_parts", [B, ROW_MASK, H, T], BF16)
    k_self, v_self = dram("k_self", [B, PARTS * D, H, T], BF16), dram("v_self", [B, T, C])
    k_cross = [dram(f"k_cross{i}", [B, PARTS * D, H, LC], BF16) for i in range(3)]
    v_cross = [dram(f"v_cross{i}", [B, LC, C]) for i in range(3)]

    ada1, b_ada1, ada2, b_ada2 = p[n1 + "w_ada"], p[n1 + "b_ada"], p[n2 + "adaln_w"], p[n2 + "adaln_b"]
    ss_q, b_ss_q, ss_kv, b_ss_kv = p[n3 + "Wss_q"], p[n3 + "bss_q"], p[n3 + "Wss_kv"], p[n3 + "bss_kv"]
    blocks = [(block_of(ada1, k), bias_of(b_ada1, k), True, True) for k in (1, 4, 7)]
    blocks += [(block_of(ada2, k), bias_of(b_ada2, k), True, True) for k in (1, 4)]
    blocks += [(block_of(ss_q, 0), bias_of(b_ss_q, 0), True, True), (block_of(ss_kv, 0), bias_of(b_ss_kv, 0), True, True)]
    blocks += [(block_of(ada1, k), bias_of(b_ada1, k), True, False) for k in (0, 3, 6)]
    blocks += [(block_of(ada2, k), bias_of(b_ada2, k), True, False) for k in (0, 3)]
    blocks += [(block_of(ss_q, 1), bias_of(b_ss_q, 1), True, False), (block_of(ss_kv, 1), bias_of(b_ss_kv, 1), True, False)]
    NSC = 7
    MSA, MCA, MLP, SA2, FF2, Q3, KV3 = ((k, k + NSC) for k in range(NSC))
    EXPERT_COLS = len(blocks)
    for e in range(3):
        for r in range(2):
            blocks.append((l0["e_w1"][e, 2 * C:3 * C, r * 128:(r + 1) * 128],
                           l0["e_b1"][e, r * 128:(r + 1) * 128], False, False))
    blocks.append((l0["gate_w1"][2 * C:3 * C, :], l0["gate_b1"], False, False))
    scale = float(D) ** -0.5
    tokens = [(0, 0, T), (1, 0, T)]
    ctx_items = [(0, r, min(BANK, LC - r)) for r in range(0, LC, BANK)]

    with ExitStack() as stack:
        def sb(name, shape):
            return stack.enter_context(nc.sbuf_tensor(name, shape, F32))
        X = sb("X", [128, NTILE, C])
        silu_t, cond_sb = sb("silu_t", [128, B]), sb("cond_sb", [128, B])
        columns = sb("columns", [128, len(blocks), B])
        gate = sb("gate", [128, B * C])
        negative_mean, inverse = sb("negative_mean", [128, NTILE]), sb("inverse", [128, NTILE])
        probs = sb("probs", [128, NTILE, 3])
        x_loaded = stack.enter_context(nc.semaphore("x_loaded"))
        x_stored = stack.enter_context(nc.semaphore("x_stored"))

        with nc.Block() as block:
            @block.sync
            def _(sp):
                for b in range(B):
                    sp.dma_start(X[:, b * QT:(b + 1) * QT, :], x_in[b].rearrange("(q p) c -> p q c", p=128)
                                 ).then_inc(x_loaded, 16)
                sp.dma_start(q_parts[:, ROW_SHIFT:ROW_MASK, :, :].rearrange("b r h t -> b r (h t)"), p["zero_rows"]
                             ).then_inc(x_loaded, 16)
                sp.wait_ge(x_loaded, 16 * (B + 1))

        modulation(nc, "modulation", p["cond_t"], silu_t, cond_sb, columns, blocks)
        prepare(nc, "ctx", X, ctx_items, columns, 1e-5,
                [("split", block_of(p[n1 + "w_kv"], 0), bias_of(p[n1 + "b_kv"], 0), 1.0, k_cross[0]),
                 ("rows", block_of(p[n1 + "w_kv"], 1), bias_of(p[n1 + "b_kv"], 1), 1.0, v_cross[0]),
                 ("split", block_of(p[n2 + "kv_w"], 0), bias_of(p[n2 + "kv_b"], 0), 1.0, k_cross[1]),
                 ("rows", block_of(p[n2 + "kv_w"], 1), bias_of(p[n2 + "kv_b"], 1), 1.0, v_cross[1])],
                [("split", block_of(p[n3 + "Wkv"], 0), bias_of(p[n3 + "bkv"], 0), 1.0, k_cross[2]),
                 ("rows", block_of(p[n3 + "Wkv"], 1), bias_of(p[n3 + "bkv"], 1), 1.0, v_cross[2])],
                KV3, const, ctx, ctx_turned)

        row_stats(nc, "stats0", X, negative_mean, inverse, 1e-5)
        evidence(nc, "evidence", X, negative_mean, inverse, cond_sb, probs, l0, ctx, ctx_turned, nx_dram, ev_dram, const)
        experts(nc, "experts", X, probs, columns, EXPERT_COLS, l0, nx_dram, ev_dram, const)

        def self_attention(tag, w_qkv, b_qkv, cols, w_out, b_out, g, consts):
            prepare(nc, tag + "_qkv", X, tokens, columns, 1e-6, [],
                    [("split_q", block_of(w_qkv, 0), bias_of(b_qkv, 0), scale, q_parts),
                     ("split", block_of(w_qkv, 1), bias_of(b_qkv, 1), 1.0, k_self),
                     ("rows", block_of(w_qkv, 2), bias_of(b_qkv, 2), 1.0, v_self)], cols, const)
            attention(nc, tag, X, q_parts, k_self, v_self, T, w_out, b_out, g, consts)

        def cross_attention(tag, w_q, b_q, cols, eps, kv, w_out, b_out, g, topk=False):
            prepare(nc, tag + "_q", X, tokens, columns, eps, [], [("split_q", w_q, b_q, scale, q_parts)], cols, const)
            attention(nc, tag, X, q_parts, k_cross[kv], v_cross[kv], LC, w_out, b_out, g, plain[True], topk)

        gate_rows(nc, "gate_msa", silu_t, gate, block_of(ada1, 2), bias_of(b_ada1, 2))
        self_attention("self1", p[n1 + "w_qkv"], p[n1 + "b_qkv"], MSA, p[n1 + "w_so"], p["b_so_row"], gate, windows)
        gate_rows(nc, "gate_mca", silu_t, gate, block_of(ada1, 5), bias_of(b_ada1, 5))
        cross_attention("cross1", p[n1 + "w_q"], p[n1 + "b_q"], MCA, 1e-6, 0, p[n1 + "w_co"], p["b_co_row"], gate, True)
        gate_rows(nc, "gate_mlp", silu_t, gate, block_of(ada1, 8), bias_of(b_ada1, 8))
        row_stats(nc, "stats1", X, negative_mean, inverse, 1e-6)
        mlp(nc, "mlp1", X, negative_mean, inverse, columns, MLP, p[n1 + "w_m1"], p[n1 + "b_m1"], p[n1 + "w_m2"],
            p[n1 + "b_m2"], gate, True, const)

        gate_rows(nc, "gate_sa", silu_t, gate, block_of(ada2, 2), bias_of(b_ada2, 2))
        self_attention("self2", p[n2 + "qkv_w"], p[n2 + "qkv_b"], SA2, p[n2 + "sa_proj_w"], p["sa_proj_b_row"], gate,
                       plain[False])
        cross_attention("cross2", p[n2 + "q_w"], p[n2 + "q_b"], None, 1e-6, 1, p[n2 + "ca_proj_w"], p["ca_proj_b_row"], None)
        gate_rows(nc, "gate_ff", silu_t, gate, block_of(ada2, 5), bias_of(b_ada2, 5))
        row_stats(nc, "stats2", X, negative_mean, inverse, 1e-6)
        mlp(nc, "mlp2", X, negative_mean, inverse, columns, FF2, p[n2 + "fc1_w"], p[n2 + "fc1_b"], p[n2 + "fc2_w"],
            p[n2 + "fc2_b"], gate, False, const)

        cross_attention("cross3", p[n3 + "Wq"], p[n3 + "bq"], Q3, 1e-5, 2, p[n3 + "Wp"], p["bp_row"], None)

        with nc.Block() as block:
            @block.sync
            def _(sp):
                for b in range(B):
                    sp.dma_start(x_out[b].rearrange("(q p) c -> p q c", p=128), X[:, b * QT:(b + 1) * QT, :]
                                 ).then_inc(x_stored, 16)
                sp.wait_ge(x_stored, 16 * B)


def layout(inputs):
    import numpy as np
    bf16 = np.dtype("bfloat16")
    arrays = {k: np.ascontiguousarray(v) for k, v in inputs.items()}
    arrays["cond_t"] = np.ascontiguousarray(arrays.pop("cond_1024").T)
    arrays["L0_xcond_Wk_t"] = np.ascontiguousarray(arrays.pop("L0_xcond_Wk").T)
    for name in ("L1_xcond_b_so", "L1_xcond_b_co", "L2_xcond_sa_proj_b", "L2_xcond_ca_proj_b", "L3_xcond_bp"):
        arrays[name.split("xcond_")[1] + "_row"] = arrays.pop(name).reshape(1, C)
    for name, blocks in (("L1_xcond_%s_qkv", 2), ("L1_xcond_%s_q", 1), ("L1_xcond_%s_kv", 1), ("L2_xcond_qkv_%s", 2),
                         ("L2_xcond_q_%s", 1), ("L2_xcond_kv_%s", 1), ("L3_xcond_%sq", 1), ("L3_xcond_%skv", 1)):
        for kind in (("W", "b") if name.startswith("L3") else ("w", "b")):
            a = arrays[name % kind].copy()
            for k in range(blocks):
                block = a[..., k * C:(k + 1) * C]
                block[...] = block.reshape(*a.shape[:-1], H, D).swapaxes(-1, -2).reshape(block.shape).copy()
            arrays[name % kind] = a
    arrays["ident_f"] = np.eye(128, dtype=np.float32)
    arrays["ident_bf"] = np.eye(128).astype(bf16)
    arrays["neg_ident_bf"] = (-np.eye(128)).astype(bf16)
    arrays["zero_rows"] = np.zeros((B, PARTS, H * T), bf16)
    window = (np.arange(T) - SHIFT) % T // WINDOW
    for name, n in (("cross", LC), ("self", T), ("window", T)):
        k_rows = np.zeros((NWIN + PARTS, HQ, n), np.float32)
        k_rows[0:PARTS] = 1
        if name == "window":
            k_rows[PARTS:] = (window == np.arange(NWIN)[:, None])[:, None, :]
        arrays["k_rows_" + name] = k_rows.astype(bf16)
    q_rows = np.zeros((NWIN, HQ, T), np.float32)
    arrays["q_rows_plain"] = q_rows.astype(bf16)
    q_rows[:] = np.where(window == np.arange(NWIN)[:, None], 0.0, -30000.0)[:, None, :]
    arrays["q_rows_window"] = q_rows.astype(bf16)
    return arrays


def kernel(**inputs):
    import concourse.bacc as bacc
    import numpy as np
    from concourse.bass_utils import run_bass_kernel_spmd

    nc = bacc.Bacc("TRN2", target_bir_lowering=False, num_devices=1)
    arrays = layout(inputs)
    p = {k: nc.dram_tensor(k, list(a.shape), mybir.dt.from_np(a.dtype), kind="ExternalInput").ap()
         for k, a in arrays.items()}
    out = nc.dram_tensor("out", [B, T, C], F32, kind="ExternalOutput").ap()
    network(nc, p, p["x"], out)
    result = run_bass_kernel_spmd(nc, [arrays], core_ids=[0])
    return np.array(result.results[0]["out"])
```
